# Optimizing a Trainium2 kernel written in Bass

```python
import numpy as np
import jax
import jax.numpy as jnp

def _softmax(x, axis=-1):
    return jax.nn.softmax(x, axis=axis)

def _gelu(x):
    return jax.nn.gelu(x, approximate=True)

def _silu(x):
    return jax.nn.silu(x)

def _sigmoid(x):
    return jax.nn.sigmoid(x)

def _layernorm(x, axis=-1, eps=1e-05):
    m = jnp.mean(x, axis=axis, keepdims=True)
    v = jnp.var(x, axis=axis, keepdims=True)
    return (x - m) / jnp.sqrt(v + eps)

def _scatter_add(tgt, idx, src, axis=0):
    return tgt.at[idx].add(src)

def _segment_sum(src, seg, n):
    return jax.ops.segment_sum(src, seg, n)
kernel_name = 'mk_gnn_preln_d2_gnn_r64_ce7fb1'

def setup_inputs(seed: int=0):
    np.random.seed(seed)
    _w = jnp.asarray

    def _rec_inputs():
        import jax
        import jax.numpy as jnp
        _gk = jax.random.key(seed)
        x = -0.0003713 + 1 * jax.random.normal(jax.random.fold_in(_gk, 1), (50000, 128), jnp.float32)
        src = jax.random.randint(jax.random.fold_in(_gk, 2), (12500,), 0, 50000, jnp.int32)
        dst = jnp.minimum((50000 * jax.random.uniform(jax.random.fold_in(_gk, 3), (12500,)) ** 2.0).astype(jnp.int32), 49999)
        _o = jnp.argsort(dst, stable=True)
        src = src[_o]
        dst = dst[_o]
        edge_type_4 = jax.random.randint(jax.random.fold_in(_gk, 13), (12500,), 0, 4, jnp.int32)
        return (x, src, dst, edge_type_4)
    x, src, dst, edge_type_4 = _rec_inputs()

    def _L0_gnn_setup():
        import jax, jax.numpy as jnp
        import numpy as np
        N_NODES = 100000
        N_EDGES = 25000
        IN_DIM = 128
        OUT_DIM = 128
        N_HEADS = 4
        HEAD_DIM = OUT_DIM // N_HEADS
        NEG_SLOPE = 0.2
        key = jax.random.key(seed)
        k1, k2, k3, k4 = jax.random.split(key, 4)
        h = jax.random.normal(k1, (N_NODES, IN_DIM), dtype=jnp.float32)
        edge_index = jax.random.randint(k2, (2, N_EDGES), 0, N_NODES, dtype=jnp.int32)
        W = jax.random.normal(k3, (IN_DIM, OUT_DIM), dtype=jnp.float32) / np.sqrt(IN_DIM)
        a = jax.random.normal(k4, (N_HEADS, 2 * HEAD_DIM), dtype=jnp.float32) / np.sqrt(2 * HEAD_DIM)
        return {'h': h, 'edge_index': edge_index, 'W': W, 'a': a}
    _L0_gnn_all = _L0_gnn_setup()
    _L0_gnn_in = {k: v for k, v in _L0_gnn_all.items() if k in ('W', 'a')}
    del _L0_gnn_all

    def _L1_gnn_setup():
        import jax, jax.numpy as jnp
        import numpy as np
        N = 100000
        E = 25000
        D = 128
        G = 128
        K = 4
        STEPS = 3

        def _gru_cell(a, h, W_ih, b_ih, W_hh, b_hh):
            gi = a @ W_ih.T + b_ih
            gh = h @ W_hh.T + b_hh
            ir, iz, in_ = jnp.split(gi, 3, axis=1)
            hr, hz, hn = jnp.split(gh, 3, axis=1)
            r = jax.nn.sigmoid(ir + hr)
            z = jax.nn.sigmoid(iz + hz)
            n = jnp.tanh(in_ + r * hn)
            return (1.0 - z) * n + z * h
        key = jax.random.key(seed)
        ks = jax.random.split(key, 16)
        s = 0.05
        return {'features': jax.random.normal(ks[0], (N, D), jnp.float32), 'src': jax.random.randint(ks[1], (E,), 0, N, jnp.int32), 'dst': jax.random.randint(ks[2], (E,), 0, N, jnp.int32), 'etypes': jax.random.randint(ks[3], (E,), 0, K, jnp.int32), 'W_et': jax.random.normal(ks[4], (K, D, D), jnp.float32) * s, 'b_et': jax.random.normal(ks[5], (K, D), jnp.float32) * s, 'W_ih': jax.random.normal(ks[6], (3 * D, D), jnp.float32) * s, 'b_ih': jax.random.normal(ks[7], (3 * D,), jnp.float32) * s, 'W_hh': jax.random.normal(ks[8], (3 * D, D), jnp.float32) * s, 'b_hh': jax.random.normal(ks[9], (3 * D,), jnp.float32) * s, 'i_w': jax.random.normal(ks[10], (G, D + D), jnp.float32) * s, 'i_b': jax.random.normal(ks[11], (G,), jnp.float32) * s, 'j_w': jax.random.normal(ks[12], (G, D), jnp.float32) * s, 'j_b': jax.random.normal(ks[13], (G,), jnp.float32) * s}
    _L1_gnn_all = _L1_gnn_setup()
    _L1_gnn_in = {k: v for k, v in _L1_gnn_all.items() if k in ('W_et', 'b_et', 'W_ih', 'b_ih', 'W_hh', 'b_hh', 'i_w', 'i_b', 'j_w', 'j_b')}
    del _L1_gnn_all
    return {'x': x, 'src': src, 'dst': dst, 'edge_type_4': edge_type_4, 'L0_gnn_W': _L0_gnn_in['W'], 'L0_gnn_a': _L0_gnn_in['a'], 'L1_gnn_W_et': _L1_gnn_in['W_et'], 'L1_gnn_b_et': _L1_gnn_in['b_et'], 'L1_gnn_W_ih': _L1_gnn_in['W_ih'], 'L1_gnn_b_ih': _L1_gnn_in['b_ih'], 'L1_gnn_W_hh': _L1_gnn_in['W_hh'], 'L1_gnn_b_hh': _L1_gnn_in['b_hh'], 'L1_gnn_i_w': _L1_gnn_in['i_w'], 'L1_gnn_i_b': _L1_gnn_in['i_b'], 'L1_gnn_j_w': _L1_gnn_in['j_w'], 'L1_gnn_j_b': _L1_gnn_in['j_b']}

def reference(x, src, dst, edge_type_4, L0_gnn_W, L0_gnn_a, L1_gnn_W_et, L1_gnn_b_et, L1_gnn_W_ih, L1_gnn_b_ih, L1_gnn_W_hh, L1_gnn_b_hh, L1_gnn_i_w, L1_gnn_i_b, L1_gnn_j_w, L1_gnn_j_b):
    import jax
    import jax.numpy as jnp

    def _L0_gnn_ref(h, edge_index, W, a):
        import jax, jax.numpy as jnp
        import numpy as np
        N_NODES = 100000
        N_EDGES = 25000
        IN_DIM = 128
        OUT_DIM = 128
        N_HEADS = 4
        HEAD_DIM = OUT_DIM // N_HEADS
        NEG_SLOPE = 0.2
        n = h.shape[0]
        src, dst = (edge_index[0], edge_index[1])
        wh = (h @ W).reshape(n, N_HEADS, HEAD_DIM)
        a_src, a_dst = (a[:, :HEAD_DIM], a[:, HEAD_DIM:])
        s_src = jnp.einsum('nhd,hd->nh', wh, a_src)
        s_dst = jnp.einsum('nhd,hd->nh', wh, a_dst)
        e = jax.nn.leaky_relu(s_src[src] + s_dst[dst], negative_slope=NEG_SLOPE)
        m = jax.ops.segment_max(e, dst, num_segments=n)
        ex = jnp.exp(e - m[dst])
        denom = jax.ops.segment_sum(ex, dst, num_segments=n)
        w = ex / denom[dst]
        out = jax.ops.segment_sum(w[:, :, None] * wh[src], dst, num_segments=n)
        return out.reshape(n, OUT_DIM)

    def _L1_gnn_ref(features, src, dst, etypes, W_et, b_et, W_ih, b_ih, W_hh, b_hh, i_w, i_b, j_w, j_b):
        import jax, jax.numpy as jnp
        import numpy as np
        N = 100000
        E = 25000
        D = 128
        G = 128
        K = 4
        STEPS = 3

        def _gru_cell(a, h, W_ih, b_ih, W_hh, b_hh):
            gi = a @ W_ih.T + b_ih
            gh = h @ W_hh.T + b_hh
            ir, iz, in_ = jnp.split(gi, 3, axis=1)
            hr, hz, hn = jnp.split(gh, 3, axis=1)
            r = jax.nn.sigmoid(ir + hr)
            z = jax.nn.sigmoid(iz + hz)
            n = jnp.tanh(in_ + r * hn)
            return (1.0 - z) * n + z * h
        n_nodes = features.shape[0]
        h = features
        for _ in range(STEPS):
            t = jnp.einsum('nd,kod->kno', h, W_et) + b_et[:, None, :]
            msg = t[etypes, src]
            a = jax.ops.segment_sum(msg, dst, num_segments=n_nodes)
            h = _gru_cell(a, h, W_ih, b_ih, W_hh, b_hh)
        gate = jax.nn.sigmoid(jnp.concatenate([h, features], axis=1) @ i_w.T + i_b)
        return gate * (h @ j_w.T + j_b)
    edge_index = jnp.stack([src, dst])
    h = jnp.maximum(_layernorm(x, axis=-1), 0.0)
    x = x + _L0_gnn_ref(h, edge_index, L0_gnn_W, L0_gnn_a)
    h = jnp.maximum(_layernorm(x, axis=-1), 0.0)
    x = x + _L1_gnn_ref(h, src, dst, edge_type_4, L1_gnn_W_et, L1_gnn_b_et, L1_gnn_W_ih, L1_gnn_b_ih, L1_gnn_W_hh, L1_gnn_b_hh, L1_gnn_i_w, L1_gnn_i_b, L1_gnn_j_w, L1_gnn_j_b)
    return x

_drawn_inputs = setup_inputs


def setup_inputs(seed=0):
    import zlib

    import numpy as np

    out = dict(_drawn_inputs(seed))
    spreads = {}
    factors = {'L0_gnn_a': 4.315,
     'L1_gnn_W_et': 4.358,
     'L1_gnn_b_et': 8.0,
     'L1_gnn_W_ih': 4.327,
     'L1_gnn_b_ih': 5.214,
     'L1_gnn_b_hh': 8.0,
     'L1_gnn_i_w': 5.894,
     'L1_gnn_i_b': 32.562}
    for name, (base, spread) in spreads.items():
        noise = np.random.default_rng([zlib.crc32(name.encode()), seed]).standard_normal(out[name].shape)
        drawn = base * np.exp(spread * noise) if base else spread * noise
        out[name] = jnp.asarray(drawn.astype(out[name].dtype))
    for name, factor in factors.items():
        out[name] = (out[name] * factor).astype(out[name].dtype)
    return out
```

```python
import concourse.bass as bass
from concourse import mybir
from contextlib import ExitStack

P = 125
J = 4
T = P * J
D = 128
K = 4
HEADS = 4
STEPS = 3
EPS = 1e-5
SLOPE = 0.2
FAR = 3.0e38
LANES = 4
TB = 10
WORK = 13700


def run(eng, body, n, head=1):
    pairs = (n - head - 2) // 2
    for i in range(head):
        body(i, i % 2, False)
    with eng.Fori(0, pairs) as pair:
        body(pair * 2 + head, 1, False)
        body(pair * 2 + (head + 1), 0, False)
    for i in range(head + 2 * pairs, n):
        body(i, i % 2, i == n - 1)


def need(eng, semaphore, value):
    if not isinstance(value, int) or value > 0:
        eng.wait_ge(semaphore, value)


def alone(eng, semaphore, value, passed):
    if not isinstance(value, int) or value > 0:
        eng.wait_ge(semaphore, value)
        eng.sem_inc(passed, 1)


def gnn_kernel(nc, x, src, dst, etype, w0, w0T, a_cols, wetT, b_et, wihT, bih, whhT, bhh, iwT, ib, jwT, jb,
               ident_in, headmask_in, part_type_in, split_in, out):
    f32, bf16, i32, u8 = mybir.dt.float32, mybir.dt.bfloat16, mybir.dt.int32, mybir.dt.uint8
    ALU, ACT = mybir.AluOpType, mybir.ActivationFunctionType

    N, E = x.shape[0], src.shape[0]
    NT, ET = N // T, E // T
    NG = NT // LANES
    NB = E // P
    SKIP = N + 10000
    GU, RU = STEPS * LANES, LANES
    MMG = 3 * GU + 2 * RU

    ctx = ExitStack()
    with ctx:
        def sb(name, shape, dt=f32):
            return ctx.enter_context(nc.sbuf_tensor(name, shape, dt))

        def bank(name, shape=(128, 512)):
            return ctx.enter_context(nc.psum_tensor(name, list(shape), f32))

        def sem(name):
            return ctx.enter_context(nc.semaphore(name))

        first_slot = nc.dram_tensor("slot_of_node", (N, 1), i32, kind="Internal").ap()
        h0_rows = nc.dram_tensor("h0_rows", (2 * E, D), f32, kind="Internal").ap()
        h_rows = [h0_rows] + [nc.dram_tensor(f"h{t}_rows", (E + N, D), f32, kind="Internal").ap() for t in (1, 2)]
        x1_rows = nc.dram_tensor("x1_rows", (E, D), f32, kind="Internal").ap()

        ident = sb("ident", [128, 128])
        headmask = sb("headmask", [128, 128])
        part_type = sb("part_type", [12, 1])
        split_mask = sb("split_mask", [12, 3])
        W0 = sb("W0", [128, D])
        W0T = sb("W0T", [128, D])
        acol = sb("acol", [128, 2])
        amat = sb("amat", [128, 2, D])
        Wse = sb("Wse", [128, 2, D])
        Wet = sb("Wet", [128, K, D])
        Wih = sb("Wih", [128, 3, D])
        Whh = sb("Whh", [128, 3, D])
        Wi = sb("Wi", [128, 2, D])
        Wj = sb("Wj", [128, D])
        bias_i = sb("bias_i", [128, 3])
        bias_h = sb("bias_h", [128, 3])
        bias_g = sb("bias_g", [128, 3])
        ibias = sb("ibias", [128, 1])
        jbias = sb("jbias", [128, 1])
        bet12 = sb("bet12", [12, D])
        bet_rest = sb("bet_rest", [12, 2, D])
        bet_part = sb("bet_part", [12, 3, D], bf16)
        bet_mix = sb("bet_mix", [12, 3, D])
        Bet = sb("Bet", [12, D], bf16)

        src_row = sb("src_row", [NB, P], i32)
        dst_row = sb("dst_row", [NB, P], i32)
        nxt_row = sb("nxt_row", [NB, P], i32)
        num_row = sb("num_row", [NB, 4, P])
        slot_iota = sb("slot_iota", [P, NB], i32)
        slot_no = sb("slot_no", [P, NB])
        edge_cols = sb("edge_cols", [P, 3, NB])
        src_idx = sb("src_idx", [P, NB], i32)
        dst_idx = sb("dst_idx", [P, NB], i32)
        put_idx = sb("put_idx", [P, NB], i32)
        slot1 = sb("slot1", [P, NB], i32)
        got_slot = sb("got_slot", [P, NB], i32)
        h0_idx = sb("h0_idx", [P, NB], i32)
        h_idx = sb("h_idx", [P, NB], i32)
        plain_row = sb("plain_row", [P, 2, NB])
        table_stage = sb("table_stage", [P, 2, TB], i32)
        row_stage = sb("row_stage", [P, 2, 2, J], i32)
        zero_i = sb("zero_i", [P, N // P], i32)

        same = sb("same", [128, E], u8)
        types = sb("types", [128, E], u8)
        arena = sb("arena", [128, 2 * E])
        F = arena[:, 0:E]
        H = arena[:, E:2 * E]
        work = sb("work", [128, WORK])

        def carver(*regions):
            left = [[ap, 0, size] for ap, size in regions]

            def carve(rows, *dims):
                n = 1
                for d in dims:
                    n *= d
                while left[0][1] + n > left[0][2]:
                    left.pop(0)
                ap = left[0][0][0:rows, left[0][1]:left[0][1] + n]
                left[0][1] += n
                if len(dims) == 3:
                    return ap.rearrange("p (a b c) -> p a b c", a=dims[0], b=dims[1])
                return ap.rearrange("p (a b) -> p a b", a=dims[0]) if len(dims) == 2 else ap
            return carve

        carve = carver((arena[:, :], 2 * E))
        Xd = carve(P, 2 * LANES, J, D)
        Fd = carve(128, 2 * LANES, T)
        Hd = carve(128, LANES, T)
        Nx = carve(P, 2, J * D)
        Rg = carve(128, 2, T)
        Zg = carve(128, 2, T)
        Ng = carve(128, 2, T)
        Keep = carve(128, 2, T)
        Take = carve(128, 2, T)
        Gt = carve(128, 2, T)
        Qo = carve(128, 2, T)
        HO = carve(P, 2, J * D)
        XO = carve(P, 2, J * D)
        stats = sb("stats", [P, LANES, J, 6])
        mean = sb("mean", [P, LANES, J])
        rstd = sb("rstd", [P, LANES, J])
        mom = sb("mom", [P, 4, 2 * J])
        halves = sb("halves", [P, 2 * J])
        inv_d = sb("inv_d", [P, 2 * J])
        eps = sb("eps", [P, 2 * J])
        minus_half = sb("minus_half", [P, 2 * J])

        carve = carver((H, E), (work[:, :], WORK))
        XS = carve(P, 2, J * D)
        XD = carve(P, 2, J * D)
        XK = carve(P, 2, J * D)
        ND = carve(P, J * D)
        SR = carve(P, 2, J * D)
        ST = carve(128, T)
        DT = carve(128, T)
        LS = carve(128, T)
        LG = carve(128, 2, T)
        BK = carve(128, T)
        MX = carve(128, 2, T + 1)
        EA = carve(128, T)
        EB = carve(128, T)
        CF = carve(128, T)
        WT = carve(128, T)
        WV = carve(128, T)
        SD = carve(128, 2, T)
        SN = carve(128, 2, T)
        AO = carve(128, T)
        X1 = carve(P, 2, J * D)
        N1 = carve(P, J * D)
        F1 = carve(P, 2, J * D)
        win_i = carve(128, 2, T + 1)
        typ_i = carve(128, 2, T)
        win = win_i.bitcast(i32)
        typ = typ_i.bitcast(i32)
        a_stats = sb("a_stats", [P, 3 * J, 6])
        a_mean = sb("a_mean", [P, 3 * J])
        a_rstd = sb("a_rstd", [P, 3 * J])

        carve = carver((work[:, :], WORK))
        HG = carve(P, 2, J * D)
        MK = carve(128, K, T)
        AG = carve(128, 2, T)
        Rs = carve(128, T)
        Zs = carve(128, T)
        Ms = carve(128, T)
        Ns = carve(128, T)
        Ks = carve(128, T)
        Ts = carve(128, T)
        HN = carve(128, T)
        HR = carve(P, 2, J * D)
        XB = carve(P, 2, J * D)
        Gs = carve(128, T)
        Qs = carve(128, T)
        OB = carve(P, 2, J * D)
        hot = sb("hot", [12, 2, T], bf16)

        banks = [bank(f"bank{i}") for i in range(8)]

        weights_in = sem("weights_in")
        edges_in = sem("edges_in")
        setup = sem("setup")
        sp_passed = sem("sp_passed")
        pool_passed = sem("pool_passed")
        iota_done = sem("iota_done")
        zero_stored = sem("zero_stored")

        block = ctx.enter_context(nc.Block())

        d_x_in = [sem(f"d_x_in{l}") for l in range(LANES)]
        d_stat = sem("d_stat")
        mom_done = sem("mom_done")
        d_rstd = sem("d_rstd")
        d_normed = sem("d_normed")
        d_x_turned = sem("d_x_turned")
        d_feat = sem("d_feat")
        d_mm = sem("d_mm")
        d_r = sem("d_r")
        d_z = sem("d_z")
        d_m = sem("d_m")
        d_n = sem("d_n")
        d_keep = sem("d_keep")
        d_take = sem("d_take")
        d_h = sem("d_h")
        d_gate = sem("d_gate")
        d_q = sem("d_q")
        d_h_turned = sem("d_h_turned")
        d_h_copied = sem("d_h_copied")
        d_h_stored = [sem(f"d_h_stored{b}") for b in range(2)]
        d_o_turned = sem("d_o_turned")
        d_o = sem("d_o")
        d_o_stored = [sem(f"d_o_stored{b}") for b in range(2)]
        rows_turned = sem("rows_turned")
        idx_steps = sem("idx_steps")
        idx_ready = sem("idx_ready")
        m_staged = sem("m_staged")
        m_put = sem("m_put")
        m_got = sem("m_got")
        got_ready = sem("got_ready")
        wse_ready = sem("wse_ready")
        wse_mm = sem("wse_mm")
        a_open = sem("a_open")
        a_staged = sem("a_staged")
        a_rows_in = [sem(f"a_rows_in{b}") for b in range(2)]
        a_edges_in = [sem(f"a_edges_in{b}") for b in range(2)]
        a_stat = sem("a_stat")
        a_rstd_ready = sem("a_rstd_ready")
        a_src_normed = sem("a_src_normed")
        a_dst_normed = sem("a_dst_normed")
        a_src_turned = sem("a_src_turned")
        a_dst_turned = sem("a_dst_turned")
        a_kept = sem("a_kept")
        a_src_relu = sem("a_src_relu")
        a_src_stored = [sem(f"a_src_stored{b}") for b in range(2)]
        a_src_feat = sem("a_src_feat")
        a_dst_feat = sem("a_dst_feat")
        a_logit_mm = sem("a_logit_mm")
        a_value_mm = sem("a_value_mm")
        a_scaled = sem("a_scaled")
        a_dve = sem("a_dve")
        a_decay = sem("a_decay")
        a_weight = sem("a_weight")
        a_types = sem("a_types")
        a_att = sem("a_att")
        a_att_turned = sem("a_att_turned")
        a_x1 = sem("a_x1")
        a_x1_stored = [sem(f"a_x1_stored{b}") for b in range(2)]
        a_x1_stat = sem("a_x1_stat")
        a_x1_rstd = sem("a_x1_rstd")
        a_x1_normed = sem("a_x1_normed")
        a_x1_turned = sem("a_x1_turned")
        a_x1_relu = sem("a_x1_relu")
        a_f1_stored = [sem(f"a_f1_stored{b}") for b in range(2)]
        a_feat = sem("a_feat")
        b_open = sem("b_open")
        b_idx = sem("b_idx")
        b_idx_steps = sem("b_idx_steps")
        b_staged = sem("b_staged")
        b_rows_in = [sem(f"b_rows_in{b}") for b in range(2)]
        b_turned = sem("b_turned")
        b_masked = sem("b_masked")
        b_hot = sem("b_hot")
        b_msg = sem("b_msg")
        b_sum = sem("b_sum")
        b_own_mm = sem("b_own_mm")
        b_r_mm = sem("b_r_mm")
        b_z_mm = sem("b_z_mm")
        b_n_mm = sem("b_n_mm")
        b_r = sem("b_r")
        b_z = sem("b_z")
        b_m1 = sem("b_m1")
        b_m2 = sem("b_m2")
        b_n = sem("b_n")
        b_keep = sem("b_keep")
        b_take = sem("b_take")
        b_h = sem("b_h")
        b_h_kept = sem("b_h_kept")
        b_h_turned = sem("b_h_turned")
        b_h_copied = sem("b_h_copied")
        b_h_stored = [sem(f"b_h_stored{b}") for b in range(2)]
        b_x1_in = [sem(f"b_x1_in{b}") for b in range(2)]
        b_gate_mm = sem("b_gate_mm")
        b_j_mm = sem("b_j_mm")
        b_gate = sem("b_gate")
        b_q = sem("b_q")
        b_q_turned = sem("b_q_turned")
        b_o = sem("b_o")
        b_o_staged = sem("b_o_staged")
        b_o_put = [sem(f"b_o_put{b}") for b in range(2)]

        A_STEPS = ("leaky", "same", "back", "carry", "max", "lift", "decay_arg", "weight_arg", "weighted", "sum_w", "sum_v",
                   "inverse", "attended")

        def a_count(i, step):
            return i * len(A_STEPS) + (A_STEPS.index(step) + 1)

        def uses(i, b, n):
            return i * (n // 2) if b == 0 else (i - 1) * (n // 2)

        edge_tiles = lambda rows, at: rows[at:at + E, :].rearrange("(t j p) f -> t p j f", p=P, j=J)
        f_tiles, s_tiles = edge_tiles(h0_rows, 0), edge_tiles(h0_rows, E)
        x1_tiles = edge_tiles(x1_rows, 0)
        hs_tiles = [None] + [edge_tiles(h_rows[t], 0) for t in (1, 2)]
        rows4 = lambda ap: ap.rearrange("p (j f) -> p j f", j=J)
        all_of = lambda i: slice(i * T, (i + 1) * T) if isinstance(i, int) else bass.ds(i * T, T)

        x_tiles = x.rearrange("(t p j) f -> t p (j f)", p=P, j=J)
        out_tiles = out.rearrange("(t p j) f -> t p (j f)", p=P, j=J)
        h_tiles = [None] + [h_rows[t][E:E + N, :].rearrange("(t p j) f -> t p (j f)", p=P, j=J) for t in (1, 2)]

        def unit(g, s, l):
            return g * GU + (s * LANES + l + 1)

        def lane(g, l):
            return g * LANES + (l + 1)

        def mm_count(g, s, l, part):
            within = 3 * (s * LANES + l) + part + 1 if s < STEPS else 3 * GU + 2 * l + part + 1
            return g * MMG + within

        n_weights = 21

        @block.sync
        def _(sp):
            for dst_ap, src_ap in ((ident[:], ident_in), (headmask[:], headmask_in), (part_type[:], part_type_in),
                                   (split_mask[:], split_in), (W0[:], w0), (W0T[:], w0T), (acol[:], a_cols),
                                   (Wih[:], wihT.rearrange("d (g o) -> d g o", g=3)),
                                   (Whh[:], whhT.rearrange("d (g o) -> d g o", g=3)),
                                   (Wi[:], iwT.rearrange("(c d) o -> d c o", c=2)), (Wj[:], jwT),
                                   (Wet[:], wetT.rearrange("k d o -> d k o")),
                                   (bias_i[:], bih), (bias_h[:], bhh), (ibias[:], ib), (jbias[:], jb),
                                   (bet12[0:4, :], b_et), (bet12[4:8, :], b_et), (bet12[8:12, :], b_et),
                                   (src_row[:], src.rearrange("(b p) -> b p", p=P)),
                                   (dst_row[:], dst.rearrange("(b p) -> b p", p=P))):
                sp.dma_start(dst_ap, src_ap).then_inc(weights_in, 16)
            sp.wait_ge(setup, 1)
            sp.dma_start(nxt_row[0:NB - 1, :], dst[1:E - P + 1].rearrange("(b p) -> b p", p=P)).then_inc(edges_in, 16)
            sp.dma_start(nxt_row[NB - 1:NB, 0:P - 1], dst[E - P + 1:E].rearrange("(b p) -> b p", b=1)).then_inc(edges_in, 16)
            sp.wait_ge(iota_done, 6)
            sp.dma_start(first_slot.rearrange("(p c) o -> p (c o)", p=P), zero_i[:]).then_inc(zero_stored, 16)

            def load(g, par, l):
                sp.dma_start(Xd[:, par * LANES + l, :, :], x_tiles[g * LANES + l, :, :].rearrange("p (j f) -> p j f", j=J)).then_inc(d_x_in[l], 16)

            for l in range(LANES):
                load(0, 0, l)

            def group(g, par, last):
                for l in range(LANES):
                    if not last:
                        alone(sp, d_o, g * LANES + (l + 1 - LANES), sp_passed)
                        alone(sp, d_stat, lane(g, l), sp_passed)
                        load(g + 1, 1 - par, l)
                for s in (1, 2):
                    for l in range(LANES):
                        alone(sp, d_h_copied, g * 8 + ((s - 1) * LANES + l + 1), sp_passed)
                        sp.dma_start(h_tiles[s][g * LANES + l, :, :], HO[:, l % 2, :]).then_inc(d_h_stored[l % 2], 16)
                for l in range(LANES):
                    alone(sp, d_o, lane(g, l), sp_passed)
                    sp.dma_start(out_tiles[g * LANES + l, :, :], XO[:, l % 2, :]).then_inc(d_o_stored[l % 2], 16)

            run(sp, group, NG)

            bcast = lambda ap: ap.partition_broadcast(128)

            def edge_load(i, b):
                alone(sp, a_dve, a_count(i - 2, "same"), sp_passed)
                alone(sp, a_types, i - 1, sp_passed)
                if isinstance(i, int) and i == 0:
                    sp.dma_start(win[:, b, 1:T + 1], bcast(dst[0:T])).then_inc(a_edges_in[b], 16)
                else:
                    at = slice(i * T - 1, (i + 1) * T) if isinstance(i, int) else bass.ds(i * T - 1, T + 1)
                    sp.dma_start(win[:, b, :], bcast(dst[at])).then_inc(a_edges_in[b], 16)
                sp.dma_start(typ[:, b, :], bcast(etype[all_of(i)])).then_inc(a_edges_in[b], 16)

            def attend(i, b, last):
                if not last:
                    edge_load(i + 1, 1 - b)
                    alone(sp, a_src_relu, i + 2, sp_passed)
                    sp.dma_start(s_tiles[i + 1, :, :, :], rows4(SR[:, 1 - b, :])).then_inc(a_src_stored[1 - b], 16)
                if not (isinstance(i, int) and i == 0):
                    alone(sp, a_x1_relu, i + 0, sp_passed)
                    sp.dma_start(f_tiles[i - 1, :, :, :], rows4(F1[:, 1 - b, :])).then_inc(a_f1_stored[1 - b], 16)
                alone(sp, a_x1, i + 1, sp_passed)
                sp.dma_start(x1_tiles[i, :, :, :], rows4(X1[:, b, :])).then_inc(a_x1_stored[b], 16)

            sp.wait_ge(a_open, 2)
            edge_load(0, 0)
            sp.wait_ge(a_src_relu, 1)
            sp.dma_start(s_tiles[0, :, :, :], rows4(SR[:, 0, :])).then_inc(a_src_stored[0], 16)
            run(sp, attend, ET, 3)
            sp.wait_ge(a_x1_relu, ET)
            sp.dma_start(f_tiles[ET - 1, :, :, :], rows4(F1[:, (ET - 1) % 2, :])).then_inc(a_f1_stored[(ET - 1) % 2], 16)

            for t in range(STEPS):
                c = t * ET

                def step(i, b, last):
                    if t < STEPS - 1:
                        alone(sp, b_h_copied, i + (c + 1), sp_passed)
                        sp.dma_start(hs_tiles[t + 1][i, :, :, :], rows4(HR[:, b, :])).then_inc(b_h_stored[b], 16)
                    else:
                        alone(sp, b_o, i - 1, sp_passed)
                        sp.dma_start(rows4(XB[:, b, :]), x1_tiles[i, :, :, :]).then_inc(b_x1_in[b], 16)
                if t == STEPS - 1:
                    sp.wait_ge(b_open, 1)
                run(sp, step, ET, 3)
            sp.wait_ge(edges_in, 32)

        @block.gpsimd
        def _(pool):
            nc.gpsimd.iota(slot_iota[:], pattern=[[P, NB]], base=0, channel_multiplier=1).then_inc(iota_done, 1)
            p = nc.gpsimd
            p.memset(zero_i[:], 0).then_inc(iota_done, 1)
            p.memset(halves[:], 0.5).then_inc(iota_done, 1)
            p.memset(inv_d[:], 1.0 / D).then_inc(iota_done, 1)
            p.memset(eps[:], EPS).then_inc(iota_done, 1)
            p.memset(minus_half[:], -0.5).then_inc(iota_done, 1)
            pool.wait_ge(iota_done, 6)

            def moments(st, mean_out, rstd_out, n, before):
                c = [mom[:, i, 0:n] for i in range(4)]
                p.tensor_tensor(c[0], st[:, :, 1], st[:, :, 4], ALU.add)
                p.tensor_tensor(c[1], st[:, :, 1], st[:, :, 4], ALU.subtract)
                p.tensor_tensor(c[2], st[:, :, 2], st[:, :, 5], ALU.add).then_inc(mom_done, 1)
                pool.wait_ge(mom_done, before + 1)
                p.tensor_tensor(mean_out, c[0], halves[:, 0:n], ALU.mult)
                p.tensor_tensor(c[1], c[1], halves[:, 0:n], ALU.mult)
                p.tensor_tensor(c[2], c[2], inv_d[:, 0:n], ALU.mult).then_inc(mom_done, 1)
                pool.wait_ge(mom_done, before + 2)
                p.tensor_tensor(c[1], c[1], c[1], ALU.mult)
                p.tensor_tensor(c[2], c[2], eps[:, 0:n], ALU.add).then_inc(mom_done, 1)
                pool.wait_ge(mom_done, before + 3)
                p.tensor_tensor(c[3], c[1], c[2], ALU.add).then_inc(mom_done, 1)
                pool.wait_ge(mom_done, before + 4)
                return p.tensor_tensor(rstd_out, c[3], minus_half[:, 0:n], ALU.pow)

            def dense_rstd(g, l):
                pool.wait_ge(d_stat, lane(g, l))
                pool.wait_ge(d_normed, g * LANES + (l + 1 - LANES)) if not (isinstance(g, int) and g == 0) else None
                moments(stats[:, l, :, :], mean[:, l, :], rstd[:, l, :], J, lane(g, l) * 4 - 4).then_inc(d_rstd, 1)

            for l in range(LANES):
                dense_rstd(0, l)
            pool.wait_ge(idx_ready, 1)
            pool.wait_ge(zero_stored, 16)
            goes = NB // TB
            of_go = lambda k: slice(k * TB, (k + 1) * TB) if isinstance(k, int) else bass.ds(k * TB, TB)

            def put(k):
                p.tensor_copy(table_stage[:, 0, :], put_idx[:, of_go(k)]).then_inc(m_staged, 1)
                p.tensor_copy(table_stage[:, 1, :], slot1[:, of_go(k)]).then_inc(m_staged, 1)
                alone(pool, m_staged, k * 2 + 2, pool_passed)
                for c in range(TB):
                    p.indirect_dma_start(first_slot, bass.IndirectOffsetOnAxis(ap=table_stage[:, 0, c:c + 1], axis=0),
                                         table_stage[:, 1, c:c + 1], None, bounds_check=N - 1,
                                         oob_is_err=False).then_inc(m_put, 16)
                pool.wait_ge(m_put, k * (16 * TB) + 16 * TB)

            def get(k):
                p.tensor_copy(table_stage[:, 0, :], src_idx[:, of_go(k)]).then_inc(m_staged, 1)
                alone(pool, m_staged, k + (2 * goes + 1), pool_passed)
                for c in range(TB):
                    p.indirect_dma_start(table_stage[:, 1, c:c + 1], None, first_slot,
                                         bass.IndirectOffsetOnAxis(ap=table_stage[:, 0, c:c + 1], axis=0),
                                         ).then_inc(m_got, 16)
                pool.wait_ge(m_got, k * (16 * TB) + 16 * TB)
                p.tensor_copy(got_slot[:, of_go(k)], table_stage[:, 1, :]).then_inc(got_ready, 1)
                pool.wait_ge(got_ready, k + 1)

            def dense_group(g):
                for l in range(LANES):
                    dense_rstd(g + 1, l)

            with pool.Fori(0, goes) as g:
                dense_group(g)
                put(g)
            with pool.Fori(0, goes) as g:
                dense_group(g + goes)
                get(g)
            with pool.Fori(2 * goes, NG - 1) as g:
                dense_group(g)

            pool.wait_ge(d_o, LANES * NG)
            pool.wait_ge(d_h_copied, 2 * LANES * NG)
            for b in range(2):
                pool.wait_ge(d_h_stored[b], 16 * LANES * NG)
                pool.wait_ge(d_o_stored[b], 8 * LANES * NG)
            p.memset(win[:, 0, 0:1], -1).then_inc(a_open, 1)
            p.memset(MX[:, 0, 0:1], 0.0).then_inc(a_open, 1)
            pool.wait_ge(a_open, 2)

            def fetch(i, b):
                if not (isinstance(i, int) and i < 2):
                    pool.wait_ge(a_src_turned, i - 1)
                    pool.wait_ge(a_src_relu, i - 1)
                    pool.wait_ge(a_dst_normed, i - 1)
                    pool.wait_ge(a_kept, i - 1)
                    pool.wait_ge(a_stat, i - 1)
                ks = slice(i * J, (i + 1) * J) if isinstance(i, int) else bass.ds(i * J, J)
                p.tensor_copy(row_stage[:, b, 0, :], src_idx[:, ks]).then_inc(a_staged, 1)
                p.tensor_copy(row_stage[:, b, 1, :], dst_idx[:, ks]).then_inc(a_staged, 1)
                alone(pool, a_staged, i * 2 + 2, pool_passed)
                for w, rows in enumerate((XS, XD)):
                    for j in range(J):
                        p.indirect_dma_start(rows[:, b, j * D:(j + 1) * D], None, x,
                                             bass.IndirectOffsetOnAxis(ap=row_stage[:, b, w, j:j + 1], axis=0),
                                             ).then_inc(a_rows_in[b], 16)

            dense_moments = 4 * LANES * NG

            def edge_rstd(i):
                pool.wait_ge(a_stat, i + 1)
                need(pool, a_dst_normed, i)
                moments(a_stats[:, 0:2 * J, :], a_mean[:, 0:2 * J], a_rstd[:, 0:2 * J], 2 * J,
                        dense_moments if isinstance(i, int) and i == 0 else i * 8 + (dense_moments - 4)
                        ).then_inc(a_rstd_ready, 1)

            def x1_rstd(i, last):
                pool.wait_ge(a_x1_stat, i + 1)
                need(pool, a_x1_normed, i)
                moments(a_stats[:, 2 * J:3 * J, :], a_mean[:, 2 * J:3 * J], a_rstd[:, 2 * J:3 * J], J,
                        i * 8 + (dense_moments + (4 if last else 8))).then_inc(a_x1_rstd, 1)

            def attend(i, b, last):
                if not last:
                    edge_rstd(i + 1)
                if not (isinstance(i, int) and i + 2 >= ET):
                    fetch(i + 2, b)
                x1_rstd(i, last)

            fetch(0, 0)
            fetch(1, 1)
            edge_rstd(0)
            run(pool, attend, ET, 3)

            pool.wait_ge(a_feat, ET)
            pool.wait_ge(a_types, ET)
            for b, n in ((0, (ET + 1) // 2), (1, ET // 2)):
                pool.wait_ge(a_src_stored[b], 16 * n)
                pool.wait_ge(a_x1_stored[b], 16 * n)
                pool.wait_ge(a_f1_stored[b], 16 * n)
            pool.wait_ge(b_idx, 1)
            pool.sem_inc(b_open, 1)
            for t in range(STEPS):
                c = t * ET

                def fetch(i, b):
                    if not (isinstance(i, int) and i < 2):
                        pool.wait_ge(b_turned, i + (c - 1))
                    ks = slice(i * J, (i + 1) * J) if isinstance(i, int) else bass.ds(i * J, J)
                    p.tensor_copy(row_stage[:, b, 0, :], (h_idx if t else h0_idx)[:, ks]).then_inc(b_staged, 1)
                    alone(pool, b_staged, i + (c + 1), pool_passed)
                    for j in range(J):
                        p.indirect_dma_start(HG[:, b, j * D:(j + 1) * D], None, h_rows[t],
                                             bass.IndirectOffsetOnAxis(ap=row_stage[:, b, 0, j:j + 1], axis=0),
                                             ).then_inc(b_rows_in[b], 16)

                def put_rows(i, b):
                    ks = slice(i * J, (i + 1) * J) if isinstance(i, int) else bass.ds(i * J, J)
                    need(pool, b_o_put[b], i * 32 if b == 0 else (i - 1) * 32)
                    p.tensor_copy(row_stage[:, b, 1, :], put_idx[:, ks]).then_inc(b_o_staged, 1)
                    alone(pool, b_o_staged, i + 1, pool_passed)
                    alone(pool, b_o, i + 1, pool_passed)
                    for j in range(J):
                        p.indirect_dma_start(out, bass.IndirectOffsetOnAxis(ap=row_stage[:, b, 1, j:j + 1], axis=0),
                                             OB[:, b, j * D:(j + 1) * D], None, bounds_check=N - 1,
                                             oob_is_err=False).then_inc(b_o_put[b], 16)

                def step(i, b, last):
                    if not (isinstance(i, int) and i + 2 >= ET):
                        fetch(i + 2, b)
                    if t == STEPS - 1 and not (isinstance(i, int) and i == 0):
                        put_rows(i - 1, 1 - b)

                if t:
                    pool.wait_ge(b_turned, c)
                    for b, n in ((0, (ET + 1) // 2), (1, ET // 2)):
                        pool.wait_ge(b_h_stored[b], 16 * n * t)
                fetch(0, 0)
                fetch(1, 1)
                run(pool, step, ET, 3)
            put_rows(ET - 1, (ET - 1) % 2)
            for b, n in ((0, (ET + 1) // 2), (1, ET // 2)):
                pool.wait_ge(b_o_put[b], 16 * J * n)

        @block.vector
        def _(dve):
            v = nc.vector
            chained = [0]

            def chain(ins):
                chained[0] += 1
                ins.then_inc(setup, 1)
                dve.wait_ge(setup, chained[0])

            chain(v.memset(nxt_row[:], -1))
            dve.wait_ge(weights_in, 16 * n_weights)
            chain(v.tensor_tensor(bias_g[:, :], bias_i[:, :], bias_h[:, :], ALU.add))
            for i in range(2):
                chain(v.tensor_scalar(amat[:, i, :], headmask[:], acol[:, i:i + 1], None, ALU.mult))
            chain(v.tensor_copy(bet_part[:, 0, :], bet12[:]))
            chain(v.tensor_tensor(bet_rest[:, 0, :], bet12[:], bet_part[:, 0, :], ALU.subtract))
            chain(v.tensor_copy(bet_part[:, 1, :], bet_rest[:, 0, :]))
            chain(v.tensor_tensor(bet_rest[:, 1, :], bet_rest[:, 0, :], bet_part[:, 1, :], ALU.subtract))
            chain(v.tensor_copy(bet_part[:, 2, :], bet_rest[:, 1, :]))
            chain(v.tensor_scalar(bet_mix[:, 0, :], bet_part[:, 0, :], split_mask[:, 0:1], None, ALU.mult))
            for i in (1, 2):
                chain(v.scalar_tensor_tensor(out=bet_mix[:, i, :], in0=bet_part[:, i, :], scalar=split_mask[:, i:i + 1],
                                             in1=bet_mix[:, i - 1, :], op0=ALU.mult, op1=ALU.add))
            chain(v.tensor_copy(Bet[:], bet_mix[:, 2, :]))
            chain(v.tensor_copy(num_row[:, 0, :], src_row[:]))
            chain(v.tensor_copy(num_row[:, 1, :], dst_row[:]))
            dve.wait_ge(edges_in, 32)
            v.tensor_tensor(num_row[:, 2, :], dst_row[:], nxt_row[:], ALU.is_equal).then_inc(idx_steps, 1)
            dve.wait_ge(rows_turned, 1)
            v.tensor_copy(edge_cols[:, :, :], banks[7][0:P, 0:3 * NB].rearrange("p (a b) -> p a b", a=3)).then_inc(idx_steps, 1)
            dve.wait_ge(idx_steps, 2)
            v.tensor_copy(src_idx[:], edge_cols[:, 0, :])
            v.tensor_copy(dst_idx[:], edge_cols[:, 1, :])
            v.scalar_tensor_tensor(out=put_idx[:], in0=edge_cols[:, 2, :], scalar=float(SKIP), in1=edge_cols[:, 1, :],
                                   op0=ALU.mult, op1=ALU.add)
            dve.wait_ge(iota_done, 6)
            v.tensor_scalar(slot1[:], slot_iota[:], 1.0, None, ALU.add)
            v.tensor_scalar(plain_row[:, 0, :], slot_iota[:], float(E + 1), None, ALU.add)
            v.tensor_scalar(plain_row[:, 1, :], edge_cols[:, 0, :], float(E + 1), None, ALU.add).then_inc(idx_ready, 1)
            dve.wait_ge(wse_mm, 1)
            v.tensor_copy(Wse[:, :, :], banks[6][:, 0:2 * D].rearrange("p (a b) -> p a b", a=2)).then_inc(wse_ready, 1)

            def group(g, par, last):
                for s in range(STEPS):
                    for l in range(LANES):
                        dense_unit(g, par, s, l)
                        if s == 1 and not last:
                            dense_stats(g + 1, 1 - par, l)
                        if s == 2 and not last:
                            dense_norm(g + 1, 1 - par, l)
                finish_unit(g, par, STEPS - 1, LANES - 1)
                for l in range(LANES):
                    b = l % 2
                    dve.wait_ge(d_gate, lane(g, l))
                    dve.wait_ge(d_mm, mm_count(g, STEPS, l, 1))
                    need(dve, d_o_turned, g * LANES + (l - 1))
                    v.scalar_tensor_tensor(out=Qo[:, b, :], in0=banks[3 * b + 1][:, 0:T], scalar=jbias[:, 0:1],
                                           in1=Gt[:, b, :], op0=ALU.add, op1=ALU.mult).then_inc(d_q, 1)
                    if l >= 1:
                        residual(g, par, l - 1)
                residual(g, par, LANES - 1)

            def residual(g, par, l):
                b = l % 2
                dve.wait_ge(d_o_turned, lane(g, l))
                need(dve, d_o_stored[b], g * 32 + 16 * (l // 2))
                v.tensor_tensor(XO[:, b, :], Xd[:, par * LANES + l, :, :].rearrange("p j f -> p (j f)"),
                                banks[7][0:P, :], ALU.add).then_inc(d_o, 1)

            def dense_unit(g, par, s, l):
                q = s * LANES + l
                b = l % 2
                H_in = Fd[:, par * LANES + l, :] if s == 0 else Hd[:, l, :]
                dve.wait_ge(d_mm, mm_count(g, s, l, 2))
                dve.wait_ge(d_r, unit(g, s, l))
                v.scalar_tensor_tensor(out=banks[3 * b + 2][:, 0:T], in0=banks[3 * b + 2][:, 0:T], scalar=bias_h[:, 2:3],
                                       in1=Rg[:, b, :], op0=ALU.add, op1=ALU.mult).then_inc(d_m, 1)
                need(dve, d_h, g * GU + (q - 1))
                dve.wait_ge(d_z, unit(g, s, l))
                v.tensor_tensor(Keep[:, b, :], Zg[:, b, :], H_in, ALU.mult).then_inc(d_keep, 1)
                if q >= 1:
                    finish_unit(g, par, (q - 1) // LANES, (q - 1) % LANES)

            def finish_unit(g, par, s, l):
                b = l % 2
                dve.wait_ge(d_n, unit(g, s, l))
                v.scalar_tensor_tensor(out=Take[:, b, :], in0=Zg[:, b, :], scalar=1.0, in1=Ng[:, b, :],
                                       op0=ALU.subtract, op1=ALU.mult).then_inc(d_take, 1)
                dve.wait_ge(d_take, unit(g, s, l))
                dve.wait_ge(d_keep, unit(g, s, l))
                v.tensor_tensor(Hd[:, l, :], Keep[:, b, :], Take[:, b, :], ALU.subtract).then_inc(d_h, 1)

            def dense_stats(g, par, l):
                X = Xd[:, par * LANES + l, :, :]
                dve.wait_ge(d_x_in[l], g * 16 + 16)
                need(dve, d_rstd, g * LANES + (l + 1 - LANES))
                for j in range(J):
                    ins = v.bn_stats(stats[:, l, j, :], X[:, j, :])
                ins.then_inc(d_stat, 1)

            def dense_norm(g, par, l):
                X = Xd[:, par * LANES + l, :, :]
                dve.wait_ge(d_rstd, lane(g, l))
                need(dve, d_x_turned, g * LANES + (l - 1))
                for j in range(J):
                    ins = v.tensor_scalar(Nx[:, l % 2, j * D:(j + 1) * D], X[:, j, :], mean[:, l, j:j + 1], rstd[:, l, j:j + 1],
                                          ALU.subtract, ALU.mult)
                ins.then_inc(d_normed, 1)

            for l in range(LANES):
                dense_stats(0, 0, l)
            for l in range(LANES):
                dense_norm(0, 0, l)
            run(dve, group, NG)

            def stats_of(i, b):
                dve.wait_ge(a_rows_in[b], uses(i, b, 128) + 128)
                need(dve, a_rstd_ready, i)
                for w, rows in enumerate((XS, XD)):
                    for j in range(J):
                        ins = v.bn_stats(a_stats[:, w * J + j, :], rows[:, b, j * D:(j + 1) * D])
                ins.then_inc(a_stat, 1)

            def norm_of(i, b):
                dve.wait_ge(a_rstd_ready, i + 1)
                for j in range(J):
                    js = slice(j * D, (j + 1) * D)
                    ins = v.tensor_scalar(XS[:, b, js], XS[:, b, js], a_mean[:, j:j + 1], a_rstd[:, j:j + 1],
                                          ALU.subtract, ALU.mult)
                ins.then_inc(a_src_normed, 1)
                need(dve, a_dst_turned, i)
                for j in range(J):
                    js = slice(j * D, (j + 1) * D)
                    ins = v.tensor_scalar(ND[:, js], XD[:, b, js], a_mean[:, J + j:J + j + 1],
                                          a_rstd[:, J + j:J + j + 1], ALU.subtract, ALU.mult)
                ins.then_inc(a_dst_normed, 1)

            def x1_norm(i, b):
                dve.wait_ge(a_x1_rstd, i + 1)
                need(dve, a_x1_turned, i)
                need(dve, a_x1_relu, i)
                for j in range(J):
                    js = slice(j * D, (j + 1) * D)
                    ins = v.tensor_scalar(N1[:, js], X1[:, b, js], a_mean[:, 2 * J + j:2 * J + j + 1],
                                          a_rstd[:, 2 * J + j:2 * J + j + 1], ALU.subtract, ALU.mult)
                ins.then_inc(a_x1_normed, 1)

            def attend(i, b, last):
                first = isinstance(i, int) and i == 0
                at = lambda step: dve.wait_ge(a_dve, a_count(i, step))
                if not last:
                    stats_of(i + 1, 1 - b)
                dve.wait_ge(a_scaled, i + 1)
                v.tensor_tensor(LG[:, b, :], banks[2][:, 0:T], LS[:], ALU.max).then_inc(a_dve, 1)
                dve.wait_ge(a_edges_in[b], uses(i, b, 32) + 32)
                v.tensor_tensor(same[:, all_of(i)], win[:, b, 1:T + 1], win[:, b, 0:T], ALU.is_equal).then_inc(a_dve, 1)
                at("same")
                v.tensor_scalar(BK[:], same[:, all_of(i)], 1.0, FAR, ALU.subtract, ALU.mult).then_inc(a_dve, 1)
                if first:
                    v.tensor_copy(MX[:, 0, 0:1], MX[:, 0, 0:1]).then_inc(a_dve, 1)
                else:
                    v.tensor_copy(MX[:, b, 0:1], MX[:, 1 - b, T:T + 1]).then_inc(a_dve, 1)
                at("carry")
                v.tensor_tensor_scan(MX[:, b, 1:T + 1], BK[:], LG[:, b, :], MX[:, b, 0:1], ALU.add, ALU.max).then_inc(a_dve, 1)
                at("max")
                need(dve, a_decay, i)
                v.tensor_tensor(EA[:], MX[:, b, 0:T], BK[:], ALU.add).then_inc(a_dve, 1)
                at("lift")
                v.tensor_tensor(EA[:], EA[:], MX[:, b, 1:T + 1], ALU.subtract).then_inc(a_dve, 1)
                need(dve, a_weight, i)
                v.tensor_tensor(EB[:], LG[:, b, :], MX[:, b, 1:T + 1], ALU.subtract).then_inc(a_dve, 1)
                if not last:
                    norm_of(i + 1, 1 - b)
                if not first:
                    x1_norm(i - 1, 1 - b)
                dve.wait_ge(a_weight, i + 1)
                dve.wait_ge(a_value_mm, i + 1)
                v.tensor_tensor(WV[:], WT[:], banks[3 + b][:, 0:T], ALU.mult).then_inc(a_dve, 1)
                dve.wait_ge(a_decay, i + 1)
                v.tensor_tensor_scan(SD[:, b, :], CF[:], WT[:], 0.0 if first else SD[:, 1 - b, T - 1:T], ALU.mult,
                                     ALU.add).then_inc(a_dve, 1)
                at("weighted")
                v.tensor_tensor_scan(SN[:, b, :], CF[:], WV[:], 0.0 if first else SN[:, 1 - b, T - 1:T], ALU.mult,
                                     ALU.add).then_inc(a_dve, 1)
                need(dve, a_att_turned, i)
                at("sum_w")
                v.reciprocal(AO[:], SD[:, b, :]).then_inc(a_dve, 1)
                at("inverse")
                v.tensor_tensor(AO[:], SN[:, b, :], AO[:], ALU.mult).then_inc(a_dve, 1)
                dve.wait_ge(a_att_turned, i + 1)
                dve.wait_ge(a_kept, i + 1)
                need(dve, a_x1_stored[b], uses(i, b, 16))
                v.tensor_tensor(X1[:, b, :], XK[:, b, :], banks[5][0:P, :], ALU.add).then_inc(a_x1, 1)
                dve.wait_ge(a_x1, i + 1)
                need(dve, a_x1_rstd, i)
                for j in range(J):
                    ins = v.bn_stats(a_stats[:, 2 * J + j, :], X1[:, b, j * D:(j + 1) * D])
                ins.then_inc(a_x1_stat, 1)

            stats_of(0, 0)
            norm_of(0, 0)
            run(dve, attend, ET, 3)
            x1_norm(ET - 1, (ET - 1) % 2)

            dve.wait_ge(got_ready, NB // TB)
            for w, idx in enumerate((h0_idx, h_idx)):
                v.scalar_tensor_tensor(out=edge_cols[:, w, :], in0=got_slot[:], scalar=0.0, in1=plain_row[:, w, :],
                                       op0=ALU.is_equal, op1=ALU.mult).then_inc(b_idx_steps, 1)
                dve.wait_ge(b_idx_steps, 2 * w + 1)
                v.scalar_tensor_tensor(out=idx[:], in0=got_slot[:], scalar=-1.0, in1=edge_cols[:, w, :],
                                       op0=ALU.add, op1=ALU.add).then_inc(b_idx_steps, 1)
            dve.wait_ge(b_idx_steps, 4)
            dve.sem_inc(b_idx, 1)

            for t in range(STEPS):
                c = t * ET
                state = H if t else F

                def mask(i, b):
                    dve.wait_ge(b_turned, i + (c + 1))
                    need(dve, b_msg, i + c)
                    for k in range(K):
                        ins = v.scalar_tensor_tensor(out=MK[:, k, :], in0=types[:, all_of(i)], scalar=float(k),
                                                     in1=banks[0][:, 0:T], op0=ALU.is_equal, op1=ALU.mult)
                    ins.then_inc(b_masked, 1)
                    v.tensor_scalar(hot[:, b, :], types[0:12, all_of(i)], part_type[:, 0:1], None,
                                    ALU.is_equal).then_inc(b_hot, 1)

                def sum_messages(i, b):
                    first = isinstance(i, int) and i == 0
                    dve.wait_ge(b_msg, i + (c + 1))
                    need(dve, b_n_mm, max(i + c - 1, c) if isinstance(i, int) else i + (c - 1))
                    if not first:
                        dve.wait_ge(b_sum, i + c)
                    v.tensor_tensor_scan(AG[:, b, :], same[:, all_of(i)], banks[1][:, 0:T],
                                         0.0 if first else AG[:, 1 - b, T - 1:T], ALU.mult, ALU.add).then_inc(b_sum, 1)

                def readout(i, b):
                    dve.wait_ge(b_gate, i + 1)
                    dve.wait_ge(b_j_mm, i + 1)
                    need(dve, b_q_turned, i)
                    v.scalar_tensor_tensor(out=Qs[:], in0=banks[7][:, 0:T], scalar=jbias[:, 0:1], in1=Gs[:],
                                           op0=ALU.add, op1=ALU.mult).then_inc(b_q, 1)

                def residual(i, b):
                    dve.wait_ge(b_q_turned, i + 1)
                    dve.wait_ge(b_x1_in[b], uses(i, b, 16) + 16)
                    need(dve, b_o_put[b], uses(i, b, 16 * J))
                    v.tensor_tensor(OB[:, b, :], XB[:, b, :], banks[6][0:P, :], ALU.add).then_inc(b_o, 1)

                def step(i, b, last):
                    first = isinstance(i, int) and i == 0
                    if not last:
                        mask(i + 1, 1 - b)
                    if t == STEPS - 1 and not first:
                        readout(i - 1, 1 - b)
                    dve.wait_ge(b_own_mm, i + (c + 1))
                    dve.wait_ge(b_r, i + (c + 1))
                    need(dve, b_m2, i + c)
                    v.scalar_tensor_tensor(out=Ms[:], in0=banks[4][:, 0:T], scalar=bias_h[:, 2:3], in1=Rs[:],
                                           op0=ALU.add, op1=ALU.mult).then_inc(b_m1, 1)
                    dve.wait_ge(b_m1, i + (c + 1))
                    dve.wait_ge(b_n_mm, i + (c + 1))
                    v.tensor_tensor(banks[5][:, 0:T], Ms[:], banks[5][:, 0:T], ALU.add).then_inc(b_m2, 1)
                    dve.wait_ge(b_z, i + (c + 1))
                    need(dve, b_h, i + c)
                    if t:
                        dve.wait_ge(b_h_kept, i + (c - ET + 1))
                    v.tensor_tensor(Ks[:], Zs[:], state[:, all_of(i)], ALU.mult).then_inc(b_keep, 1)
                    if t == STEPS - 1 and not first:
                        residual(i - 1, 1 - b)
                    dve.wait_ge(b_n, i + (c + 1))
                    v.scalar_tensor_tensor(out=Ts[:], in0=Zs[:], scalar=1.0, in1=Ns[:], op0=ALU.subtract,
                                           op1=ALU.mult).then_inc(b_take, 1)
                    dve.wait_ge(b_take, i + (c + 1))
                    if t < STEPS - 1:
                        need(dve, b_h_kept, i + c)
                        need(dve, b_h_turned, i + c)
                    elif first:
                        dve.wait_ge(b_h_kept, c)
                        dve.wait_ge(b_h_turned, c)
                    else:
                        dve.wait_ge(b_j_mm, i)
                    v.tensor_tensor(HN[:], Ks[:], Ts[:], ALU.subtract).then_inc(b_h, 1)
                    if not last:
                        sum_messages(i + 1, 1 - b)

                mask(0, 0)
                sum_messages(0, 0)
                run(dve, step, ET, 3)
            readout(ET - 1, (ET - 1) % 2)
            residual(ET - 1, (ET - 1) % 2)

        @block.scalar
        def _(act):
            a = nc.scalar
            act.wait_ge(setup, 2)

            def feature_copy(g, par, l):
                act.wait_ge(d_x_turned, lane(g, l))
                a.activation(Fd[:, par * LANES + l, :], banks[6][:, 0:T], ACT.Relu).then_inc(d_feat, 1)

            def tanh_of(g, s, l):
                b = l % 2
                act.wait_ge(d_m, unit(g, s, l))
                a.activation(Ng[:, b, :], banks[3 * b + 2][:, 0:T], ACT.Tanh, bias=bias_i[:, 2:3]).then_inc(d_n, 1)

            def dense_unit(g, par, s, l):
                b = l % 2
                if s >= 1:
                    i = (s - 1) * LANES + l
                    act.wait_ge(d_h_turned, g * 8 + (i + 1))
                    need(act, d_h_stored[b], g * 64 + 16 * (i // 2))
                    a.activation(HO[:, b, :], banks[7][0:P, :], ACT.Copy).then_inc(d_h_copied, 1)
                q = s * LANES + l
                need(act, d_m, g * GU + (q - 1))
                act.wait_ge(d_mm, mm_count(g, s, l, 0))
                a.activation(Rg[:, b, :], banks[3 * b][:, 0:T], ACT.Sigmoid, bias=bias_g[:, 0:1]).then_inc(d_r, 1)
                act.wait_ge(d_mm, mm_count(g, s, l, 1))
                need(act, d_take, g * GU + (q - 1))
                a.activation(Zg[:, b, :], banks[3 * b + 1][:, 0:T], ACT.Sigmoid, bias=bias_g[:, 1:2]).then_inc(d_z, 1)
                if q >= 1:
                    tanh_of(g, (q - 1) // LANES, (q - 1) % LANES)

            def group(g, par, last):
                for s in range(STEPS):
                    for l in range(LANES):
                        dense_unit(g, par, s, l)
                        if s == STEPS - 1 and l >= 1 and not last:
                            feature_copy(g + 1, 1 - par, l - 1)
                tanh_of(g, STEPS - 1, LANES - 1)
                for l in range(LANES):
                    b = l % 2
                    act.wait_ge(d_mm, mm_count(g, STEPS, l, 0))
                    need(act, d_q, g * LANES + (l - 1))
                    a.activation(Gt[:, b, :], banks[3 * b][:, 0:T], ACT.Sigmoid, bias=ibias[:, 0:1]).then_inc(d_gate, 1)
                    if l == 0 and not last:
                        feature_copy(g + 1, 1 - par, LANES - 1)

            for l in range(LANES):
                feature_copy(0, 0, l)
            run(act, group, NG)

            def sources(i, b):
                act.wait_ge(a_rows_in[b], uses(i, b, 128) + 128)
                need(act, a_x1, i - 1)
                a.activation(XK[:, b, :], XD[:, b, :], ACT.Copy).then_inc(a_kept, 1)
                act.wait_ge(a_src_normed, i + 1)
                need(act, a_src_stored[b], uses(i, b, 16))
                a.activation(SR[:, b, :], XS[:, b, :], ACT.Relu).then_inc(a_src_relu, 1)
                act.wait_ge(a_src_turned, i + 1)
                need(act, a_value_mm, i)
                a.activation(ST[:], banks[0][:, 0:T], ACT.Relu).then_inc(a_src_feat, 1)
                act.wait_ge(a_dst_turned, i + 1)
                need(act, a_logit_mm, i)
                a.activation(DT[:], banks[1][:, 0:T], ACT.Relu).then_inc(a_dst_feat, 1)
                act.wait_ge(a_logit_mm, i + 1)
                need(act, a_dve, a_count(i - 1, "leaky"))
                a.activation(LS[:], banks[2][:, 0:T], ACT.Copy, scale=SLOPE).then_inc(a_scaled, 1)

            def new_rows(i, b):
                act.wait_ge(a_x1_normed, i + 1)
                need(act, a_f1_stored[b], uses(i, b, 16))
                a.activation(F1[:, b, :], N1[:], ACT.Relu).then_inc(a_x1_relu, 1)
                act.wait_ge(a_x1_turned, i + 1)
                a.activation(F[:, all_of(i)], banks[6][:, 0:T], ACT.Relu).then_inc(a_feat, 1)

            def attend(i, b, last):
                act.wait_ge(a_dve, a_count(i, "decay_arg"))
                need(act, a_dve, a_count(i - 1, "sum_v"))
                a.activation(CF[:], EA[:], ACT.Exp).then_inc(a_decay, 1)
                act.wait_ge(a_dve, a_count(i, "weight_arg"))
                a.activation(WT[:], EB[:], ACT.Exp).then_inc(a_weight, 1)
                act.wait_ge(a_edges_in[b], uses(i, b, 32) + 32)
                a.activation(types[:, all_of(i)], typ[:, b, :], ACT.Copy).then_inc(a_types, 1)
                if not last:
                    sources(i + 1, 1 - b)
                if not (isinstance(i, int) and i == 0):
                    new_rows(i - 1, 1 - b)

            sources(0, 0)
            run(act, attend, ET, 3)
            new_rows(ET - 1, (ET - 1) % 2)

            for t in range(STEPS):
                c = t * ET

                def step(i, b, last):
                    act.wait_ge(b_r_mm, i + (c + 1))
                    need(act, b_m1, i + c)
                    a.activation(Rs[:], banks[2][:, 0:T], ACT.Sigmoid, bias=bias_g[:, 0:1]).then_inc(b_r, 1)
                    act.wait_ge(b_z_mm, i + (c + 1))
                    need(act, b_take, i + c)
                    a.activation(Zs[:], banks[3][:, 0:T], ACT.Sigmoid, bias=bias_g[:, 1:2]).then_inc(b_z, 1)
                    act.wait_ge(b_m2, i + (c + 1))
                    a.activation(Ns[:], banks[5][:, 0:T], ACT.Tanh, bias=bias_i[:, 2:3]).then_inc(b_n, 1)
                    if t < STEPS - 1:
                        act.wait_ge(b_h, i + (c + 1))
                        a.activation(H[:, all_of(i)], HN[:], ACT.Copy).then_inc(b_h_kept, 1)
                        act.wait_ge(b_h_turned, i + (c + 1))
                        need(act, b_h_stored[b], uses(i, b, 16) + 16 * t * ((ET + 1 - b) // 2))
                        a.activation(HR[:, b, :], banks[6][0:P, :], ACT.Copy).then_inc(b_h_copied, 1)
                    else:
                        act.wait_ge(b_gate_mm, i + 1)
                        need(act, b_q, i)
                        a.activation(Gs[:], banks[2][:, 0:T], ACT.Sigmoid, bias=ibias[:, 0:1]).then_inc(b_gate, 1)

                run(act, step, ET, 3)

        @block.tensor
        def _(pe):
            m = nc.tensor
            pe.wait_ge(weights_in, 16 * n_weights)
            pe.wait_ge(idx_steps, 1)
            for i in range(3):
                ins = m.transpose(banks[7][0:P, i * NB:(i + 1) * NB], num_row[:, i, :], ident[0:NB, 0:NB])
            ins.then_inc(rows_turned, 1)
            pe.wait_ge(idx_steps, 2)
            for i in range(2):
                ins = m.matmul(banks[6][:, i * D:(i + 1) * D], W0T[:], amat[:, i, :], start=True, stop=True)
            ins.then_inc(wse_mm, 1)
            pe.wait_ge(wse_ready, 1)

            def turn_in(g, l):
                pe.wait_ge(d_normed, lane(g, l))
                need(pe, d_feat, g * LANES + l)
                for j in range(J):
                    ins = m.transpose(banks[6][:, j * P:(j + 1) * P], Nx[:, l % 2, j * D:(j + 1) * D], ident[0:P, 0:P])
                ins.then_inc(d_x_turned, 1)

            def turn_out(src_ap):
                for j in range(J):
                    ins = m.transpose(banks[7][0:P, j * D:(j + 1) * D], src_ap[:, j * P:(j + 1) * P], ident[:])
                return ins

            def group(g, par, last):
                for s in range(STEPS):
                    for l in range(LANES):
                        q = s * LANES + l
                        b = l % 2
                        if s == 0:
                            pe.wait_ge(d_feat, lane(g, l))
                            H_in = Fd[:, par * LANES + l, :]
                        else:
                            pe.wait_ge(d_h, unit(g, s - 1, l))
                            H_in = Hd[:, l, :]
                            i = (s - 1) * LANES + l
                            if i == 0:
                                need(pe, d_o, g * LANES)
                            else:
                                pe.wait_ge(d_h_copied, g * 8 + i)
                            turn_out(H_in).then_inc(d_h_turned, 1)
                        if q >= 2:
                            pe.wait_ge(d_r, g * GU + (q - 1))
                        else:
                            need(pe, d_gate, g * LANES + (l - 1))
                        m.matmul(banks[3 * b][:, 0:T], Whh[:, 0, :], H_in, start=True, stop=True).then_inc(d_mm, 1)
                        if q >= 2:
                            pe.wait_ge(d_z, g * GU + (q - 1))
                        else:
                            need(pe, d_q, g * LANES + (l - 1))
                        m.matmul(banks[3 * b + 1][:, 0:T], Whh[:, 1, :], H_in, start=True, stop=True).then_inc(d_mm, 1)
                        need(pe, d_n, g * GU + (q - 1))
                        m.matmul(banks[3 * b + 2][:, 0:T], Whh[:, 2, :], H_in, start=True, stop=True).then_inc(d_mm, 1)
                        if s == STEPS - 1 and l >= 1 and not last:
                            turn_in(g + 1, l - 1)
                for l in range(LANES):
                    b = l % 2
                    pe.wait_ge(d_h, unit(g, STEPS - 1, l))
                    if l >= 2:
                        pe.wait_ge(d_gate, g * LANES + (l - 1))
                    else:
                        pe.wait_ge(d_r, g * GU + (GU - 1 + l))
                    m.matmul(banks[3 * b][:, 0:T], Wi[:, 0, :], Hd[:, l, :], start=True, stop=False)
                    m.matmul(banks[3 * b][:, 0:T], Wi[:, 1, :], Fd[:, par * LANES + l, :], start=False, stop=True).then_inc(d_mm, 1)
                    if l >= 2:
                        pe.wait_ge(d_q, g * LANES + (l - 1))
                    else:
                        pe.wait_ge(d_z, g * GU + (GU - 1 + l))
                    m.matmul(banks[3 * b + 1][:, 0:T], Wj[:], Hd[:, l, :], start=True, stop=True).then_inc(d_mm, 1)
                    if l == 0 and not last:
                        turn_in(g + 1, LANES - 1)
                    if l >= 1:
                        readout_rows(g, l - 1)
                readout_rows(g, LANES - 1)

            def readout_rows(g, l):
                pe.wait_ge(d_q, lane(g, l))
                if l == 0:
                    pe.wait_ge(d_h_copied, g * 8 + 8)
                else:
                    pe.wait_ge(d_o, lane(g, l - 1))
                turn_out(Qo[:, l % 2, :]).then_inc(d_o_turned, 1)

            for l in range(LANES):
                turn_in(0, l)
            run(pe, group, NG)

            def turn(bank_ap, rows):
                for j in range(J):
                    ins = m.transpose(bank_ap[:, j * P:(j + 1) * P], rows[:, j * D:(j + 1) * D], ident[0:P, 0:P])
                return ins

            def turn_back(bank_ap, cols):
                for j in range(J):
                    ins = m.transpose(bank_ap[0:P, j * D:(j + 1) * D], cols[:, j * P:(j + 1) * P], ident[:])
                return ins

            def sources(i, b):
                pe.wait_ge(a_src_normed, i + 1)
                need(pe, a_src_feat, i)
                turn(banks[0], XS[:, b, :]).then_inc(a_src_turned, 1)
                pe.wait_ge(a_dst_normed, i + 1)
                need(pe, a_dst_feat, i)
                turn(banks[1], ND).then_inc(a_dst_turned, 1)
                pe.wait_ge(a_src_feat, i + 1)
                pe.wait_ge(a_dst_feat, i + 1)
                need(pe, a_dve, a_count(i - 1, "leaky"))
                m.matmul(banks[2][:, 0:T], Wse[:, 0, :], ST[:], start=True, stop=False)
                m.matmul(banks[2][:, 0:T], Wse[:, 1, :], DT[:], start=False, stop=True).then_inc(a_logit_mm, 1)
                need(pe, a_dve, a_count(i - 2, "weighted"))
                m.matmul(banks[3 + b][:, 0:T], W0[:], ST[:], start=True, stop=True).then_inc(a_value_mm, 1)

            def new_rows(i):
                pe.wait_ge(a_x1_normed, i + 1)
                need(pe, a_feat, i)
                turn(banks[6], N1).then_inc(a_x1_turned, 1)

            def attend(i, b, last):
                if not last:
                    sources(i + 1, 1 - b)
                if not (isinstance(i, int) and i == 0):
                    new_rows(i - 1)
                pe.wait_ge(a_dve, a_count(i, "attended"))
                need(pe, a_x1, i)
                turn_back(banks[5], AO).then_inc(a_att_turned, 1)

            sources(0, 0)
            run(pe, attend, ET, 3)
            new_rows(ET - 1)

            for t in range(STEPS):
                c = t * ET
                state = H if t else F

                def fetched(i, b):
                    pe.wait_ge(b_rows_in[b], uses(i, b, 16 * J) + 16 * J * (1 + t * ((ET + 1 - b) // 2)))
                    need(pe, b_masked, i + c)
                    turn(banks[0], HG[:, b, :]).then_inc(b_turned, 1)

                def messages(i, b):
                    pe.wait_ge(b_masked, i + (c + 1))
                    need(pe, b_sum, i + c)
                    for k in range(K):
                        m.matmul(banks[1][:, 0:T], Wet[:, k, :], MK[:, k, :], start=(k == 0), stop=False)
                    pe.wait_ge(b_hot, i + (c + 1))
                    m.matmul(banks[1][:, 0:T], Bet[:], hot[:, b, :], start=False, stop=True).then_inc(b_msg, 1)

                def readout(i):
                    pe.wait_ge(b_h, i + (c + 1))
                    pe.wait_ge(b_r, i + (c + 1))
                    m.matmul(banks[2][:, 0:T], Wi[:, 0, :], HN[:], start=True, stop=False)
                    m.matmul(banks[2][:, 0:T], Wi[:, 1, :], F[:, all_of(i)], start=False, stop=True).then_inc(b_gate_mm, 1)
                    need(pe, b_q, i)
                    m.matmul(banks[7][:, 0:T], Wj[:], HN[:], start=True, stop=True).then_inc(b_j_mm, 1)

                def readout_rows(i):
                    pe.wait_ge(b_q, i + 1)
                    need(pe, b_o, i)
                    turn_back(banks[6], Qs).then_inc(b_q_turned, 1)

                def step(i, b, last):
                    first = isinstance(i, int) and i == 0
                    if not last:
                        fetched(i + 1, 1 - b)
                    own = state[:, all_of(i)]
                    need(pe, b_r, i + c)
                    if t:
                        pe.wait_ge(b_h_kept, i + (c - ET + 1))
                    if t == STEPS - 1:
                        need(pe, b_gate, i)
                    m.matmul(banks[2][:, 0:T], Whh[:, 0, :], own, start=True, stop=False)
                    need(pe, b_z, i + c)
                    m.matmul(banks[3][:, 0:T], Whh[:, 1, :], own, start=True, stop=False)
                    need(pe, b_m1, i + c)
                    m.matmul(banks[4][:, 0:T], Whh[:, 2, :], own, start=True, stop=True).then_inc(b_own_mm, 1)
                    pe.wait_ge(b_sum, i + (c + 1))
                    m.matmul(banks[2][:, 0:T], Wih[:, 0, :], AG[:, b, :], start=False, stop=True).then_inc(b_r_mm, 1)
                    m.matmul(banks[3][:, 0:T], Wih[:, 1, :], AG[:, b, :], start=False, stop=True).then_inc(b_z_mm, 1)
                    need(pe, b_n, i + c)
                    m.matmul(banks[5][:, 0:T], Wih[:, 2, :], AG[:, b, :], start=True, stop=True).then_inc(b_n_mm, 1)
                    if t == STEPS - 1 and not first:
                        readout_rows(i - 1)
                    if not last:
                        messages(i + 1, 1 - b)
                    if t < STEPS - 1:
                        pe.wait_ge(b_h, i + (c + 1))
                        need(pe, b_h_copied, i + c)
                        turn_back(banks[6], HN).then_inc(b_h_turned, 1)
                    else:
                        readout(i)

                fetched(0, 0)
                messages(0, 0)
                run(pe, step, ET, 3)
            readout_rows(ET - 1)


def kernel(**inputs):
    import numpy as np
    import concourse.bacc as bacc
    from concourse.bass_utils import run_bass_kernel_spmd

    a = {k: np.asarray(v) for k, v in inputs.items()}
    cols = lambda v, n: v.reshape(n, D).T
    att = a["L0_gnn_a"]
    arrays = {
        "x": a["x"], "src": a["src"], "dst": a["dst"], "etype": a["edge_type_4"],
        "w0": a["L0_gnn_W"], "w0T": a["L0_gnn_W"].T,
        "a_cols": np.stack([att[:, :32].reshape(D), att[:, 32:].reshape(D)], axis=1),
        "wetT": a["L1_gnn_W_et"].transpose(0, 2, 1), "b_et": a["L1_gnn_b_et"],
        "wihT": a["L1_gnn_W_ih"].T, "bih": cols(a["L1_gnn_b_ih"], 3),
        "whhT": a["L1_gnn_W_hh"].T, "bhh": cols(a["L1_gnn_b_hh"], 3),
        "iwT": a["L1_gnn_i_w"].T, "ib": cols(a["L1_gnn_i_b"], 1),
        "jwT": a["L1_gnn_j_w"].T, "jb": cols(a["L1_gnn_j_b"], 1),
        "ident_in": np.eye(128, dtype=np.float32),
        "headmask_in": np.kron(np.eye(HEADS, dtype=np.float32), np.ones((D // HEADS, D // HEADS), np.float32)),
        "part_type_in": (np.arange(12) % K).astype(np.float32)[:, None],
        "split_in": np.repeat(np.eye(3, dtype=np.float32), K, axis=0),
    }
    arrays = {"in_" + k: np.ascontiguousarray(v) for k, v in arrays.items()}
    nc = bacc.Bacc("TRN2", target_bir_lowering=False, num_devices=1)
    args = [nc.dram_tensor(k, v.shape, mybir.dt.from_np(v.dtype), kind="ExternalInput").ap() for k, v in arrays.items()]
    out = nc.dram_tensor("out_0", a["x"].shape, mybir.dt.float32, kind="ExternalOutput").ap()
    gnn_kernel(nc, *args, out)
    r = run_bass_kernel_spmd(nc, [arrays], core_ids=[0])
    return r.results[0]["out_0"]
```

```python
import concourse.bass as bass
from concourse import mybir
from contextlib import ExitStack

P = 125
J = 4
T = P * J
D = 128
K = 4
HEADS = 4
STEPS = 3
EPS = 1e-5
SLOPE = 0.2
FAR = 3.0e38
LANES = 4
TB = 10
WORK = 13700


def run(eng, body, n, head=1):
    pairs = (n - head - 2) // 2
    for i in range(head):
        body(i, i % 2, False)
    with eng.Fori(0, pairs) as pair:
        body(pair * 2 + head, 1, False)
        body(pair * 2 + (head + 1), 0, False)
    for i in range(head + 2 * pairs, n):
        body(i, i % 2, i == n - 1)


def need(eng, semaphore, value):
    if not isinstance(value, int) or value > 0:
        eng.wait_ge(semaphore, value)


def alone(eng, semaphore, value, passed):
    if not isinstance(value, int) or value > 0:
        eng.wait_ge(semaphore, value)
        eng.sem_inc(passed, 1)


def gnn_kernel(nc, x, src, dst, etype, w0, w0T, a_cols, wetT, b_et, wihT, bih, whhT, bhh, iwT, ib, jwT, jb,
               ident_in, headmask_in, head_pick_in, part_type_in, split_in, out):
    f32, bf16, i32, u8 = mybir.dt.float32, mybir.dt.bfloat16, mybir.dt.int32, mybir.dt.uint8
    ALU, ACT = mybir.AluOpType, mybir.ActivationFunctionType

    N, E = x.shape[0], src.shape[0]
    NT, ET = N // T, E // T
    NG = NT // LANES
    NB = E // P
    SKIP = N + 10000
    GU, RU = STEPS * LANES, LANES
    MMG = 3 * GU + 2 * RU

    ctx = ExitStack()
    with ctx:
        def sb(name, shape, dt=f32):
            return ctx.enter_context(nc.sbuf_tensor(name, shape, dt))

        def bank(name, shape=(128, 512)):
            return ctx.enter_context(nc.psum_tensor(name, list(shape), f32))

        def sem(name):
            return ctx.enter_context(nc.semaphore(name))

        first_slot = nc.dram_tensor("slot_of_node", (N, 1), i32, kind="Internal").ap()
        h0_rows = nc.dram_tensor("h0_rows", (E + 2 * N, D), f32, kind="Internal").ap()
        node_pairs = h0_rows.rearrange("(n two) f -> n (two f)", two=2)
        h_rows = [h0_rows] + [nc.dram_tensor(f"h{t}_rows", (E + N, D), f32, kind="Internal").ap() for t in (1, 2)]
        x1_rows = nc.dram_tensor("x1_rows", (E, D), f32, kind="Internal").ap()

        ident = sb("ident", [128, 128])
        headmask = sb("headmask", [128, 128])
        head_pick = sb("head_pick", [128, HEADS])
        part_type = sb("part_type", [12, 1])
        split_mask = sb("split_mask", [12, 3])
        W0 = sb("W0", [128, D])
        W0T = sb("W0T", [128, D])
        acol = sb("acol", [128, 2])
        amat = sb("amat", [128, 2, D])
        Wse = sb("Wse", [128, 2, D])
        Wet = sb("Wet", [128, K, D])
        Wih = sb("Wih", [128, 3, D])
        Whh = sb("Whh", [128, 3, D])
        Wi = sb("Wi", [128, 2, D])
        Wj = sb("Wj", [128, D])
        bias_i = sb("bias_i", [128, 3])
        bias_h = sb("bias_h", [128, 3])
        bias_g = sb("bias_g", [128, 3])
        ibias = sb("ibias", [128, 1])
        jbias = sb("jbias", [128, 1])
        bet12 = sb("bet12", [12, D])
        bet_rest = sb("bet_rest", [12, 2, D])
        bet_part = sb("bet_part", [12, 3, D], bf16)
        bet_mix = sb("bet_mix", [12, 3, D])
        Bet = sb("Bet", [12, D], bf16)

        src_row = sb("src_row", [NB, P], i32)
        dst_row = sb("dst_row", [NB, P], i32)
        nxt_row = sb("nxt_row", [NB, P], i32)
        num_row = sb("num_row", [NB, 4, P])
        slot_iota = sb("slot_iota", [P, NB], i32)
        slot_no = sb("slot_no", [P, NB])
        edge_cols = sb("edge_cols", [P, 3, NB])
        src_idx = sb("src_idx", [P, NB], i32)
        src_row_idx = sb("src_row_idx", [P, NB], i32)
        dst_pair_idx = sb("dst_pair_idx", [P, NB], i32)
        put_idx = sb("put_idx", [P, NB], i32)
        slot1 = sb("slot1", [P, NB], i32)
        got_slot = sb("got_slot", [P, NB], i32)
        h0_idx = sb("h0_idx", [P, NB], i32)
        h_idx = sb("h_idx", [P, NB], i32)
        plain_row = sb("plain_row", [P, 2, NB])
        table_stage = sb("table_stage", [P, 2, TB], i32)
        row_stage = sb("row_stage", [P, 2, 2, J], i32)
        zero_i = sb("zero_i", [P, N // P], i32)
        zero_rows = sb("zero_rows", [P, J * D])

        same = sb("same", [128, E], u8)
        types = sb("types", [128, E], u8)
        arena = sb("arena", [128, 2 * E])
        F = arena[:, 0:E]
        H = arena[:, E:2 * E]
        work = sb("work", [128, WORK])

        def carver(*regions):
            left = [[ap, 0, size] for ap, size in regions]

            def carve(rows, *dims):
                n = 1
                for d in dims:
                    n *= d
                while left[0][1] + n > left[0][2]:
                    left.pop(0)
                ap = left[0][0][0:rows, left[0][1]:left[0][1] + n]
                left[0][1] += n
                if len(dims) == 3:
                    return ap.rearrange("p (a b c) -> p a b c", a=dims[0], b=dims[1])
                return ap.rearrange("p (a b) -> p a b", a=dims[0]) if len(dims) == 2 else ap
            return carve

        carve = carver((arena[:, :], 2 * E))
        Xd = carve(P, 2 * LANES, J * 2 * D).rearrange("p l (j two f) -> p l j two f", j=J, two=2)
        Fd = carve(128, 2 * LANES, T)
        Hd = carve(128, LANES, T)
        Rg = carve(128, 2, T)
        Zg = carve(128, 2, T)
        Ng = carve(128, 2, T)
        Keep = carve(128, 2, T)
        Take = carve(128, 2, T)
        Gt = carve(128, 2, T)
        Qo = carve(128, 2, T)
        HO = carve(P, 2, J * D)
        XO = carve(P, 2, J * D)
        stats = sb("stats", [P, LANES, J, 6])
        mean = sb("mean", [P, LANES, J])
        rstd = sb("rstd", [P, LANES, J])
        mom = sb("mom", [P, 4, 2 * J])
        halves = sb("halves", [P, 2 * J])
        inv_d = sb("inv_d", [P, 2 * J])
        eps = sb("eps", [P, 2 * J])
        minus_half = sb("minus_half", [P, 2 * J])

        carve = carver((H, E), (work[:, :], WORK))
        XS = carve(P, 2, J * D)
        XD = carve(P, 2, J * 2 * D)
        XK = carve(P, 2, J * D)
        ST = carve(128, T)
        DT = carve(128, T)
        LS = carve(128, T)
        LG = carve(128, 2, T)
        BK = carve(128, T)
        MX = carve(128, 2, T + 1)
        EA = carve(128, T)
        EB = carve(128, T)
        CF = carve(128, T)
        WT = carve(128, T)
        WV = carve(128, T)
        SD = carve(128, 2, T)
        SN = carve(128, 2, T)
        RD = carve(P, J * HEADS)
        AO = carve(P, J * D)
        X1 = carve(P, 2, J * D)
        N1 = carve(P, 2, J * D)
        win_i = carve(128, 2, T + 1)
        typ_i = carve(128, 2, T)
        win = win_i.bitcast(i32)
        typ = typ_i.bitcast(i32)
        a_stats = sb("a_stats", [P, J, 6])
        a_mean = sb("a_mean", [P, J])
        a_rstd = sb("a_rstd", [P, J])

        carve = carver((work[:, :], WORK))
        HG = carve(P, 2, J * D)
        RG = carve(128, T)
        MK = carve(128, K, T)
        AG = carve(128, 2, T)
        Rs = carve(128, T)
        Zs = carve(128, T)
        Ms = carve(128, T)
        Ns = carve(128, T)
        Ks = carve(128, T)
        Ts = carve(128, T)
        HN = carve(128, T)
        HR = carve(P, 2, J * D)
        XB = carve(P, 2, J * D)
        Gs = carve(128, T)
        Qs = carve(128, T)
        OB = carve(P, 2, J * D)
        hot = sb("hot", [12, 2, T], bf16)

        banks = [bank(f"bank{i}") for i in range(8)]

        weights_in = sem("weights_in")
        edges_in = sem("edges_in")
        setup = sem("setup")
        sp_passed = sem("sp_passed")
        pool_passed = sem("pool_passed")
        iota_done = sem("iota_done")
        zero_stored = sem("zero_stored")
        slots_zeroed = sem("slots_zeroed")

        block = ctx.enter_context(nc.Block())

        d_x_in = [sem(f"d_x_in{l}") for l in range(LANES)]
        d_stat = sem("d_stat")
        mom_done = sem("mom_done")
        d_rstd = sem("d_rstd")
        d_normed = sem("d_normed")
        d_x_turned = sem("d_x_turned")
        d_feat = sem("d_feat")
        d_mm = sem("d_mm")
        d_r = sem("d_r")
        d_z = sem("d_z")
        d_m = sem("d_m")
        d_n = sem("d_n")
        d_keep = sem("d_keep")
        d_take = sem("d_take")
        d_h = sem("d_h")
        d_gate = sem("d_gate")
        d_q = sem("d_q")
        d_pairs_stored = [[sem(f"d_pairs_stored{par}{l}") for l in range(LANES)] for par in range(2)]
        d_h_turned = sem("d_h_turned")
        d_h_copied = sem("d_h_copied")
        d_h_stored = [sem(f"d_h_stored{b}") for b in range(2)]
        d_o_turned = sem("d_o_turned")
        d_o = sem("d_o")
        d_o_stored = [sem(f"d_o_stored{b}") for b in range(2)]
        rows_turned = sem("rows_turned")
        idx_steps = sem("idx_steps")
        idx_ready = sem("idx_ready")
        m_staged = sem("m_staged")
        m_put = sem("m_put")
        m_got = sem("m_got")
        got_ready = sem("got_ready")
        wse_ready = sem("wse_ready")
        wse_mm = sem("wse_mm")
        a_open = sem("a_open")
        a_staged = sem("a_staged")
        a_rows_in = [sem(f"a_rows_in{b}") for b in range(2)]
        a_edges_in = [sem(f"a_edges_in{b}") for b in range(2)]
        a_src_turned = sem("a_src_turned")
        a_dst_turned = sem("a_dst_turned")
        a_kept = sem("a_kept")
        a_src_feat = sem("a_src_feat")
        a_dst_feat = sem("a_dst_feat")
        a_logit_mm = sem("a_logit_mm")
        a_value_mm = sem("a_value_mm")
        a_scaled = sem("a_scaled")
        a_dve = sem("a_dve")
        a_decay = sem("a_decay")
        a_weight = sem("a_weight")
        a_types = sem("a_types")
        a_out = sem("a_out")
        a_att_turned = sem("a_att_turned")
        a_x1 = sem("a_x1")
        a_x1_stored = [sem(f"a_x1_stored{b}") for b in range(2)]
        a_x1_stat = sem("a_x1_stat")
        a_x1_rstd = sem("a_x1_rstd")
        a_x1_normed = sem("a_x1_normed")
        a_x1_turned = sem("a_x1_turned")
        a_f1_stored = [sem(f"a_f1_stored{b}") for b in range(2)]
        a_feat = sem("a_feat")
        b_open = sem("b_open")
        b_idx = sem("b_idx")
        b_idx_steps = sem("b_idx_steps")
        b_staged = sem("b_staged")
        b_rows_in = [sem(f"b_rows_in{b}") for b in range(2)]
        b_turned = sem("b_turned")
        b_relu = sem("b_relu")
        b_masked = sem("b_masked")
        b_hot = sem("b_hot")
        b_msg = sem("b_msg")
        b_sum = sem("b_sum")
        b_own_mm = sem("b_own_mm")
        b_r_mm = sem("b_r_mm")
        b_z_mm = sem("b_z_mm")
        b_n_mm = sem("b_n_mm")
        b_r = sem("b_r")
        b_z = sem("b_z")
        b_m1 = sem("b_m1")
        b_m2 = sem("b_m2")
        b_n = sem("b_n")
        b_keep = sem("b_keep")
        b_take = sem("b_take")
        b_h = sem("b_h")
        b_h_kept = sem("b_h_kept")
        b_h_turned = sem("b_h_turned")
        b_h_copied = sem("b_h_copied")
        b_h_stored = [sem(f"b_h_stored{b}") for b in range(2)]
        b_x1_in = [sem(f"b_x1_in{b}") for b in range(2)]
        b_gate_mm = sem("b_gate_mm")
        b_j_mm = sem("b_j_mm")
        b_gate = sem("b_gate")
        b_q = sem("b_q")
        b_q_turned = sem("b_q_turned")
        b_o = sem("b_o")
        b_o_staged = sem("b_o_staged")
        b_o_put = [sem(f"b_o_put{b}") for b in range(2)]

        A_STEPS = ("leaky", "same", "back", "carry", "max", "lift", "decay_arg", "weight_arg", "weighted", "sum_w", "sum_v")

        def a_count(i, step):
            return i * len(A_STEPS) + (A_STEPS.index(step) + 1)

        def uses(i, b, n):
            return i * (n // 2) if b == 0 else (i - 1) * (n // 2)

        edge_tiles = lambda rows, at: rows[at:at + E, :].rearrange("(t j p) f -> t p j f", p=P, j=J)
        f_tiles = edge_tiles(h0_rows, 0)
        x1_tiles = edge_tiles(x1_rows, 0)
        hs_tiles = [None] + [edge_tiles(h_rows[t], 0) for t in (1, 2)]
        rows4 = lambda ap: ap.rearrange("p (j f) -> p j f", j=J)
        all_of = lambda i: slice(i * T, (i + 1) * T) if isinstance(i, int) else bass.ds(i * T, T)

        x_tiles = x.rearrange("(t p j) f -> t p (j f)", p=P, j=J)
        out_tiles = out.rearrange("(t p j) f -> t p (j f)", p=P, j=J)
        pair_tiles = h0_rows[E:E + 2 * N, :].rearrange("(t p j) f -> t p (j f)", p=P, j=2 * J)
        h_tiles = [None] + [h_rows[t][E:E + N, :].rearrange("(t p j) f -> t p (j f)", p=P, j=J) for t in (1, 2)]

        def unit(g, s, l):
            return g * GU + (s * LANES + l + 1)

        def lane(g, l):
            return g * LANES + (l + 1)

        def mm_count(g, s, l, part):
            within = 3 * (s * LANES + l) + part + 1 if s < STEPS else 3 * GU + 2 * l + part + 1
            return g * MMG + within

        assert ET == NG
        n_weights = 22

        @block.sync
        def _(sp):
            for dst_ap, src_ap in ((ident[:], ident_in), (headmask[:], headmask_in), (head_pick[:], head_pick_in), (part_type[:], part_type_in),
                                   (split_mask[:], split_in), (W0[:], w0), (W0T[:], w0T), (acol[:], a_cols),
                                   (Wih[:], wihT.rearrange("d (g o) -> d g o", g=3)),
                                   (Whh[:], whhT.rearrange("d (g o) -> d g o", g=3)),
                                   (Wi[:], iwT.rearrange("(c d) o -> d c o", c=2)), (Wj[:], jwT),
                                   (Wet[:], wetT.rearrange("k d o -> d k o")),
                                   (bias_i[:], bih), (bias_h[:], bhh), (ibias[:], ib), (jbias[:], jb),
                                   (bet12[0:4, :], b_et), (bet12[4:8, :], b_et), (bet12[8:12, :], b_et),
                                   (src_row[:], src.rearrange("(b p) -> b p", p=P)),
                                   (dst_row[:], dst.rearrange("(b p) -> b p", p=P))):
                sp.dma_start(dst_ap, src_ap).then_inc(weights_in, 16)
            sp.wait_ge(setup, 1)
            sp.dma_start(nxt_row[0:NB - 1, :], dst[1:E - P + 1].rearrange("(b p) -> b p", p=P)).then_inc(edges_in, 16)
            sp.dma_start(nxt_row[NB - 1:NB, 0:P - 1], dst[E - P + 1:E].rearrange("(b p) -> b p", b=1)).then_inc(edges_in, 16)
            sp.wait_ge(iota_done, 7)
            sp.dma_start(first_slot.rearrange("(p c) o -> p (c o)", p=P), zero_i[:]).then_inc(zero_stored, 16)

            def load(g, par, l):
                sp.dma_start(Xd[:, par * LANES + l, :, 0, :], rows4(x_tiles[g * LANES + l, :, :])).then_inc(d_x_in[l], 16)

            def store_pairs(g, par, l):
                alone(sp, d_normed, lane(g, l), sp_passed)
                sp.dma_start(pair_tiles[g * LANES + l, :, :],
                             Xd[:, par * LANES + l, :, :, :].rearrange("p j two f -> p (j two f)")
                             ).then_inc(d_pairs_stored[par][l], 16)

            for l in range(LANES):
                load(0, 0, l)
            for l in range(LANES):
                store_pairs(0, 0, l)

            def group(g, par, last):
                if not (isinstance(g, int) and g == 0):
                    store_out(g - 1, LANES - 1)
                for l in range(LANES):
                    if not last:
                        alone(sp, d_o, g * LANES + (l + 1 - LANES), sp_passed)
                        alone(sp, d_stat, lane(g, l), sp_passed)
                        alone(sp, d_pairs_stored[1 - par][l], g * 8 + (0 if par == 0 else 8), sp_passed)
                        load(g + 1, 1 - par, l)
                for s in (1, 2):
                    for l in range(LANES):
                        alone(sp, d_h_copied, g * 8 + ((s - 1) * LANES + l + 1), sp_passed)
                        sp.dma_start(h_tiles[s][g * LANES + l, :, :], HO[:, l % 2, :]).then_inc(d_h_stored[l % 2], 16)
                        if s == 2 and not last:
                            store_pairs(g + 1, 1 - par, l)
                for l in range(LANES - 1):
                    store_out(g, l)
                sp.dma_start(f_tiles[g, :, :, :], rows4(zero_rows[:])).then_inc(slots_zeroed, 16)

            def store_out(g, l):
                alone(sp, d_o, lane(g, l), sp_passed)
                sp.dma_start(out_tiles[g * LANES + l, :, :], XO[:, l % 2, :]).then_inc(d_o_stored[l % 2], 16)

            run(sp, group, NG)
            store_out(NG - 1, LANES - 1)

            bcast = lambda ap: ap.partition_broadcast(128)

            def edge_load(i, b):
                alone(sp, a_dve, a_count(i - 2, "same"), sp_passed)
                alone(sp, a_types, i - 1, sp_passed)
                if isinstance(i, int) and i == 0:
                    sp.dma_start(win[:, b, 1:T + 1], bcast(dst[0:T])).then_inc(a_edges_in[b], 16)
                else:
                    at = slice(i * T - 1, (i + 1) * T) if isinstance(i, int) else bass.ds(i * T - 1, T + 1)
                    sp.dma_start(win[:, b, :], bcast(dst[at])).then_inc(a_edges_in[b], 16)
                sp.dma_start(typ[:, b, :], bcast(etype[all_of(i)])).then_inc(a_edges_in[b], 16)

            def attend(i, b, last):
                if not last:
                    edge_load(i + 1, 1 - b)
                if not (isinstance(i, int) and i == 0):
                    store_normed(i - 1, 1 - b)
                alone(sp, a_x1, i + 1, sp_passed)
                sp.dma_start(x1_tiles[i, :, :, :], rows4(X1[:, b, :])).then_inc(a_x1_stored[b], 16)

            def store_normed(i, b):
                alone(sp, a_x1_normed, i + 1, sp_passed)
                sp.dma_start(f_tiles[i, :, :, :], rows4(N1[:, b, :])).then_inc(a_f1_stored[b], 16)

            sp.wait_ge(a_open, 2)
            edge_load(0, 0)
            run(sp, attend, ET, 3)
            store_normed(ET - 1, (ET - 1) % 2)

            for t in range(STEPS):
                c = t * ET

                def step(i, b, last):
                    if t < STEPS - 1:
                        alone(sp, b_h_copied, i + (c + 1), sp_passed)
                        sp.dma_start(hs_tiles[t + 1][i, :, :, :], rows4(HR[:, b, :])).then_inc(b_h_stored[b], 16)
                    else:
                        alone(sp, b_o, i - 1, sp_passed)
                        sp.dma_start(rows4(XB[:, b, :]), x1_tiles[i, :, :, :]).then_inc(b_x1_in[b], 16)
                if t == STEPS - 1:
                    sp.wait_ge(b_open, 1)
                run(sp, step, ET, 3)
            sp.wait_ge(edges_in, 32)

        @block.gpsimd
        def _(pool):
            nc.gpsimd.iota(slot_iota[:], pattern=[[P, NB]], base=0, channel_multiplier=1).then_inc(iota_done, 1)
            p = nc.gpsimd
            p.memset(zero_i[:], 0).then_inc(iota_done, 1)
            p.memset(halves[:], 0.5).then_inc(iota_done, 1)
            p.memset(inv_d[:], 1.0 / D).then_inc(iota_done, 1)
            p.memset(eps[:], EPS).then_inc(iota_done, 1)
            p.memset(minus_half[:], -0.5).then_inc(iota_done, 1)
            p.memset(zero_rows[:], 0.0).then_inc(iota_done, 1)
            pool.wait_ge(iota_done, 7)

            def moments(st, mean_out, rstd_out, n, before):
                c = [mom[:, i, 0:n] for i in range(4)]
                p.tensor_tensor(c[0], st[:, :, 1], st[:, :, 4], ALU.add)
                p.tensor_tensor(c[1], st[:, :, 1], st[:, :, 4], ALU.subtract)
                p.tensor_tensor(c[2], st[:, :, 2], st[:, :, 5], ALU.add).then_inc(mom_done, 1)
                pool.wait_ge(mom_done, before + 1)
                p.tensor_tensor(mean_out, c[0], halves[:, 0:n], ALU.mult)
                p.tensor_tensor(c[1], c[1], halves[:, 0:n], ALU.mult)
                p.tensor_tensor(c[2], c[2], inv_d[:, 0:n], ALU.mult).then_inc(mom_done, 1)
                pool.wait_ge(mom_done, before + 2)
                p.tensor_tensor(c[1], c[1], c[1], ALU.mult)
                p.tensor_tensor(c[2], c[2], eps[:, 0:n], ALU.add).then_inc(mom_done, 1)
                pool.wait_ge(mom_done, before + 3)
                p.tensor_tensor(c[3], c[1], c[2], ALU.add).then_inc(mom_done, 1)
                pool.wait_ge(mom_done, before + 4)
                return p.tensor_tensor(rstd_out, c[3], minus_half[:, 0:n], ALU.pow)

            def dense_rstd(g, l):
                pool.wait_ge(d_stat, lane(g, l))
                pool.wait_ge(d_normed, g * LANES + (l + 1 - LANES)) if not (isinstance(g, int) and g == 0) else None
                moments(stats[:, l, :, :], mean[:, l, :], rstd[:, l, :], J, lane(g, l) * 4 - 4).then_inc(d_rstd, 1)

            for l in range(LANES):
                dense_rstd(0, l)
            pool.wait_ge(idx_ready, 1)
            pool.wait_ge(zero_stored, 16)
            goes = NB // TB
            of_go = lambda k: slice(k * TB, (k + 1) * TB) if isinstance(k, int) else bass.ds(k * TB, TB)

            def put(k):
                p.tensor_copy(table_stage[:, 0, :], put_idx[:, of_go(k)]).then_inc(m_staged, 1)
                p.tensor_copy(table_stage[:, 1, :], slot1[:, of_go(k)]).then_inc(m_staged, 1)
                alone(pool, m_staged, k * 2 + 2, pool_passed)
                for c in range(TB):
                    p.indirect_dma_start(first_slot, bass.IndirectOffsetOnAxis(ap=table_stage[:, 0, c:c + 1], axis=0),
                                         table_stage[:, 1, c:c + 1], None, bounds_check=N - 1,
                                         oob_is_err=False).then_inc(m_put, 16)
                pool.wait_ge(m_put, k * (16 * TB) + 16 * TB)

            def get(k):
                p.tensor_copy(table_stage[:, 0, :], src_idx[:, of_go(k)]).then_inc(m_staged, 1)
                alone(pool, m_staged, k + (2 * goes + 1), pool_passed)
                for c in range(TB):
                    p.indirect_dma_start(table_stage[:, 1, c:c + 1], None, first_slot,
                                         bass.IndirectOffsetOnAxis(ap=table_stage[:, 0, c:c + 1], axis=0),
                                         ).then_inc(m_got, 16)
                pool.wait_ge(m_got, k * (16 * TB) + 16 * TB)
                p.tensor_copy(got_slot[:, of_go(k)], table_stage[:, 1, :]).then_inc(got_ready, 1)
                pool.wait_ge(got_ready, k + 1)

            def dense_group(g):
                for l in range(LANES):
                    dense_rstd(g + 1, l)

            with pool.Fori(0, goes) as g:
                dense_group(g)
                put(g)
            with pool.Fori(0, goes) as g:
                dense_group(g + goes)
                get(g)
            with pool.Fori(2 * goes, NG - 1) as g:
                dense_group(g)

            pool.wait_ge(d_o, LANES * NG)
            pool.wait_ge(d_h_copied, 2 * LANES * NG)
            pool.wait_ge(slots_zeroed, 16 * ET)
            for b in range(2):
                pool.wait_ge(d_h_stored[b], 16 * LANES * NG)
                pool.wait_ge(d_o_stored[b], 8 * LANES * NG)
                for l in range(LANES):
                    pool.wait_ge(d_pairs_stored[b][l], 16 * ((NG + 1 - b) // 2))
            p.memset(win[:, 0, 0:1], -1).then_inc(a_open, 1)
            p.memset(MX[:, 0, 0:1], 0.0).then_inc(a_open, 1)
            pool.wait_ge(a_open, 2)

            def fetch(i, b):
                if not (isinstance(i, int) and i < 2):
                    pool.wait_ge(a_dst_turned, i - 1)
                    pool.wait_ge(a_kept, i - 1)
                ks = slice(i * J, (i + 1) * J) if isinstance(i, int) else bass.ds(i * J, J)
                p.tensor_copy(row_stage[:, b, 0, :], src_row_idx[:, ks]).then_inc(a_staged, 1)
                p.tensor_copy(row_stage[:, b, 1, :], dst_pair_idx[:, ks]).then_inc(a_staged, 1)
                alone(pool, a_staged, i * 2 + 2, pool_passed)
                for w, rows, wide, table in ((0, XS, D, h0_rows), (1, XD, 2 * D, node_pairs)):
                    for j in range(J):
                        p.indirect_dma_start(rows[:, b, j * wide:(j + 1) * wide], None, table,
                                             bass.IndirectOffsetOnAxis(ap=row_stage[:, b, w, j:j + 1], axis=0),
                                             ).then_inc(a_rows_in[b], 16)

            dense_moments = 4 * LANES * NG

            def x1_rstd(i):
                pool.wait_ge(a_x1_stat, i + 1)
                need(pool, a_x1_normed, i)
                moments(a_stats[:, :, :], a_mean[:], a_rstd[:], J, i * 4 + dense_moments).then_inc(a_x1_rstd, 1)

            def attend(i, b, last):
                if not (isinstance(i, int) and i + 2 >= ET):
                    fetch(i + 2, b)
                x1_rstd(i)

            fetch(0, 0)
            fetch(1, 1)
            run(pool, attend, ET, 3)

            pool.wait_ge(a_feat, ET)
            pool.wait_ge(a_types, ET)
            for b, n in ((0, (ET + 1) // 2), (1, ET // 2)):
                pool.wait_ge(a_x1_stored[b], 16 * n)
                pool.wait_ge(a_f1_stored[b], 16 * n)
            pool.wait_ge(b_idx, 1)
            pool.sem_inc(b_open, 1)
            for t in range(STEPS):
                c = t * ET

                def fetch(i, b):
                    if not (isinstance(i, int) and i < 2):
                        pool.wait_ge(b_turned, i + (c - 1))
                    ks = slice(i * J, (i + 1) * J) if isinstance(i, int) else bass.ds(i * J, J)
                    p.tensor_copy(row_stage[:, b, 0, :], (h_idx if t else h0_idx)[:, ks]).then_inc(b_staged, 1)
                    alone(pool, b_staged, i + (c + 1), pool_passed)
                    for j in range(J):
                        p.indirect_dma_start(HG[:, b, j * D:(j + 1) * D], None, h_rows[t],
                                             bass.IndirectOffsetOnAxis(ap=row_stage[:, b, 0, j:j + 1], axis=0),
                                             ).then_inc(b_rows_in[b], 16)

                def put_rows(i, b):
                    ks = slice(i * J, (i + 1) * J) if isinstance(i, int) else bass.ds(i * J, J)
                    need(pool, b_o_put[b], i * 32 if b == 0 else (i - 1) * 32)
                    p.tensor_copy(row_stage[:, b, 1, :], put_idx[:, ks]).then_inc(b_o_staged, 1)
                    alone(pool, b_o_staged, i + 1, pool_passed)
                    alone(pool, b_o, i + 1, pool_passed)
                    for j in range(J):
                        p.indirect_dma_start(out, bass.IndirectOffsetOnAxis(ap=row_stage[:, b, 1, j:j + 1], axis=0),
                                             OB[:, b, j * D:(j + 1) * D], None, bounds_check=N - 1,
                                             oob_is_err=False).then_inc(b_o_put[b], 16)

                def step(i, b, last):
                    if not (isinstance(i, int) and i + 2 >= ET):
                        fetch(i + 2, b)
                    if t == STEPS - 1 and not (isinstance(i, int) and i == 0):
                        put_rows(i - 1, 1 - b)

                if t:
                    pool.wait_ge(b_turned, c)
                    for b, n in ((0, (ET + 1) // 2), (1, ET // 2)):
                        pool.wait_ge(b_h_stored[b], 16 * n * t)
                fetch(0, 0)
                fetch(1, 1)
                run(pool, step, ET, 3)
            put_rows(ET - 1, (ET - 1) % 2)
            for b, n in ((0, (ET + 1) // 2), (1, ET // 2)):
                pool.wait_ge(b_o_put[b], 16 * J * n)

        @block.vector
        def _(dve):
            v = nc.vector
            chained = [0]

            def chain(ins):
                chained[0] += 1
                ins.then_inc(setup, 1)
                dve.wait_ge(setup, chained[0])

            chain(v.memset(nxt_row[:], -1))
            dve.wait_ge(weights_in, 16 * n_weights)
            chain(v.tensor_tensor(bias_g[:, :], bias_i[:, :], bias_h[:, :], ALU.add))
            for i in range(2):
                chain(v.tensor_scalar(amat[:, i, :], headmask[:], acol[:, i:i + 1], None, ALU.mult))
            chain(v.tensor_copy(bet_part[:, 0, :], bet12[:]))
            chain(v.tensor_tensor(bet_rest[:, 0, :], bet12[:], bet_part[:, 0, :], ALU.subtract))
            chain(v.tensor_copy(bet_part[:, 1, :], bet_rest[:, 0, :]))
            chain(v.tensor_tensor(bet_rest[:, 1, :], bet_rest[:, 0, :], bet_part[:, 1, :], ALU.subtract))
            chain(v.tensor_copy(bet_part[:, 2, :], bet_rest[:, 1, :]))
            chain(v.tensor_scalar(bet_mix[:, 0, :], bet_part[:, 0, :], split_mask[:, 0:1], None, ALU.mult))
            for i in (1, 2):
                chain(v.scalar_tensor_tensor(out=bet_mix[:, i, :], in0=bet_part[:, i, :], scalar=split_mask[:, i:i + 1],
                                             in1=bet_mix[:, i - 1, :], op0=ALU.mult, op1=ALU.add))
            chain(v.tensor_copy(Bet[:], bet_mix[:, 2, :]))
            chain(v.tensor_copy(num_row[:, 0, :], src_row[:]))
            chain(v.tensor_copy(num_row[:, 1, :], dst_row[:]))
            dve.wait_ge(edges_in, 32)
            v.tensor_tensor(num_row[:, 2, :], dst_row[:], nxt_row[:], ALU.is_equal).then_inc(idx_steps, 1)
            dve.wait_ge(rows_turned, 1)
            v.tensor_copy(edge_cols[:, :, :], banks[7][0:P, 0:3 * NB].rearrange("p (a b) -> p a b", a=3)).then_inc(idx_steps, 1)
            dve.wait_ge(idx_steps, 2)
            v.tensor_copy(src_idx[:], edge_cols[:, 0, :])
            v.tensor_scalar(src_row_idx[:], edge_cols[:, 0, :], 2.0, float(E + 1), ALU.mult, ALU.add)
            v.tensor_scalar(dst_pair_idx[:], edge_cols[:, 1, :], float(E // 2), None, ALU.add)
            v.scalar_tensor_tensor(out=put_idx[:], in0=edge_cols[:, 2, :], scalar=float(SKIP), in1=edge_cols[:, 1, :],
                                   op0=ALU.mult, op1=ALU.add)
            dve.wait_ge(iota_done, 7)
            v.tensor_scalar(slot1[:], slot_iota[:], 1.0, None, ALU.add)
            v.tensor_scalar(plain_row[:, 0, :], edge_cols[:, 0, :], 2.0, float(E + 2), ALU.mult, ALU.add)
            v.tensor_scalar(plain_row[:, 1, :], edge_cols[:, 0, :], float(E + 1), None, ALU.add).then_inc(idx_ready, 1)
            dve.wait_ge(wse_mm, 1)
            v.tensor_copy(Wse[:, :, :], banks[6][:, 0:2 * D].rearrange("p (a b) -> p a b", a=2)).then_inc(wse_ready, 1)

            def group(g, par, last):
                for s in range(STEPS):
                    for l in range(LANES):
                        dense_unit(g, par, s, l)
                        if s == 0 and l == 0 and not (isinstance(g, int) and g == 0):
                            residual(g - 1, 1 - par, LANES - 1)
                        if s == 1 and not last:
                            dense_stats(g + 1, 1 - par, l)
                        if s == 2 and not last:
                            dense_norm(g + 1, 1 - par, l)
                finish_unit(g, par, STEPS - 1, LANES - 1)
                for l in range(LANES):
                    b = l % 2
                    dve.wait_ge(d_gate, lane(g, l))
                    dve.wait_ge(d_mm, mm_count(g, STEPS, l, 1))
                    need(dve, d_o_turned, g * LANES + (l - 1))
                    v.scalar_tensor_tensor(out=Qo[:, b, :], in0=banks[3 * b + 1][:, 0:T], scalar=jbias[:, 0:1],
                                           in1=Gt[:, b, :], op0=ALU.add, op1=ALU.mult).then_inc(d_q, 1)
                    if l >= 1:
                        residual(g, par, l - 1)

            def residual(g, par, l):
                b = l % 2
                dve.wait_ge(d_o_turned, lane(g, l))
                need(dve, d_o_stored[b], g * 32 + 16 * (l // 2))
                v.tensor_tensor(rows4(XO[:, b, :]), Xd[:, par * LANES + l, :, 0, :],
                                rows4(banks[7][0:P, :]), ALU.add).then_inc(d_o, 1)

            def dense_unit(g, par, s, l):
                q = s * LANES + l
                b = l % 2
                H_in = Fd[:, par * LANES + l, :] if s == 0 else Hd[:, l, :]
                dve.wait_ge(d_mm, mm_count(g, s, l, 2))
                dve.wait_ge(d_r, unit(g, s, l))
                v.scalar_tensor_tensor(out=banks[3 * b + 2][:, 0:T], in0=banks[3 * b + 2][:, 0:T], scalar=bias_h[:, 2:3],
                                       in1=Rg[:, b, :], op0=ALU.add, op1=ALU.mult).then_inc(d_m, 1)
                need(dve, d_h, g * GU + (q - 1))
                dve.wait_ge(d_z, unit(g, s, l))
                v.tensor_tensor(Keep[:, b, :], Zg[:, b, :], H_in, ALU.mult).then_inc(d_keep, 1)
                if q >= 1:
                    finish_unit(g, par, (q - 1) // LANES, (q - 1) % LANES)

            def finish_unit(g, par, s, l):
                b = l % 2
                dve.wait_ge(d_n, unit(g, s, l))
                v.scalar_tensor_tensor(out=Take[:, b, :], in0=Zg[:, b, :], scalar=1.0, in1=Ng[:, b, :],
                                       op0=ALU.subtract, op1=ALU.mult).then_inc(d_take, 1)
                dve.wait_ge(d_take, unit(g, s, l))
                dve.wait_ge(d_keep, unit(g, s, l))
                v.tensor_tensor(Hd[:, l, :], Keep[:, b, :], Take[:, b, :], ALU.subtract).then_inc(d_h, 1)

            def dense_stats(g, par, l):
                X = Xd[:, par * LANES + l, :, 0, :]
                dve.wait_ge(d_x_in[l], g * 16 + 16)
                need(dve, d_rstd, g * LANES + (l + 1 - LANES))
                for j in range(J):
                    ins = v.bn_stats(stats[:, l, j, :], X[:, j, :])
                ins.then_inc(d_stat, 1)

            def dense_norm(g, par, l):
                X = Xd[:, par * LANES + l, :, :, :]
                dve.wait_ge(d_rstd, lane(g, l))
                for j in range(J):
                    ins = v.tensor_scalar(X[:, j, 1, :], X[:, j, 0, :], mean[:, l, j:j + 1], rstd[:, l, j:j + 1],
                                          ALU.subtract, ALU.mult)
                ins.then_inc(d_normed, 1)

            for l in range(LANES):
                dense_stats(0, 0, l)
            for l in range(LANES):
                dense_norm(0, 0, l)
            run(dve, group, NG)
            residual(NG - 1, (NG - 1) % 2, LANES - 1)

            at = lambda i, step: dve.wait_ge(a_dve, a_count(i, step))

            def x1_norm(i, b):
                dve.wait_ge(a_x1_rstd, i + 1)
                need(dve, a_x1_turned, i - 1)
                need(dve, a_f1_stored[b], uses(i, b, 16))
                for j in range(J):
                    js = slice(j * D, (j + 1) * D)
                    ins = v.tensor_scalar(N1[:, b, js], X1[:, b, js], a_mean[:, j:j + 1], a_rstd[:, j:j + 1],
                                          ALU.subtract, ALU.mult)
                ins.then_inc(a_x1_normed, 1)

            def logits(i, b):
                dve.wait_ge(a_scaled, i + 1)
                v.tensor_tensor(LG[:, b, :], banks[2][:, 0:T], LS[:], ALU.max).then_inc(a_dve, 1)
                dve.wait_ge(a_edges_in[b], uses(i, b, 32) + 32)
                v.tensor_tensor(same[:, all_of(i)], win[:, b, 1:T + 1], win[:, b, 0:T], ALU.is_equal).then_inc(a_dve, 1)
                at(i, "same")
                v.tensor_scalar(BK[:], same[:, all_of(i)], 1.0, FAR, ALU.subtract, ALU.mult).then_inc(a_dve, 1)

            def attend(i, b, last):
                first = isinstance(i, int) and i == 0
                if first:
                    v.tensor_copy(MX[:, 0, 0:1], MX[:, 0, 0:1]).then_inc(a_dve, 1)
                else:
                    v.tensor_copy(MX[:, b, 0:1], MX[:, 1 - b, T:T + 1]).then_inc(a_dve, 1)
                at(i, "carry")
                v.tensor_tensor_scan(MX[:, b, 1:T + 1], BK[:], LG[:, b, :], MX[:, b, 0:1], ALU.add, ALU.max).then_inc(a_dve, 1)
                at(i, "max")
                need(dve, a_decay, i)
                v.tensor_tensor(EA[:], MX[:, b, 0:T], BK[:], ALU.add).then_inc(a_dve, 1)
                at(i, "lift")
                v.tensor_tensor(EA[:], EA[:], MX[:, b, 1:T + 1], ALU.subtract).then_inc(a_dve, 1)
                need(dve, a_weight, i)
                v.tensor_tensor(EB[:], LG[:, b, :], MX[:, b, 1:T + 1], ALU.subtract).then_inc(a_dve, 1)
                if not first:
                    x1_norm(i - 1, 1 - b)
                dve.wait_ge(a_weight, i + 1)
                dve.wait_ge(a_value_mm, i + 1)
                v.tensor_tensor(WV[:], WT[:], banks[3 + b][:, 0:T], ALU.mult).then_inc(a_dve, 1)
                dve.wait_ge(a_decay, i + 1)
                need(dve, a_att_turned, i - 1)
                v.tensor_tensor_scan(SD[:, b, :], CF[:], WT[:], 0.0 if first else SD[:, 1 - b, T - 1:T], ALU.mult,
                                     ALU.add).then_inc(a_dve, 1)
                at(i, "weighted")
                v.tensor_tensor_scan(SN[:, b, :], CF[:], WV[:], 0.0 if first else SN[:, 1 - b, T - 1:T], ALU.mult,
                                     ALU.add).then_inc(a_dve, 1)
                if not last:
                    logits(i + 1, 1 - b)
                dve.wait_ge(a_att_turned, i + 1)
                need(dve, a_out, i * 2)
                v.reciprocal(RD[:], banks[7][0:P, 0:J * HEADS]).then_inc(a_out, 1)
                dve.wait_ge(a_out, i * 2 + 1)
                need(dve, a_x1, i)
                v.tensor_tensor(AO.rearrange("p (h f) -> p h f", h=J * HEADS),
                                banks[5][0:P, :].rearrange("p (h f) -> p h f", h=J * HEADS),
                                RD.rearrange("p (h o) -> p h o", o=1).to_broadcast([P, J * HEADS, D // HEADS]),
                                ALU.mult).then_inc(a_out, 1)
                dve.wait_ge(a_out, i * 2 + 2)
                dve.wait_ge(a_kept, i + 1)
                need(dve, a_x1_stored[b], uses(i, b, 16))
                v.tensor_tensor(X1[:, b, :], XK[:, b, :], AO[:], ALU.add).then_inc(a_x1, 1)
                dve.wait_ge(a_x1, i + 1)
                need(dve, a_x1_rstd, i)
                for j in range(J):
                    ins = v.bn_stats(a_stats[:, j, :], X1[:, b, j * D:(j + 1) * D])
                ins.then_inc(a_x1_stat, 1)

            logits(0, 0)
            run(dve, attend, ET, 3)
            x1_norm(ET - 1, (ET - 1) % 2)

            dve.wait_ge(got_ready, NB // TB)
            for w, idx in enumerate((h0_idx, h_idx)):
                v.scalar_tensor_tensor(out=edge_cols[:, w, :], in0=got_slot[:], scalar=0.0, in1=plain_row[:, w, :],
                                       op0=ALU.is_equal, op1=ALU.mult).then_inc(b_idx_steps, 1)
                dve.wait_ge(b_idx_steps, 2 * w + 1)
                v.scalar_tensor_tensor(out=idx[:], in0=got_slot[:], scalar=-1.0, in1=edge_cols[:, w, :],
                                       op0=ALU.add, op1=ALU.add).then_inc(b_idx_steps, 1)
            dve.wait_ge(b_idx_steps, 4)
            dve.sem_inc(b_idx, 1)

            for t in range(STEPS):
                c = t * ET
                state = H if t else F

                def mask(i, b):
                    if t:
                        dve.wait_ge(b_turned, i + (c + 1))
                    else:
                        dve.wait_ge(b_relu, i + 1)
                    need(dve, b_msg, i + c)
                    for k in range(K):
                        ins = v.scalar_tensor_tensor(out=MK[:, k, :], in0=types[:, all_of(i)], scalar=float(k),
                                                     in1=banks[0][:, 0:T] if t else RG[:], op0=ALU.is_equal, op1=ALU.mult)
                    ins.then_inc(b_masked, 1)
                    v.tensor_scalar(hot[:, b, :], types[0:12, all_of(i)], part_type[:, 0:1], None,
                                    ALU.is_equal).then_inc(b_hot, 1)

                def sum_messages(i, b):
                    first = isinstance(i, int) and i == 0
                    dve.wait_ge(b_msg, i + (c + 1))
                    need(dve, b_n_mm, max(i + c - 1, c) if isinstance(i, int) else i + (c - 1))
                    if not first:
                        dve.wait_ge(b_sum, i + c)
                    v.tensor_tensor_scan(AG[:, b, :], same[:, all_of(i)], banks[1][:, 0:T],
                                         0.0 if first else AG[:, 1 - b, T - 1:T], ALU.mult, ALU.add).then_inc(b_sum, 1)

                def readout(i, b):
                    dve.wait_ge(b_gate, i + 1)
                    dve.wait_ge(b_j_mm, i + 1)
                    need(dve, b_q_turned, i)
                    v.scalar_tensor_tensor(out=Qs[:], in0=banks[7][:, 0:T], scalar=jbias[:, 0:1], in1=Gs[:],
                                           op0=ALU.add, op1=ALU.mult).then_inc(b_q, 1)

                def residual(i, b):
                    dve.wait_ge(b_q_turned, i + 1)
                    dve.wait_ge(b_x1_in[b], uses(i, b, 16) + 16)
                    need(dve, b_o_put[b], uses(i, b, 16 * J))
                    v.tensor_tensor(OB[:, b, :], XB[:, b, :], banks[6][0:P, :], ALU.add).then_inc(b_o, 1)

                def step(i, b, last):
                    first = isinstance(i, int) and i == 0
                    if not last:
                        mask(i + 1, 1 - b)
                    if t == STEPS - 1 and not first:
                        readout(i - 1, 1 - b)
                    dve.wait_ge(b_own_mm, i + (c + 1))
                    dve.wait_ge(b_r, i + (c + 1))
                    need(dve, b_m2, i + c)
                    v.scalar_tensor_tensor(out=Ms[:], in0=banks[4][:, 0:T], scalar=bias_h[:, 2:3], in1=Rs[:],
                                           op0=ALU.add, op1=ALU.mult).then_inc(b_m1, 1)
                    dve.wait_ge(b_m1, i + (c + 1))
                    dve.wait_ge(b_n_mm, i + (c + 1))
                    v.tensor_tensor(banks[5][:, 0:T], Ms[:], banks[5][:, 0:T], ALU.add).then_inc(b_m2, 1)
                    dve.wait_ge(b_z, i + (c + 1))
                    need(dve, b_h, i + c)
                    if t:
                        dve.wait_ge(b_h_kept, i + (c - ET + 1))
                    v.tensor_tensor(Ks[:], Zs[:], state[:, all_of(i)], ALU.mult).then_inc(b_keep, 1)
                    if t == STEPS - 1 and not first:
                        residual(i - 1, 1 - b)
                    dve.wait_ge(b_n, i + (c + 1))
                    v.scalar_tensor_tensor(out=Ts[:], in0=Zs[:], scalar=1.0, in1=Ns[:], op0=ALU.subtract,
                                           op1=ALU.mult).then_inc(b_take, 1)
                    dve.wait_ge(b_take, i + (c + 1))
                    if t < STEPS - 1:
                        need(dve, b_h_kept, i + c)
                        need(dve, b_h_turned, i + c)
                    elif first:
                        dve.wait_ge(b_h_kept, c)
                        dve.wait_ge(b_h_turned, c)
                    else:
                        dve.wait_ge(b_j_mm, i)
                    v.tensor_tensor(HN[:], Ks[:], Ts[:], ALU.subtract).then_inc(b_h, 1)
                    if not last:
                        sum_messages(i + 1, 1 - b)

                mask(0, 0)
                sum_messages(0, 0)
                run(dve, step, ET, 3)
            readout(ET - 1, (ET - 1) % 2)
            residual(ET - 1, (ET - 1) % 2)

        @block.scalar
        def _(act):
            a = nc.scalar
            act.wait_ge(setup, 2)

            def feature_copy(g, par, l):
                act.wait_ge(d_x_turned, lane(g, l))
                a.activation(Fd[:, par * LANES + l, :], banks[6][:, 0:T], ACT.Relu).then_inc(d_feat, 1)

            def tanh_of(g, s, l):
                b = l % 2
                act.wait_ge(d_m, unit(g, s, l))
                a.activation(Ng[:, b, :], banks[3 * b + 2][:, 0:T], ACT.Tanh, bias=bias_i[:, 2:3]).then_inc(d_n, 1)

            def dense_unit(g, par, s, l):
                b = l % 2
                if s >= 1:
                    i = (s - 1) * LANES + l
                    act.wait_ge(d_h_turned, g * 8 + (i + 1))
                    need(act, d_h_stored[b], g * 64 + 16 * (i // 2))
                    a.activation(HO[:, b, :], banks[7][0:P, :], ACT.Copy).then_inc(d_h_copied, 1)
                q = s * LANES + l
                need(act, d_m, g * GU + (q - 1))
                act.wait_ge(d_mm, mm_count(g, s, l, 0))
                a.activation(Rg[:, b, :], banks[3 * b][:, 0:T], ACT.Sigmoid, bias=bias_g[:, 0:1]).then_inc(d_r, 1)
                act.wait_ge(d_mm, mm_count(g, s, l, 1))
                need(act, d_take, g * GU + (q - 1))
                a.activation(Zg[:, b, :], banks[3 * b + 1][:, 0:T], ACT.Sigmoid, bias=bias_g[:, 1:2]).then_inc(d_z, 1)
                if q >= 1:
                    tanh_of(g, (q - 1) // LANES, (q - 1) % LANES)

            def group(g, par, last):
                for s in range(STEPS):
                    for l in range(LANES):
                        dense_unit(g, par, s, l)
                        if s == STEPS - 1 and l >= 1 and not last:
                            feature_copy(g + 1, 1 - par, l - 1)
                tanh_of(g, STEPS - 1, LANES - 1)
                for l in range(LANES):
                    b = l % 2
                    act.wait_ge(d_mm, mm_count(g, STEPS, l, 0))
                    need(act, d_q, g * LANES + (l - 1))
                    a.activation(Gt[:, b, :], banks[3 * b][:, 0:T], ACT.Sigmoid, bias=ibias[:, 0:1]).then_inc(d_gate, 1)
                    if l == 0 and not last:
                        feature_copy(g + 1, 1 - par, LANES - 1)

            for l in range(LANES):
                feature_copy(0, 0, l)
            run(act, group, NG)

            def sources(i, b):
                act.wait_ge(a_rows_in[b], uses(i, b, 128) + 128)
                need(act, a_x1, i - 1)
                a.activation(rows4(XK[:, b, :]), XD[:, b, :].rearrange("p (j w) -> p j w", j=J)[:, :, 0:D],
                             ACT.Copy).then_inc(a_kept, 1)
                act.wait_ge(a_src_turned, i + 1)
                need(act, a_value_mm, i)
                a.activation(ST[:], banks[0][:, 0:T], ACT.Relu).then_inc(a_src_feat, 1)
                act.wait_ge(a_dst_turned, i + 1)
                need(act, a_logit_mm, i)
                a.activation(DT[:], banks[1][:, 0:T], ACT.Relu).then_inc(a_dst_feat, 1)
                act.wait_ge(a_logit_mm, i + 1)
                need(act, a_dve, a_count(i - 1, "leaky"))
                a.activation(LS[:], banks[2][:, 0:T], ACT.Copy, scale=SLOPE).then_inc(a_scaled, 1)

            def new_rows(i, b):
                act.wait_ge(a_x1_turned, i + 1)
                a.activation(F[:, all_of(i)], banks[6][:, 0:T], ACT.Relu).then_inc(a_feat, 1)

            def attend(i, b, last):
                act.wait_ge(a_dve, a_count(i, "decay_arg"))
                need(act, a_dve, a_count(i - 1, "sum_v"))
                a.activation(CF[:], EA[:], ACT.Exp).then_inc(a_decay, 1)
                act.wait_ge(a_dve, a_count(i, "weight_arg"))
                a.activation(WT[:], EB[:], ACT.Exp).then_inc(a_weight, 1)
                act.wait_ge(a_edges_in[b], uses(i, b, 32) + 32)
                a.activation(types[:, all_of(i)], typ[:, b, :], ACT.Copy).then_inc(a_types, 1)
                if not last:
                    sources(i + 1, 1 - b)
                if not (isinstance(i, int) and i == 0):
                    new_rows(i - 1, 1 - b)

            sources(0, 0)
            run(act, attend, ET, 3)
            new_rows(ET - 1, (ET - 1) % 2)

            for t in range(STEPS):
                c = t * ET

                def relu_of(i):
                    act.wait_ge(b_turned, i + 1)
                    need(act, b_masked, i)
                    a.activation(RG[:], banks[0][:, 0:T], ACT.Relu).then_inc(b_relu, 1)

                def step(i, b, last):
                    if t == 0 and not last:
                        relu_of(i + 1)
                    act.wait_ge(b_r_mm, i + (c + 1))
                    need(act, b_m1, i + c)
                    a.activation(Rs[:], banks[2][:, 0:T], ACT.Sigmoid, bias=bias_g[:, 0:1]).then_inc(b_r, 1)
                    act.wait_ge(b_z_mm, i + (c + 1))
                    need(act, b_take, i + c)
                    a.activation(Zs[:], banks[3][:, 0:T], ACT.Sigmoid, bias=bias_g[:, 1:2]).then_inc(b_z, 1)
                    act.wait_ge(b_m2, i + (c + 1))
                    a.activation(Ns[:], banks[5][:, 0:T], ACT.Tanh, bias=bias_i[:, 2:3]).then_inc(b_n, 1)
                    if t < STEPS - 1:
                        act.wait_ge(b_h, i + (c + 1))
                        a.activation(H[:, all_of(i)], HN[:], ACT.Copy).then_inc(b_h_kept, 1)
                        act.wait_ge(b_h_turned, i + (c + 1))
                        need(act, b_h_stored[b], uses(i, b, 16) + 16 * t * ((ET + 1 - b) // 2))
                        a.activation(HR[:, b, :], banks[6][0:P, :], ACT.Copy).then_inc(b_h_copied, 1)
                    else:
                        act.wait_ge(b_gate_mm, i + 1)
                        need(act, b_q, i)
                        a.activation(Gs[:], banks[2][:, 0:T], ACT.Sigmoid, bias=ibias[:, 0:1]).then_inc(b_gate, 1)

                if t == 0:
                    relu_of(0)
                run(act, step, ET, 3)

        @block.tensor
        def _(pe):
            m = nc.tensor
            pe.wait_ge(weights_in, 16 * n_weights)
            pe.wait_ge(idx_steps, 1)
            for i in range(3):
                ins = m.transpose(banks[7][0:P, i * NB:(i + 1) * NB], num_row[:, i, :], ident[0:NB, 0:NB])
            ins.then_inc(rows_turned, 1)
            pe.wait_ge(idx_steps, 2)
            for i in range(2):
                ins = m.matmul(banks[6][:, i * D:(i + 1) * D], W0T[:], amat[:, i, :], start=True, stop=True)
            ins.then_inc(wse_mm, 1)
            pe.wait_ge(wse_ready, 1)

            def turn_in(g, par, l):
                pe.wait_ge(d_normed, lane(g, l))
                need(pe, d_feat, g * LANES + l)
                for j in range(J):
                    ins = m.transpose(banks[6][:, j * P:(j + 1) * P], Xd[:, par * LANES + l, j, 1, :], ident[0:P, 0:P])
                ins.then_inc(d_x_turned, 1)

            def turn_out(src_ap):
                for j in range(J):
                    ins = m.transpose(banks[7][0:P, j * D:(j + 1) * D], src_ap[:, j * P:(j + 1) * P], ident[:])
                return ins

            def group(g, par, last):
                for s in range(STEPS):
                    for l in range(LANES):
                        q = s * LANES + l
                        b = l % 2
                        if s == 0:
                            pe.wait_ge(d_feat, lane(g, l))
                            H_in = Fd[:, par * LANES + l, :]
                        else:
                            pe.wait_ge(d_h, unit(g, s - 1, l))
                            H_in = Hd[:, l, :]
                            i = (s - 1) * LANES + l
                            if i == 0:
                                need(pe, d_o, g * LANES)
                            else:
                                pe.wait_ge(d_h_copied, g * 8 + i)
                            turn_out(H_in).then_inc(d_h_turned, 1)
                        if q >= 2:
                            pe.wait_ge(d_r, g * GU + (q - 1))
                        else:
                            need(pe, d_gate, g * LANES + (l - 1))
                        m.matmul(banks[3 * b][:, 0:T], Whh[:, 0, :], H_in, start=True, stop=True).then_inc(d_mm, 1)
                        if q >= 2:
                            pe.wait_ge(d_z, g * GU + (q - 1))
                        else:
                            need(pe, d_q, g * LANES + (l - 1))
                        m.matmul(banks[3 * b + 1][:, 0:T], Whh[:, 1, :], H_in, start=True, stop=True).then_inc(d_mm, 1)
                        need(pe, d_n, g * GU + (q - 1))
                        m.matmul(banks[3 * b + 2][:, 0:T], Whh[:, 2, :], H_in, start=True, stop=True).then_inc(d_mm, 1)
                        if q == 0 and not (isinstance(g, int) and g == 0):
                            readout_rows(g - 1, LANES - 1)
                        if s == STEPS - 1 and l >= 1 and not last:
                            turn_in(g + 1, 1 - par, l - 1)
                for l in range(LANES):
                    b = l % 2
                    pe.wait_ge(d_h, unit(g, STEPS - 1, l))
                    if l >= 2:
                        pe.wait_ge(d_gate, g * LANES + (l - 1))
                    else:
                        pe.wait_ge(d_r, g * GU + (GU - 1 + l))
                    m.matmul(banks[3 * b][:, 0:T], Wi[:, 0, :], Hd[:, l, :], start=True, stop=False)
                    m.matmul(banks[3 * b][:, 0:T], Wi[:, 1, :], Fd[:, par * LANES + l, :], start=False, stop=True).then_inc(d_mm, 1)
                    if l >= 2:
                        pe.wait_ge(d_q, g * LANES + (l - 1))
                    else:
                        pe.wait_ge(d_z, g * GU + (GU - 1 + l))
                    m.matmul(banks[3 * b + 1][:, 0:T], Wj[:], Hd[:, l, :], start=True, stop=True).then_inc(d_mm, 1)
                    if l == 0 and not last:
                        turn_in(g + 1, 1 - par, LANES - 1)
                    if l >= 1:
                        readout_rows(g, l - 1)

            def readout_rows(g, l):
                pe.wait_ge(d_q, lane(g, l))
                if l == 0:
                    pe.wait_ge(d_h_copied, g * 8 + 8)
                else:
                    pe.wait_ge(d_o, lane(g, l - 1))
                turn_out(Qo[:, l % 2, :]).then_inc(d_o_turned, 1)

            for l in range(LANES):
                turn_in(0, 0, l)
            run(pe, group, NG)
            readout_rows(NG - 1, LANES - 1)

            def turn(bank_ap, rows):
                for j in range(J):
                    ins = m.transpose(bank_ap[:, j * P:(j + 1) * P], rows[:, j * D:(j + 1) * D], ident[0:P, 0:P])
                return ins

            def turn_back(bank_ap, cols):
                for j in range(J):
                    ins = m.transpose(bank_ap[0:P, j * D:(j + 1) * D], cols[:, j * P:(j + 1) * P], ident[:])
                return ins

            def sources(i, b):
                pe.wait_ge(a_rows_in[b], uses(i, b, 128) + 128)
                need(pe, a_src_feat, i)
                turn(banks[0], XS[:, b, :]).then_inc(a_src_turned, 1)
                need(pe, a_dst_feat, i)
                for j in range(J):
                    ins = m.transpose(banks[1][:, j * P:(j + 1) * P], XD[:, b, (2 * j + 1) * D:(2 * j + 2) * D],
                                      ident[0:P, 0:P])
                ins.then_inc(a_dst_turned, 1)
                pe.wait_ge(a_src_feat, i + 1)
                pe.wait_ge(a_dst_feat, i + 1)
                need(pe, a_dve, a_count(i - 1, "leaky"))
                m.matmul(banks[2][:, 0:T], Wse[:, 0, :], ST[:], start=True, stop=False)
                m.matmul(banks[2][:, 0:T], Wse[:, 1, :], DT[:], start=False, stop=True).then_inc(a_logit_mm, 1)
                need(pe, a_dve, a_count(i - 2, "weighted"))
                m.matmul(banks[3 + b][:, 0:T], W0[:], ST[:], start=True, stop=True).then_inc(a_value_mm, 1)

            def new_rows(i, b):
                pe.wait_ge(a_x1_normed, i + 1)
                need(pe, a_feat, i)
                turn(banks[6], N1[:, b, :]).then_inc(a_x1_turned, 1)

            def attend(i, b, last):
                if not last:
                    sources(i + 1, 1 - b)
                if not (isinstance(i, int) and i == 0):
                    new_rows(i - 1, 1 - b)
                pe.wait_ge(a_dve, a_count(i, "sum_v"))
                need(pe, a_out, i * 2)
                turn_back(banks[5], SN[:, b, :])
                for j in range(J):
                    ins = m.matmul(banks[7][0:P, j * HEADS:(j + 1) * HEADS], SD[:, b, j * P:(j + 1) * P], head_pick[:],
                                   start=True, stop=True)
                ins.then_inc(a_att_turned, 1)

            sources(0, 0)
            run(pe, attend, ET, 3)
            new_rows(ET - 1, (ET - 1) % 2)

            for t in range(STEPS):
                c = t * ET
                state = H if t else F

                def fetched(i, b):
                    pe.wait_ge(b_rows_in[b], uses(i, b, 16 * J) + 16 * J * (1 + t * ((ET + 1 - b) // 2)))
                    need(pe, b_masked, i + c)
                    turn(banks[0], HG[:, b, :]).then_inc(b_turned, 1)

                def messages(i, b):
                    pe.wait_ge(b_masked, i + (c + 1))
                    need(pe, b_sum, i + c)
                    for k in range(K):
                        m.matmul(banks[1][:, 0:T], Wet[:, k, :], MK[:, k, :], start=(k == 0), stop=False)
                    pe.wait_ge(b_hot, i + (c + 1))
                    m.matmul(banks[1][:, 0:T], Bet[:], hot[:, b, :], start=False, stop=True).then_inc(b_msg, 1)

                def readout(i):
                    pe.wait_ge(b_h, i + (c + 1))
                    pe.wait_ge(b_r, i + (c + 1))
                    m.matmul(banks[2][:, 0:T], Wi[:, 0, :], HN[:], start=True, stop=False)
                    m.matmul(banks[2][:, 0:T], Wi[:, 1, :], F[:, all_of(i)], start=False, stop=True).then_inc(b_gate_mm, 1)
                    need(pe, b_q, i)
                    m.matmul(banks[7][:, 0:T], Wj[:], HN[:], start=True, stop=True).then_inc(b_j_mm, 1)

                def readout_rows(i):
                    pe.wait_ge(b_q, i + 1)
                    need(pe, b_o, i)
                    turn_back(banks[6], Qs).then_inc(b_q_turned, 1)

                def step(i, b, last):
                    first = isinstance(i, int) and i == 0
                    if not last:
                        fetched(i + 1, 1 - b)
                    own = state[:, all_of(i)]
                    need(pe, b_r, i + c)
                    if t:
                        pe.wait_ge(b_h_kept, i + (c - ET + 1))
                    if t == STEPS - 1:
                        need(pe, b_gate, i)
                    m.matmul(banks[2][:, 0:T], Whh[:, 0, :], own, start=True, stop=False)
                    need(pe, b_z, i + c)
                    m.matmul(banks[3][:, 0:T], Whh[:, 1, :], own, start=True, stop=False)
                    need(pe, b_m1, i + c)
                    m.matmul(banks[4][:, 0:T], Whh[:, 2, :], own, start=True, stop=True).then_inc(b_own_mm, 1)
                    pe.wait_ge(b_sum, i + (c + 1))
                    m.matmul(banks[2][:, 0:T], Wih[:, 0, :], AG[:, b, :], start=False, stop=True).then_inc(b_r_mm, 1)
                    m.matmul(banks[3][:, 0:T], Wih[:, 1, :], AG[:, b, :], start=False, stop=True).then_inc(b_z_mm, 1)
                    need(pe, b_n, i + c)
                    m.matmul(banks[5][:, 0:T], Wih[:, 2, :], AG[:, b, :], start=True, stop=True).then_inc(b_n_mm, 1)
                    if t == STEPS - 1 and not first:
                        readout_rows(i - 1)
                    if not last:
                        messages(i + 1, 1 - b)
                    if t < STEPS - 1:
                        pe.wait_ge(b_h, i + (c + 1))
                        need(pe, b_h_copied, i + c)
                        turn_back(banks[6], HN).then_inc(b_h_turned, 1)
                    else:
                        readout(i)

                fetched(0, 0)
                messages(0, 0)
                run(pe, step, ET, 3)
            readout_rows(ET - 1)


def kernel(**inputs):
    import numpy as np
    import concourse.bacc as bacc
    from concourse.bass_utils import run_bass_kernel_spmd

    a = {k: np.asarray(v) for k, v in inputs.items()}
    cols = lambda v, n: v.reshape(n, D).T
    att = a["L0_gnn_a"]
    arrays = {
        "x": a["x"], "src": a["src"], "dst": a["dst"], "etype": a["edge_type_4"],
        "w0": a["L0_gnn_W"], "w0T": a["L0_gnn_W"].T,
        "a_cols": np.stack([att[:, :32].reshape(D), att[:, 32:].reshape(D)], axis=1),
        "wetT": a["L1_gnn_W_et"].transpose(0, 2, 1), "b_et": a["L1_gnn_b_et"],
        "wihT": a["L1_gnn_W_ih"].T, "bih": cols(a["L1_gnn_b_ih"], 3),
        "whhT": a["L1_gnn_W_hh"].T, "bhh": cols(a["L1_gnn_b_hh"], 3),
        "iwT": a["L1_gnn_i_w"].T, "ib": cols(a["L1_gnn_i_b"], 1),
        "jwT": a["L1_gnn_j_w"].T, "jb": cols(a["L1_gnn_j_b"], 1),
        "ident_in": np.eye(128, dtype=np.float32),
        "headmask_in": np.kron(np.eye(HEADS, dtype=np.float32), np.ones((D // HEADS, D // HEADS), np.float32)),
        "head_pick_in": np.eye(D, dtype=np.float32)[:, ::D // HEADS],
        "part_type_in": (np.arange(12) % K).astype(np.float32)[:, None],
        "split_in": np.repeat(np.eye(3, dtype=np.float32), K, axis=0),
    }
    arrays = {"in_" + k: np.ascontiguousarray(v) for k, v in arrays.items()}
    nc = bacc.Bacc("TRN2", target_bir_lowering=False, num_devices=1)
    args = [nc.dram_tensor(k, v.shape, mybir.dt.from_np(v.dtype), kind="ExternalInput").ap() for k, v in arrays.items()]
    out = nc.dram_tensor("out_0", a["x"].shape, mybir.dt.float32, kind="ExternalOutput").ap()
    gnn_kernel(nc, *args, out)
    r = run_bass_kernel_spmd(nc, [arrays], core_ids=[0])
    return r.results[0]["out_0"]
```

```python
import concourse.bass as bass
from concourse import mybir
from contextlib import ExitStack

P = 125
J = 4
T = P * J
D = 128
K = 4
HEADS = 4
STEPS = 3
EPS = 1e-5
SLOPE = 0.2
FAR = 3.0e38
LANES = 4
CHUNKS = 25
MOVED = 32
TB = 10
WORK = 13600


def run(eng, body, n, head=1):
    pairs = (n - head - 2) // 2
    for i in range(head):
        body(i, i % 2, False)
    with eng.Fori(0, pairs) as pair:
        body(pair * 2 + head, 1, False)
        body(pair * 2 + (head + 1), 0, False)
    for i in range(head + 2 * pairs, n):
        body(i, i % 2, i == n - 1)


def move_rows(eng, dst, src, semaphore):
    for rows in (slice(0, P // 16 * 16), slice(P // 16 * 16, P)):
        eng.dma_start(dst[rows], src[rows]).then_inc(semaphore, 16)


def need(eng, semaphore, value):
    if not isinstance(value, int) or value > 0:
        eng.wait_ge(semaphore, value)


def alone(eng, semaphore, value, passed):
    if not isinstance(value, int) or value > 0:
        eng.wait_ge(semaphore, value)
        eng.sem_inc(passed, 1)


def gnn_kernel(nc, x, src, dst, etype, w0, w0T, a_cols, wetT, b_et, wihT, bih, whhT, bhh, iwT, ib, jwT, jb,
               ident_in, headmask_in, head_pick_in, part_type_in, split_in, within_in, out):
    f32, bf16, i32, u8 = mybir.dt.float32, mybir.dt.bfloat16, mybir.dt.int32, mybir.dt.uint8
    part = mybir.dt.float32r
    ALU, ACT = mybir.AluOpType, mybir.ActivationFunctionType

    N, E = x.shape[0], src.shape[0]
    NT, ET = N // T, E // T
    NG = NT // LANES
    NB = E // P
    SKIP = N + 10000
    GU, RU = STEPS * LANES, LANES
    MMG = 3 * GU + 2 * RU

    ctx = ExitStack()
    with ctx:
        def sb(name, shape, dt=f32):
            return ctx.enter_context(nc.sbuf_tensor(name, shape, dt))

        def bank(name, shape=(128, 512)):
            return ctx.enter_context(nc.psum_tensor(name, list(shape), f32))

        def sem(name):
            return ctx.enter_context(nc.semaphore(name))

        s_src, s_dst, s_type = (nc.dram_tensor(f"slot_{what}", (E, 1), i32, kind="Internal").ap()
                                for what in ("src", "dst", "type"))
        rank_row = nc.dram_tensor("rank_row", (E,), i32, kind="Internal").ap()
        first_slot = nc.dram_tensor("slot_of_node", (N, 1), i32, kind="Internal").ap()
        h0_rows = nc.dram_tensor("h0_rows", (E + 2 * N, D), f32, kind="Internal").ap()
        node_pairs = h0_rows.rearrange("(n two) f -> n (two f)", two=2)
        h_rows = [h0_rows] + [nc.dram_tensor(f"h{t}_rows", (E + N, D), f32, kind="Internal").ap() for t in (1, 2)]
        x1_rows = nc.dram_tensor("x1_rows", (E, D), f32, kind="Internal").ap()

        ident = sb("ident", [128, 128])
        head_pick = sb("head_pick", [128, HEADS])
        part_type = sb("part_type", [12, 1])
        split_mask = sb("split_mask", [12, 3])
        W0 = sb("W0", [128, D])
        acol = sb("acol", [128, 2])
        Wse = sb("Wse", [128, 2, D])
        Wet = sb("Wet", [128, K, D])
        Wi = sb("Wi", [128, 2, D])
        Wj = sb("Wj", [128, D])
        Wih_part = sb("Wih_part", [128, 2, 3, D], part)
        Whh_part = sb("Whh_part", [128, 2, 3, D], part)
        Wi_part = sb("Wi_part", [128, 2, D], part)
        bias_i = sb("bias_i", [128, 3])
        bias_h = sb("bias_h", [128, 3])
        bias_g = sb("bias_g", [128, 3])
        ibias = sb("ibias", [128, 1])
        jbias = sb("jbias", [128, 1])
        bet12 = sb("bet12", [12, D])
        bet_rest = sb("bet_rest", [12, 2, D])
        bet_part = sb("bet_part", [12, 3, D], bf16)
        bet_mix = sb("bet_mix", [12, 3, D])
        Bet = sb("Bet", [12, D], bf16)

        src_row = sb("src_row", [NB, P], i32)
        dst_row = sb("dst_row", [NB, P], i32)
        nxt_row = sb("nxt_row", [NB, P], i32)
        num_row = sb("num_row", [NB, 4, P])
        descents = sb("descents", [NB, P + 1])
        ones = sb("ones", [NB, 1])
        out_of_order = sb("out_of_order", [1, 1], i32)
        slot_iota = sb("slot_iota", [P, NB], i32)
        slot_no = sb("slot_no", [P, NB])
        edge_cols = sb("edge_cols", [P, 3, NB])
        src_idx = sb("src_idx", [P, NB], i32)
        src_row_idx = sb("src_row_idx", [P, NB], i32)
        dst_pair_idx = sb("dst_pair_idx", [P, NB], i32)
        put_idx = sb("put_idx", [P, NB], i32)
        slot1 = sb("slot1", [P, NB], i32)
        got_slot = sb("got_slot", [P, NB], i32)
        h0_idx = sb("h0_idx", [P, NB], i32)
        h_idx = sb("h_idx", [P, NB], i32)
        plain_row = sb("plain_row", [P, 2, NB])
        table_stage = sb("table_stage", [P, 2, TB], i32)
        row_stage = sb("row_stage", [P, 2, 2, J], i32)
        zero_i = sb("zero_i", [P, N // P], i32)
        zero_rows = sb("zero_rows", [P, J * D])

        edge_bytes = sb("edge_bytes", [128, 2 * E], u8)
        same = edge_bytes[:, 0:E]
        types = edge_bytes[:, E:2 * E]
        arena = sb("arena", [128, 2 * E])
        F = arena[:, 0:E]
        H = arena[:, E:2 * E]
        with nc.sbuf_tensor("parts", [128, 6 * LANES, T], part) as parts:
            Fh, Fl = parts[:, 0:2 * LANES, :], parts[:, 2 * LANES:4 * LANES, :]
            Hh, Hl = parts[:, 4 * LANES:5 * LANES, :], parts[:, 5 * LANES:6 * LANES, :]
        with nc.sbuf_tensor("work_front", [128, WORK - 4 * T], f32), \
                nc.sbuf_tensor("step_parts", [128, 4, T], part) as step_parts:
            own_high, own_low, sum_high, sum_low = (step_parts[:, i, :] for i in range(4))
        work = sb("work", [128, WORK])

        def carver(*regions):
            left = [[ap, 0, size] for ap, size in regions]

            def carve(rows, *dims):
                n = 1
                for d in dims:
                    n *= d
                while left[0][1] + n > left[0][2]:
                    left.pop(0)
                ap = left[0][0][0:rows, left[0][1]:left[0][1] + n]
                left[0][1] += n
                if len(dims) == 3:
                    return ap.rearrange("p (a b c) -> p a b c", a=dims[0], b=dims[1])
                return ap.rearrange("p (a b) -> p a b", a=dims[0]) if len(dims) == 2 else ap
            return carve

        carve = carver((arena[:, :], 2 * E))
        Xd = carve(P, 2 * LANES, J * 2 * D).rearrange("p l (j two f) -> p l j two f", j=J, two=2)
        Fd = carve(128, 2 * LANES, T)
        Hd = carve(128, LANES, T)
        Rg = carve(128, 2, T)
        Zg = carve(128, 2, T)
        Ng = carve(128, 2, T)
        Keep = carve(128, 2, T)
        headmask = Ng[:, 0, 0:D]
        W0T = Ng[:, 0, D:2 * D]
        amat = Keep[:, 0, 0:2 * D].rearrange("p (w f) -> p w f", w=2)
        Wih = Rg[:, 0, 0:3 * D].rearrange("p (w f) -> p w f", w=3)
        Whh = Zg[:, 0, 0:3 * D].rearrange("p (w f) -> p w f", w=3)
        Take = carve(128, 2, T)
        Gt = carve(128, 2, T)
        Qo = carve(128, 2, T)
        HO = carve(P, 2, J * D)
        XO = carve(P, 2, J * D)
        stats = sb("stats", [P, LANES, J, 6])
        mean = sb("mean", [P, LANES, J])
        rstd = sb("rstd", [P, LANES, J])
        mom = sb("mom", [P, 4, LANES * J])
        halves = sb("halves", [P, LANES * J])
        inv_d = sb("inv_d", [P, LANES * J])
        eps = sb("eps", [P, LANES * J])
        minus_half = sb("minus_half", [P, LANES * J])

        carve = carver((work[:, :], WORK))
        KEY = carve(P, E)
        within = carve(P, 2 * P)
        unsorted = carve(P, 3, NB).bitcast(i32)
        own_key = carve(P, NB)
        key_now = carve(P, 1)
        ranks = carve(P, NB).bitcast(i32)
        rank_stage = carve(P, 4).bitcast(i32)
        is_before = carve(P, E // 2 // CHUNKS).bitcast(bf16)
        before = edge_bytes[0:P, :].bitcast(bf16)

        carve = carver((H, E), (work[:, :], WORK))
        XS = carve(P, 2, J * D)
        XD = carve(P, 2, J * 2 * D)
        XK = carve(P, 2, J * D)
        ST = carve(128, T)
        DT = carve(128, T)
        LS = carve(128, T)
        LG = carve(128, 2, T)
        BK = carve(128, T)
        MX = carve(128, 2, T + 1)
        EA = carve(128, T)
        EB = carve(128, T)
        CF = carve(128, T)
        WT = carve(128, T)
        WV = carve(128, T)
        SD = carve(128, 2, T)
        SN = carve(128, 2, T)
        RD = carve(P, J * HEADS)
        AO = carve(P, J * D)
        X1 = carve(P, 2, J * D)
        N1 = carve(P, 2, J * D)
        win_i = carve(128, 2, T + 1)
        typ_i = carve(128, 2, T)
        win = win_i.bitcast(i32)
        typ = typ_i.bitcast(i32)
        a_stats = sb("a_stats", [P, J, 6])
        a_mv = sb("a_mv", [P, J, 2])
        a_ve = sb("a_ve", [P, J])
        a_rstd = sb("a_rstd", [P, J])

        carve = carver((work[:, :], WORK - 4 * T))
        HG = carve(P, 2, J * D)
        RG = carve(128, T)
        MK = carve(128, K, T)
        AG = carve(128, 2, T)
        Rs = carve(128, T)
        Zs = carve(128, T)
        Ms = carve(128, T)
        Ns = carve(128, T)
        Ks = carve(128, T)
        Ts = carve(128, T)
        HN = carve(128, T)
        HR = carve(P, 2, J * D)
        XB = HR
        Gs = carve(128, T)
        Qs = carve(128, T)
        OB = carve(P, 2, J * D)
        hot = carve(12, T).bitcast(bf16).rearrange("p (b t) -> p b t", b=2)

        banks = [bank(f"bank{i}") for i in range(8)]

        weights_in = sem("weights_in")
        order_in = sem("order_in")
        order_steps = sem("order_steps")
        order_mm = sem("order_mm")
        edges_copied = sem("edges_copied")
        edges_sorted = sem("edges_sorted")
        sort_in = sem("sort_in")
        sort_steps = sem("sort_steps")
        sort_put = sem("sort_put")
        edges_in = sem("edges_in")
        setup = sem("setup")
        sp_passed = sem("sp_passed")
        pool_passed = sem("pool_passed")
        act_passed = sem("act_passed")
        dve_passed = sem("dve_passed")
        iota_done = sem("iota_done")
        zero_stored = sem("zero_stored")
        slots_zeroed = sem("slots_zeroed")

        block = ctx.enter_context(nc.Block())

        d_x_in = [sem(f"d_x_in{l}") for l in range(LANES)]
        d_stat = sem("d_stat")
        mom_done = sem("mom_done")
        d_rstd = sem("d_rstd")
        d_normed = sem("d_normed")
        d_x_turned = sem("d_x_turned")
        d_feat = sem("d_feat")
        d_feat_high = sem("d_feat_high")
        d_feat_low = sem("d_feat_low")
        d_high = sem("d_high")
        d_low = [sem(f"d_low{s}") for s in range(2)]
        parts_ready = sem("parts_ready")
        d_mm = sem("d_mm")
        d_r = sem("d_r")
        d_z = sem("d_z")
        d_m = sem("d_m")
        d_n = sem("d_n")
        d_keep = sem("d_keep")
        d_take = sem("d_take")
        d_h = sem("d_h")
        d_gate = sem("d_gate")
        d_q = sem("d_q")
        d_pairs_stored = [[sem(f"d_pairs_stored{par}{l}") for l in range(LANES)] for par in range(2)]
        d_h_turned = sem("d_h_turned")
        d_h_copied = sem("d_h_copied")
        d_h_stored = [sem(f"d_h_stored{b}") for b in range(2)]
        d_o_turned = sem("d_o_turned")
        d_o = sem("d_o")
        d_o_stored = [sem(f"d_o_stored{b}") for b in range(2)]
        rows_turned = sem("rows_turned")
        idx_steps = sem("idx_steps")
        idx_ready = sem("idx_ready")
        m_staged = sem("m_staged")
        m_put = sem("m_put")
        m_got = sem("m_got")
        got_ready = sem("got_ready")
        wse_ready = sem("wse_ready")
        wse_mm = sem("wse_mm")
        a_open = sem("a_open")
        a_staged = [sem(f"a_staged{w}") for w in range(2)]
        a_rows_in = [sem(f"a_rows_in{b}") for b in range(2)]
        a_edges_in = [sem(f"a_edges_in{b}") for b in range(2)]
        a_src_turned = sem("a_src_turned")
        a_dst_turned = sem("a_dst_turned")
        a_kept = sem("a_kept")
        a_src_feat = sem("a_src_feat")
        a_dst_feat = sem("a_dst_feat")
        a_logit_mm = sem("a_logit_mm")
        a_value_mm = sem("a_value_mm")
        a_scaled = sem("a_scaled")
        a_dve = sem("a_dve")
        a_decay = sem("a_decay")
        a_weight = sem("a_weight")
        a_types = sem("a_types")
        a_out = sem("a_out")
        a_att_turned = sem("a_att_turned")
        a_x1 = sem("a_x1")
        a_x1_stored = [sem(f"a_x1_stored{b}") for b in range(2)]
        a_x1_bn = sem("a_x1_bn")
        a_x1_stat = sem("a_x1_stat")
        a_x1_rstd = sem("a_x1_rstd")
        a_x1_normed = sem("a_x1_normed")
        a_x1_turned = sem("a_x1_turned")
        a_f1_stored = [sem(f"a_f1_stored{b}") for b in range(2)]
        a_feat = sem("a_feat")
        b_open = sem("b_open")
        b_idx = sem("b_idx")
        b_idx_steps = sem("b_idx_steps")
        b_staged = sem("b_staged")
        b_rows_in = [sem(f"b_rows_in{b}") for b in range(2)]
        b_turned = sem("b_turned")
        b_relu = sem("b_relu")
        b_masked = sem("b_masked")
        b_hot = sem("b_hot")
        b_msg = sem("b_msg")
        b_sum = sem("b_sum")
        b_own_high = sem("b_own_high")
        b_own_low = sem("b_own_low")
        b_sum_high = sem("b_sum_high")
        b_sum_low = sem("b_sum_low")
        b_own_mm = sem("b_own_mm")
        b_r_mm = sem("b_r_mm")
        b_z_mm = sem("b_z_mm")
        b_n_mm = sem("b_n_mm")
        b_r = sem("b_r")
        b_z = sem("b_z")
        b_m1 = sem("b_m1")
        b_m2 = sem("b_m2")
        b_n = sem("b_n")
        b_keep = sem("b_keep")
        b_take = sem("b_take")
        b_h = sem("b_h")
        b_h_kept = sem("b_h_kept")
        b_h_turned = sem("b_h_turned")
        b_h_copied = sem("b_h_copied")
        b_h_stored = [sem(f"b_h_stored{b}") for b in range(2)]
        b_x1_in = [sem(f"b_x1_in{b}") for b in range(2)]
        b_gate_mm = sem("b_gate_mm")
        b_j_mm = sem("b_j_mm")
        b_gate = sem("b_gate")
        b_q = sem("b_q")
        b_q_turned = sem("b_q_turned")
        b_o = sem("b_o")
        b_o_staged = sem("b_o_staged")
        b_o_put = [sem(f"b_o_put{b}") for b in range(2)]

        A_STEPS = ("leaky", "same", "back", "carry", "max", "lift", "decay_arg", "weight_arg", "weighted", "sum_w", "sum_v")

        def a_count(i, step):
            return i * len(A_STEPS) + (A_STEPS.index(step) + 1)

        def uses(i, b, n):
            return i * (n // 2) if b == 0 else (i - 1) * (n // 2)

        edge_tiles = lambda rows, at: rows[at:at + E, :].rearrange("(t j p) f -> t p j f", p=P, j=J)
        f_tiles = edge_tiles(h0_rows, 0)
        x1_tiles = edge_tiles(x1_rows, 0)
        hs_tiles = [None] + [edge_tiles(h_rows[t], 0) for t in (1, 2)]
        rows4 = lambda ap: ap.rearrange("p (j f) -> p j f", j=J)
        all_of = lambda i: slice(i * T, (i + 1) * T) if isinstance(i, int) else bass.ds(i * T, T)

        x_tiles = x.rearrange("(t p j) f -> t p (j f)", p=P, j=J)
        out_tiles = out.rearrange("(t p j) f -> t p (j f)", p=P, j=J)
        pair_tiles = h0_rows[E:E + 2 * N, :].rearrange("(t p j) f -> t p (j f)", p=P, j=2 * J)
        h_tiles = [None] + [h_rows[t][E:E + N, :].rearrange("(t p j) f -> t p (j f)", p=P, j=J) for t in (1, 2)]

        def unit(g, s, l):
            return g * GU + (s * LANES + l + 1)

        def lane(g, l):
            return g * LANES + (l + 1)

        def mm_count(g, s, l, part):
            within = 3 * (s * LANES + l) + part + 1 if s < STEPS else 3 * GU + 2 * l + part + 1
            return g * MMG + within

        assert ET == NG
        NORM_AT = 8
        STATS_AT = 2
        TABLE_AT = {0: (0,), 1: (1,), 7: (2,), 8: (3,), 9: (4,), 10: (5,), GU - 1: (6, 7, 8, 9)}
        assert sum(len(c) for c in TABLE_AT.values()) == TB

        def state_low(eng, ops, g, q):
            s, l = q // LANES, q % LANES
            eng.wait_ge(d_high, g * (2 * LANES) + (q + 1))
            ops.tensor_tensor(Hl[:, l, :], Hd[:, l, :], Hh[:, l, :], ALU.subtract).then_inc(d_low[s], 1)

        def step_own_low(eng, ops, t, i):
            eng.wait_ge(b_own_high, i + (t * ET + 1))
            need(eng, b_own_mm, i + t * ET)
            ops.tensor_tensor(own_low, (H if t else F)[:, all_of(i)], own_high, ALU.subtract).then_inc(b_own_low, 1)

        n_weights = 20

        weight_loads = (
            (ident[:], ident_in), (headmask[:], headmask_in), (head_pick[:], head_pick_in),
            (part_type[:], part_type_in),
            (split_mask[:], split_in), (W0[:], w0), (W0T[:], w0T), (acol[:], a_cols),
            (Wih[:], wihT.rearrange("d (g o) -> d g o", g=3)),
            (Whh[:], whhT.rearrange("d (g o) -> d g o", g=3)),
            (Wi[:], iwT.rearrange("(c d) o -> d c o", c=2)), (Wj[:], jwT),
            (Wet[:], wetT.rearrange("k d o -> d k o")),
            (bias_i[:], bih), (bias_h[:], bhh), (ibias[:], ib), (jbias[:], jb),
            (bet12[0:4, :], b_et), (bet12[4:8, :], b_et), (bet12[8:12, :], b_et))
        assert n_weights == len(weight_loads)

        @block.sync
        def _(sp):
            blocks_of = lambda ap: ap.rearrange("(b p) -> b p", p=P)
            sp.wait_ge(setup, 1)
            for dst_ap, src_ap in ((dst_row[:], blocks_of(dst)), (nxt_row[0:NB - 1, :], blocks_of(dst[1:E - P + 1])),
                                   (nxt_row[NB - 1:NB, 0:P - 1], dst[E - P + 1:E].rearrange("(b p) -> b p", b=1))):
                sp.dma_start(dst_ap, src_ap).then_inc(order_in, 16)
            def load(g, par, l):
                move_rows(sp, Xd[:, par * LANES + l, :, 0, :], rows4(x_tiles[g * LANES + l, :, :]), d_x_in[l])

            for l in range(LANES):
                load(0, 0, l)
            for dst_ap, src_ap in weight_loads[0::2]:
                sp.dma_start(dst_ap, src_ap).then_inc(weights_in, 16)
            flat = lambda table: table.rearrange("e o -> (e o)")
            for table, edges in ((s_src, src), (s_dst, dst), (s_type, etype)):
                sp.dma_start(blocks_of(flat(table)), blocks_of(edges)).then_inc(edges_copied, 16)
            sp.wait_ge(iota_done, 7)
            sp.dma_start(first_slot.rearrange("(p c) o -> p (c o)", p=P), zero_i[:]).then_inc(zero_stored, 16)

            def store_pairs(g, par, l):
                alone(sp, d_normed, lane(g, l), sp_passed)
                move_rows(sp, pair_tiles[g * LANES + l, :, :],
                          Xd[:, par * LANES + l, :, :, :].rearrange("p j two f -> p (j two f)"),
                          d_pairs_stored[par][l])

            for l in range(LANES):
                store_pairs(0, 0, l)

            def load_slots():
                sp.wait_ge(edges_sorted, 1)
                d = flat(s_dst)
                for dst_ap, src_ap in ((src_row[:], blocks_of(flat(s_src))), (dst_row[:], blocks_of(d)),
                                       (nxt_row[0:NB - 1, :], blocks_of(d[1:E - P + 1])),
                                       (nxt_row[NB - 1:NB, 0:P - 1], d[E - P + 1:E].rearrange("(b p) -> b p", b=1))):
                    sp.dma_start(dst_ap, src_ap).then_inc(edges_in, 16)

            def group(g, par, last):
                if not (isinstance(g, int) and g == 0):
                    store_out(g - 1, LANES - 1)
                else:
                    load_slots()
                for l in range(LANES):
                    if not last:
                        alone(sp, d_o, g * LANES + (l + 1 - LANES), sp_passed)
                        alone(sp, d_stat, lane(g, l), sp_passed)
                        alone(sp, d_pairs_stored[1 - par][l], g * (MOVED // 2) + (0 if par == 0 else MOVED // 2), sp_passed)
                        load(g + 1, 1 - par, l)
                for s in (1, 2):
                    for l in range(LANES):
                        alone(sp, d_h_copied, g * 8 + ((s - 1) * LANES + l + 1), sp_passed)
                        move_rows(sp, h_tiles[s][g * LANES + l, :, :], HO[:, l % 2, :], d_h_stored[l % 2])
                        if s == 2 and not last:
                            store_pairs(g + 1, 1 - par, l)
                for l in range(LANES - 1):
                    store_out(g, l)
                move_rows(sp, f_tiles[g, :, :, :], rows4(zero_rows[:]), slots_zeroed)

            def store_out(g, l):
                alone(sp, d_o, lane(g, l), sp_passed)
                move_rows(sp, out_tiles[g * LANES + l, :, :], XO[:, l % 2, :], d_o_stored[l % 2])

            run(sp, group, NG)
            store_out(NG - 1, LANES - 1)

            bcast = lambda ap: ap.partition_broadcast(128)

            def edge_load(i, b):
                alone(sp, a_dve, a_count(i - 2, "same"), sp_passed)
                alone(sp, a_types, i - 1, sp_passed)
                if isinstance(i, int) and i == 0:
                    sp.dma_start(win[:, b, 1:T + 1], bcast(flat(s_dst)[0:T])).then_inc(a_edges_in[b], 16)
                else:
                    at = slice(i * T - 1, (i + 1) * T) if isinstance(i, int) else bass.ds(i * T - 1, T + 1)
                    sp.dma_start(win[:, b, :], bcast(flat(s_dst)[at])).then_inc(a_edges_in[b], 16)
                sp.dma_start(typ[:, b, :], bcast(flat(s_type)[all_of(i)])).then_inc(a_edges_in[b], 16)

            def attend(i, b, last):
                if not last:
                    edge_load(i + 1, 1 - b)
                if not (isinstance(i, int) and i == 0):
                    store_normed(i - 1, 1 - b)
                alone(sp, a_x1, i + 1, sp_passed)
                move_rows(sp, x1_tiles[i, :, :, :], rows4(X1[:, b, :]), a_x1_stored[b])

            def store_normed(i, b):
                alone(sp, a_x1_normed, i + 1, sp_passed)
                move_rows(sp, f_tiles[i, :, :, :], rows4(N1[:, b, :]), a_f1_stored[b])

            sp.wait_ge(a_open, 2)
            edge_load(0, 0)
            run(sp, attend, ET, 3)
            store_normed(ET - 1, (ET - 1) % 2)

            for t in range(STEPS):
                c = t * ET

                def step(i, b, last):
                    if t < STEPS - 1:
                        alone(sp, b_h_copied, i + (c + 1), sp_passed)
                        move_rows(sp, hs_tiles[t + 1][i, :, :, :], rows4(HR[:, b, :]), b_h_stored[b])
                    else:
                        alone(sp, b_o, i - 1, sp_passed)
                        move_rows(sp, rows4(XB[:, b, :]), x1_tiles[i, :, :, :], b_x1_in[b])
                if t == STEPS - 1:
                    sp.wait_ge(b_open, 1)
                    for b, n in ((0, (ET + 1) // 2), (1, ET // 2)):
                        sp.wait_ge(b_h_stored[b], MOVED * n * t)
                run(sp, step, ET, 3)

        @block.gpsimd
        def _(pool):
            nc.gpsimd.iota(slot_iota[:], pattern=[[P, NB]], base=0, channel_multiplier=1).then_inc(iota_done, 1)
            p = nc.gpsimd
            p.memset(zero_i[:], 0).then_inc(iota_done, 1)
            p.memset(halves[:], 0.5).then_inc(iota_done, 1)
            p.memset(inv_d[:], 1.0 / D).then_inc(iota_done, 1)
            p.memset(eps[:], EPS).then_inc(iota_done, 1)
            p.memset(minus_half[:], -0.5).then_inc(iota_done, 1)
            p.memset(zero_rows[:], 0.0).then_inc(iota_done, 1)
            pool.wait_ge(iota_done, 7)

            def moments(st, mean_out, rstd_out, n, before):
                c = [mom[:, i, 0:n] for i in range(4)]
                p.tensor_tensor(c[0], st[:, :, 1], st[:, :, 4], ALU.add)
                p.tensor_tensor(c[1], st[:, :, 1], st[:, :, 4], ALU.subtract)
                p.tensor_tensor(c[2], st[:, :, 2], st[:, :, 5], ALU.add).then_inc(mom_done, 1)
                pool.wait_ge(mom_done, before + 1)
                p.tensor_tensor(mean_out, c[0], halves[:, 0:n], ALU.mult)
                p.tensor_tensor(c[1], c[1], halves[:, 0:n], ALU.mult)
                p.tensor_tensor(c[2], c[2], inv_d[:, 0:n], ALU.mult).then_inc(mom_done, 1)
                pool.wait_ge(mom_done, before + 2)
                p.tensor_tensor(c[1], c[1], c[1], ALU.mult)
                p.tensor_tensor(c[2], c[2], eps[:, 0:n], ALU.add).then_inc(mom_done, 1)
                pool.wait_ge(mom_done, before + 3)
                p.tensor_tensor(c[3], c[1], c[2], ALU.add).then_inc(mom_done, 1)
                pool.wait_ge(mom_done, before + 4)
                return p.tensor_tensor(rstd_out, c[3], minus_half[:, 0:n], ALU.pow)

            def dense_rstd(g):
                pool.wait_ge(d_stat, (g + 1) * LANES)
                need(pool, d_normed, g * LANES)
                flat_lanes = lambda ap: ap.rearrange("p l j -> p (l j)")
                moments(stats[:, :, :, :].rearrange("p l j s -> p (l j) s"), flat_lanes(mean[:, :, :]),
                        flat_lanes(rstd[:, :, :]), LANES * J, g * 4).then_inc(d_rstd, 1)


            def sort_edges():
                loads = [0]

                def move(dst_ap, src_ap):
                    loads[0] += 16
                    with nc.allow_non_contiguous_dma(reason="edges in columns"):
                        pool.dma_start(dst_ap, src_ap).then_inc(sort_in, 16)
                    pool.wait_ge(sort_in, loads[0])

                def move_columns(dst_ap, edges):
                    for at in range(0, NB, NB // 4):
                        move(dst_ap[:, at:at + NB // 4],
                             edges[at * P:(at + NB // 4) * P].rearrange("(b p) -> p b", p=P))

                for at in range(0, E, E // CHUNKS):
                    move(KEY.bitcast(i32)[:, at:at + E // CHUNKS], dst[at:at + E // CHUNKS].partition_broadcast(P))
                move(within, within_in.rearrange("p w q -> p (w q)"))
                for i, edges in enumerate((src, dst, etype)):
                    move_columns(unsorted[:, i, :], edges)
                p.tensor_scalar(KEY, KEY.bitcast(i32), 0.5, None, ALU.add).then_inc(sort_steps, 1)
                p.tensor_copy(own_key, unsorted[:, 1, :]).then_inc(sort_steps, 1)
                p.memset(before, 0).then_inc(sort_steps, 1)
                alone(pool, sort_steps, 3, pool_passed)
                with pool.Fori(0, NB) as b:
                    c = b * (2 * CHUNKS + 3) + 3
                    block_keys = KEY[:, bass.ds(b * P, P)]
                    p.tensor_tensor(block_keys, block_keys, within[:, 0:P], ALU.subtract).then_inc(sort_steps, 1)
                    p.tensor_copy(key_now, own_key[:, bass.ds(b, 1)]).then_inc(sort_steps, 1)
                    alone(pool, sort_steps, c + 2, pool_passed)
                    for k in range(CHUNKS):
                        chunk = slice(k * (E // CHUNKS), (k + 1) * (E // CHUNKS))
                        p.tensor_scalar(is_before, KEY[:, chunk], key_now, None, ALU.is_gt).then_inc(sort_steps, 1)
                        alone(pool, sort_steps, c + (2 * k + 3), pool_passed)
                        p.tensor_tensor(before[:, chunk], before[:, chunk], is_before, ALU.add).then_inc(sort_steps, 1)
                        alone(pool, sort_steps, c + (2 * k + 4), pool_passed)
                    p.tensor_tensor(block_keys, block_keys, within[:, P:2 * P], ALU.subtract).then_inc(sort_steps, 1)
                    alone(pool, sort_steps, c + (2 * CHUNKS + 3), pool_passed)
                counted = (2 * CHUNKS + 3) * NB + 3
                p.tensor_reduce(KEY[0:1, :], before, mybir.AxisListType.C, ALU.add).then_inc(sort_steps, 1)
                pool.wait_ge(sort_steps, counted + 1)
                p.tensor_copy(KEY[0:1, :].bitcast(i32), KEY[0:1, :]).then_inc(sort_steps, 1)
                pool.wait_ge(sort_steps, counted + 2)
                move(rank_row.rearrange("(o e) -> o e", o=1), KEY[0:1, :].bitcast(i32))
                move_columns(ranks, rank_row)
                pool.wait_ge(edges_copied, 48)
                with pool.Fori(0, NB) as b:
                    p.tensor_copy(rank_stage[:, 0:1], ranks[:, bass.ds(b, 1)]).then_inc(sort_steps, 1)
                    p.tensor_copy(rank_stage[:, 1:4].rearrange("p (w o) -> p w o", o=1),
                                  unsorted[:, :, bass.ds(b, 1)]).then_inc(sort_steps, 1)
                    alone(pool, sort_steps, b * 2 + (counted + 4), pool_passed)
                    for i, table in enumerate((s_src, s_dst, s_type)):
                        p.indirect_dma_start(table, bass.IndirectOffsetOnAxis(ap=rank_stage[:, 0:1], axis=0),
                                             rank_stage[:, i + 1:i + 2], None, bounds_check=E - 1,
                                             oob_is_err=False).then_inc(sort_put, 16)
                    alone(pool, sort_put, b * 48 + 48, pool_passed)

            pool.wait_ge(order_steps, 4)
            found = pool.value_load(out_of_order[0:1, 0:1])
            with pool.If(found > 1):
                sort_edges()

            dense_rstd(0)
            pool.wait_ge(edges_copied, 48)
            pool.sem_inc(edges_sorted, 1)

            goes = NB // TB
            of_go = lambda k: slice(k * TB, (k + 1) * TB) if isinstance(k, int) else bass.ds(k * TB, TB)

            def put(k, q):
                if q == 0:
                    p.tensor_copy(table_stage[:, 0, :], put_idx[:, of_go(k)]).then_inc(m_staged, 1)
                    p.tensor_copy(table_stage[:, 1, :], slot1[:, of_go(k)]).then_inc(m_staged, 1)
                    alone(pool, m_staged, k * 2 + 2, pool_passed)
                for c in TABLE_AT.get(q, ()):
                    p.indirect_dma_start(first_slot, bass.IndirectOffsetOnAxis(ap=table_stage[:, 0, c:c + 1], axis=0),
                                         table_stage[:, 1, c:c + 1], None, bounds_check=N - 1,
                                         oob_is_err=False).then_inc(m_put, 16)
                if q == GU - 1:
                    pool.wait_ge(m_put, k * (16 * TB) + 16 * TB)

            def get(k, q):
                if q == 0:
                    p.tensor_copy(table_stage[:, 0, :], src_idx[:, of_go(k)]).then_inc(m_staged, 1)
                    alone(pool, m_staged, k + (2 * goes + 1), pool_passed)
                for c in TABLE_AT.get(q, ()):
                    p.indirect_dma_start(table_stage[:, 1, c:c + 1], None, first_slot,
                                         bass.IndirectOffsetOnAxis(ap=table_stage[:, 0, c:c + 1], axis=0),
                                         ).then_inc(m_got, 16)
                if q == GU - 1:
                    pool.wait_ge(m_got, k * (16 * TB) + 16 * TB)
                    p.tensor_copy(got_slot[:, of_go(k)], table_stage[:, 1, :]).then_inc(got_ready, 1)
                    pool.wait_ge(got_ready, k + 1)

            def group(g, par, last, table=None, k=0):
                for q in range(GU):
                    s, l = q // LANES, q % LANES
                    if 3 <= q < 3 + LANES:
                        state_low(pool, p, g, q - 3)
                    need(pool, d_h, g * GU + (q - 1))
                    pool.wait_ge(d_z, unit(g, s, l))
                    p.tensor_tensor(Keep[:, l % 2, :], Zg[:, l % 2, :],
                                    Fd[:, par * LANES + l, :] if s == 0 else Hd[:, l, :], ALU.mult).then_inc(d_keep, 1)
                    if q == STATS_AT + LANES and not last:
                        dense_rstd(g + 1)
                    if table:
                        table(k, q)

            group(0, 0, False)
            ahead = NG - 2 - 2 * goes
            for g in range(1, ahead):
                group(g, g % 2, False)
            pool.wait_ge(idx_ready, 1)
            pool.wait_ge(zero_stored, 16)
            for table, first in ((put, ahead), (get, ahead + goes)):
                with pool.Fori(0, goes // 2) as pair:
                    group(pair * 2 + first, 1, False, table, pair * 2)
                    group(pair * 2 + (first + 1), 0, False, table, pair * 2 + 1)
            for g in range(ahead + 2 * goes, NG):
                group(g, g % 2, g == NG - 1)

            pool.wait_ge(d_o, LANES * NG)
            pool.wait_ge(d_h_copied, 2 * LANES * NG)
            pool.wait_ge(slots_zeroed, MOVED * ET)
            for b in range(2):
                pool.wait_ge(d_h_stored[b], MOVED * LANES * NG)
                pool.wait_ge(d_o_stored[b], MOVED // 2 * LANES * NG)
                for l in range(LANES):
                    pool.wait_ge(d_pairs_stored[b][l], MOVED * ((NG + 1 - b) // 2))
            p.memset(win[:, 0, 0:1], -1).then_inc(a_open, 1)
            p.memset(MX[:, 0, 0:1], 0.0).then_inc(a_open, 1)
            pool.wait_ge(a_open, 2)

            def fetch(i, b, w):
                if not (isinstance(i, int) and i < 2):
                    if w == 0:
                        pool.wait_ge(a_src_turned, i - 1)
                    else:
                        pool.wait_ge(a_dst_turned, i - 1)
                        pool.wait_ge(a_kept, i - 1)
                ks = slice(i * J, (i + 1) * J) if isinstance(i, int) else bass.ds(i * J, J)
                p.tensor_copy(row_stage[:, b, w, :],
                              (dst_pair_idx if w else src_row_idx)[:, ks]).then_inc(a_staged[w], 1)
                alone(pool, a_staged[w], i + 1, pool_passed)
                rows, wide, table = ((XS, D, h0_rows), (XD, 2 * D, node_pairs))[w]
                for j in range(J):
                    p.indirect_dma_start(rows[:, b, j * wide:(j + 1) * wide], None, table,
                                         bass.IndirectOffsetOnAxis(ap=row_stage[:, b, w, j:j + 1], axis=0),
                                         ).then_inc(a_rows_in[b], 16)

            dense_moments = 4 * NG

            def x1_rstd(i):
                pool.wait_ge(a_x1_stat, i + 1)
                need(pool, a_x1_normed, i)
                p.tensor_tensor(a_ve[:], a_mv[:, :, 1], eps[:, 0:J], ALU.add).then_inc(mom_done, 1)
                pool.wait_ge(mom_done, i + (dense_moments + 1))
                p.tensor_tensor(a_rstd[:], a_ve[:], minus_half[:, 0:J], ALU.pow).then_inc(a_x1_rstd, 1)

            def attend(i, b, last):
                if not (isinstance(i, int) and i < 2):
                    x1_rstd(i - 2)
                if not last:
                    fetch(i + 1, 1 - b, 1)
                if not (isinstance(i, int) and i + 2 >= ET):
                    fetch(i + 2, b, 0)

            fetch(0, 0, 0)
            fetch(0, 0, 1)
            fetch(1, 1, 0)
            run(pool, attend, ET, 3)
            x1_rstd(ET - 2)
            x1_rstd(ET - 1)

            pool.wait_ge(a_feat, ET)
            pool.wait_ge(a_types, ET)
            for b, n in ((0, (ET + 1) // 2), (1, ET // 2)):
                pool.wait_ge(a_x1_stored[b], MOVED * n)
                pool.wait_ge(a_f1_stored[b], MOVED * n)
            pool.wait_ge(b_idx, 1)
            pool.sem_inc(b_open, 1)
            for t in range(STEPS):
                c = t * ET

                def fetch(i, b):
                    if not (isinstance(i, int) and i < 2):
                        pool.wait_ge(b_turned, i + (c - 1))
                    ks = slice(i * J, (i + 1) * J) if isinstance(i, int) else bass.ds(i * J, J)
                    p.tensor_copy(row_stage[:, b, 0, :], (h_idx if t else h0_idx)[:, ks]).then_inc(b_staged, 1)
                    alone(pool, b_staged, i + (c + 1), pool_passed)
                    for j in range(J):
                        p.indirect_dma_start(HG[:, b, j * D:(j + 1) * D], None, h_rows[t],
                                             bass.IndirectOffsetOnAxis(ap=row_stage[:, b, 0, j:j + 1], axis=0),
                                             ).then_inc(b_rows_in[b], 16)

                def put_rows(i, b):
                    ks = slice(i * J, (i + 1) * J) if isinstance(i, int) else bass.ds(i * J, J)
                    need(pool, b_o_put[b], i * 32 if b == 0 else (i - 1) * 32)
                    p.tensor_copy(row_stage[:, b, 1, :], put_idx[:, ks]).then_inc(b_o_staged, 1)
                    alone(pool, b_o_staged, i + 1, pool_passed)
                    alone(pool, b_o, i + 1, pool_passed)
                    for j in range(J):
                        p.indirect_dma_start(out, bass.IndirectOffsetOnAxis(ap=row_stage[:, b, 1, j:j + 1], axis=0),
                                             OB[:, b, j * D:(j + 1) * D], None, bounds_check=N - 1,
                                             oob_is_err=False).then_inc(b_o_put[b], 16)

                def step(i, b, last):
                    if not (isinstance(i, int) and i + 2 >= ET):
                        fetch(i + 2, b)
                    if t < STEPS - 1:
                        step_own_low(pool, p, t, i)
                    elif not (isinstance(i, int) and i < 2):
                        put_rows(i - 2, b)

                if t:
                    pool.wait_ge(b_turned, c)
                    for b, n in ((0, (ET + 1) // 2), (1, ET // 2)):
                        pool.wait_ge(b_h_stored[b], MOVED * n * t)
                fetch(0, 0)
                fetch(1, 1)
                run(pool, step, ET, 3)
            put_rows(ET - 2, (ET - 2) % 2)
            put_rows(ET - 1, (ET - 1) % 2)
            for b, n in ((0, (ET + 1) // 2), (1, ET // 2)):
                pool.wait_ge(b_o_put[b], 16 * J * n)

        @block.vector
        def _(dve):
            v = nc.vector
            chained = [0]

            def chain(ins):
                chained[0] += 1
                ins.then_inc(setup, 1)
                dve.wait_ge(setup, chained[0])

            chain(v.memset(nxt_row[:], -1))
            v.memset(ones[:], 1.0).then_inc(order_steps, 1)
            dve.wait_ge(order_in, 48)
            v.tensor_tensor(descents[:, 0:P], dst_row[:], nxt_row[:], ALU.is_gt).then_inc(order_steps, 1)
            dve.wait_ge(order_steps, 2)
            v.tensor_reduce(descents[:, P:P + 1], descents[:, 0:P], mybir.AxisListType.X, ALU.add).then_inc(order_steps, 1)
            dve.wait_ge(order_mm, 1)
            v.tensor_copy(out_of_order[:], banks[7][0:1, 0:1]).then_inc(order_steps, 1)

            def dense_stats(g, par, l):
                X = Xd[:, par * LANES + l, :, 0, :]
                dve.wait_ge(d_x_in[l], g * MOVED + MOVED)
                need(dve, d_rstd, g)
                for j in range(J):
                    ins = v.bn_stats(stats[:, l, j, :], X[:, j, :])
                ins.then_inc(d_stat, 1)

            def dense_norm(g, par, l):
                X = Xd[:, par * LANES + l, :, :, :]
                dve.wait_ge(d_rstd, g + 1)
                for j in range(J):
                    ins = v.tensor_scalar(X[:, j, 1, :], X[:, j, 0, :], mean[:, l, j:j + 1], rstd[:, l, j:j + 1],
                                          ALU.subtract, ALU.mult)
                ins.then_inc(d_normed, 1)

            for l in range(LANES):
                dense_stats(0, 0, l)
            for l in range(LANES):
                dense_norm(0, 0, l)
            dve.wait_ge(weights_in, 16 * n_weights)
            chain(v.tensor_tensor(bias_g[:, :], bias_i[:, :], bias_h[:, :], ALU.add))
            for i in range(2):
                chain(v.tensor_scalar(amat[:, i, :], headmask[:], acol[:, i:i + 1], None, ALU.mult))
            for whole, high, low in ((Wih[:, :, :], Wih_part[:, 0, :, :], Wih_part[:, 1, :, :]),
                                     (Whh[:, :, :], Whh_part[:, 0, :, :], Whh_part[:, 1, :, :]),
                                     (Wi[:, 1, :], Wi_part[:, 0, :], Wi_part[:, 1, :])):
                chain(v.tensor_copy(high, whole))
                chain(v.tensor_tensor(low, whole, high, ALU.subtract))
            dve.sem_inc(parts_ready, 1)
            dve.wait_ge(wse_mm, 1)
            v.tensor_copy(Wse[:, :, :], banks[7][:, 0:2 * D].rearrange("p (a b) -> p a b", a=2)).then_inc(wse_ready, 1)

            def slot_rows():
                dve.wait_ge(edges_in, 64)
                v.tensor_copy(num_row[:, 0, :], src_row[:])
                v.tensor_copy(num_row[:, 1, :], dst_row[:])
                v.tensor_tensor(num_row[:, 2, :], dst_row[:], nxt_row[:], ALU.is_equal).then_inc(idx_steps, 1)

            def slot_columns():
                dve.wait_ge(rows_turned, 1)
                v.tensor_copy(edge_cols[:, :, :], banks[6][0:P, 0:3 * NB].rearrange("p (a b) -> p a b", a=3)).then_inc(idx_steps, 1)
                dve.wait_ge(idx_steps, 2)
                v.tensor_copy(src_idx[:], edge_cols[:, 0, :])
                v.tensor_scalar(src_row_idx[:], edge_cols[:, 0, :], 2.0, float(E + 1), ALU.mult, ALU.add)
                v.tensor_scalar(dst_pair_idx[:], edge_cols[:, 1, :], float(E // 2), None, ALU.add)
                v.scalar_tensor_tensor(out=put_idx[:], in0=edge_cols[:, 2, :], scalar=float(SKIP), in1=edge_cols[:, 1, :],
                                       op0=ALU.mult, op1=ALU.add)
                dve.wait_ge(iota_done, 7)
                v.tensor_scalar(slot1[:], slot_iota[:], 1.0, None, ALU.add)
                v.tensor_scalar(plain_row[:, 0, :], edge_cols[:, 0, :], 2.0, float(E + 2), ALU.mult, ALU.add)
                v.tensor_scalar(plain_row[:, 1, :], edge_cols[:, 0, :], float(E + 1), None, ALU.add).then_inc(idx_ready, 1)

            def group(g, par, last):
                for s in range(STEPS):
                    for l in range(LANES):
                        dense_unit(g, par, s, l)
                        if s == 2 and l == 0 and isinstance(g, int) and g == 0:
                            slot_rows()
                        if s == 0 and l == 0 and not (isinstance(g, int) and g == 0):
                            residual(g - 1, 1 - par, LANES - 1)
                        if STATS_AT <= s * LANES + l < STATS_AT + LANES and not last:
                            dense_stats(g + 1, 1 - par, s * LANES + l - STATS_AT)
                        if NORM_AT <= s * LANES + l < NORM_AT + LANES and not last:
                            dense_norm(g + 1, 1 - par, s * LANES + l - NORM_AT)
                        if s == 2 and l == 3 and not last:
                            feature_low(g + 1, 1 - par, 0)
                finish_unit(g, par, STEPS - 1, LANES - 1)
                for l in range(LANES):
                    b = l % 2
                    dve.wait_ge(d_gate, lane(g, l))
                    dve.wait_ge(d_mm, mm_count(g, STEPS, l, 1))
                    need(dve, d_o_turned, g * LANES + (l - 1))
                    v.scalar_tensor_tensor(out=Qo[:, b, :], in0=banks[3 * b + 1][:, 0:T], scalar=jbias[:, 0:1],
                                           in1=Gt[:, b, :], op0=ALU.add, op1=ALU.mult).then_inc(d_q, 1)
                    if l >= 1:
                        residual(g, par, l - 1)
                    if l < 3 and not last:
                        feature_low(g + 1, 1 - par, l + 1)
                    if l == 2 and isinstance(g, int) and g == 0:
                        slot_columns()

            def residual(g, par, l):
                b = l % 2
                dve.wait_ge(d_o_turned, lane(g, l))
                need(dve, d_o_stored[b], g * (2 * MOVED) + MOVED * (l // 2))
                v.tensor_tensor(rows4(XO[:, b, :]), Xd[:, par * LANES + l, :, 0, :],
                                rows4(banks[7][0:P, :]), ALU.add).then_inc(d_o, 1)

            def dense_unit(g, par, s, l):
                q = s * LANES + l
                b = l % 2
                if LANES <= q - 3 < 2 * LANES:
                    state_low(dve, v, g, q - 3)
                dve.wait_ge(d_mm, mm_count(g, s, l, 2))
                dve.wait_ge(d_r, unit(g, s, l))
                v.scalar_tensor_tensor(out=banks[3 * b + 2][:, 0:T], in0=banks[3 * b + 2][:, 0:T], scalar=bias_h[:, 2:3],
                                       in1=Rg[:, b, :], op0=ALU.add, op1=ALU.mult).then_inc(d_m, 1)
                if q >= 1:
                    finish_unit(g, par, (q - 1) // LANES, (q - 1) % LANES)

            def finish_unit(g, par, s, l):
                b = l % 2
                dve.wait_ge(d_z, unit(g, s, l))
                dve.wait_ge(d_n, unit(g, s, l))
                v.scalar_tensor_tensor(out=Take[:, b, :], in0=Zg[:, b, :], scalar=1.0, in1=Ng[:, b, :],
                                       op0=ALU.subtract, op1=ALU.mult).then_inc(d_take, 1)
                dve.wait_ge(d_take, unit(g, s, l))
                dve.wait_ge(d_keep, unit(g, s, l))
                v.tensor_tensor(Hd[:, l, :], Keep[:, b, :], Take[:, b, :], ALU.subtract).then_inc(d_h, 1)

            def feature_low(g, par, l):
                lane_no = par * LANES + l
                dve.wait_ge(d_feat, lane(g, l))
                v.tensor_tensor(Fl[:, lane_no, :], Fd[:, lane_no, :], Fh[:, lane_no, :],
                                ALU.subtract).then_inc(d_feat_low, 1)

            for l in range(LANES):
                feature_low(0, 0, l)
            chain(v.tensor_copy(bet_part[:, 0, :], bet12[:]))
            chain(v.tensor_tensor(bet_rest[:, 0, :], bet12[:], bet_part[:, 0, :], ALU.subtract))
            chain(v.tensor_copy(bet_part[:, 1, :], bet_rest[:, 0, :]))
            chain(v.tensor_tensor(bet_rest[:, 1, :], bet_rest[:, 0, :], bet_part[:, 1, :], ALU.subtract))
            chain(v.tensor_copy(bet_part[:, 2, :], bet_rest[:, 1, :]))
            chain(v.tensor_scalar(bet_mix[:, 0, :], bet_part[:, 0, :], split_mask[:, 0:1], None, ALU.mult))
            for i in (1, 2):
                chain(v.scalar_tensor_tensor(out=bet_mix[:, i, :], in0=bet_part[:, i, :], scalar=split_mask[:, i:i + 1],
                                             in1=bet_mix[:, i - 1, :], op0=ALU.mult, op1=ALU.add))
            chain(v.tensor_copy(Bet[:], bet_mix[:, 2, :]))
            run(dve, group, NG)
            residual(NG - 1, (NG - 1) % 2, LANES - 1)

            at = lambda i, step: dve.wait_ge(a_dve, a_count(i, step))

            def x1_norm(i, b):
                dve.wait_ge(a_x1_rstd, i + 1)
                need(dve, a_x1_turned, i - 1)
                need(dve, a_f1_stored[b], uses(i, b, MOVED))
                for j in range(J):
                    js = slice(j * D, (j + 1) * D)
                    ins = v.tensor_scalar(N1[:, b, js], X1[:, b, js], a_mv[:, j, 0:1], a_rstd[:, j:j + 1],
                                          ALU.subtract, ALU.mult)
                ins.then_inc(a_x1_normed, 1)

            def logits(i, b):
                dve.wait_ge(a_scaled, i + 1)
                v.tensor_tensor(LG[:, b, :], banks[2][:, 0:T], LS[:], ALU.max).then_inc(a_dve, 1)
                dve.wait_ge(a_edges_in[b], uses(i, b, 32) + 32)
                v.tensor_tensor(same[:, all_of(i)], win[:, b, 1:T + 1], win[:, b, 0:T], ALU.is_equal).then_inc(a_dve, 1)
                at(i, "same")
                v.tensor_scalar(BK[:], same[:, all_of(i)], 1.0, FAR, ALU.subtract, ALU.mult).then_inc(a_dve, 1)

            def attend(i, b, last):
                first = isinstance(i, int) and i == 0
                if first:
                    v.tensor_copy(MX[:, 0, 0:1], MX[:, 0, 0:1]).then_inc(a_dve, 1)
                else:
                    v.tensor_copy(MX[:, b, 0:1], MX[:, 1 - b, T:T + 1]).then_inc(a_dve, 1)
                at(i, "carry")
                v.tensor_tensor_scan(MX[:, b, 1:T + 1], BK[:], LG[:, b, :], MX[:, b, 0:1], ALU.add, ALU.max).then_inc(a_dve, 1)
                at(i, "max")
                need(dve, a_decay, i)
                v.tensor_tensor(EA[:], MX[:, b, 0:T], BK[:], ALU.add).then_inc(a_dve, 1)
                at(i, "lift")
                v.tensor_tensor(EA[:], EA[:], MX[:, b, 1:T + 1], ALU.subtract).then_inc(a_dve, 1)
                need(dve, a_weight, i)
                v.tensor_tensor(EB[:], LG[:, b, :], MX[:, b, 1:T + 1], ALU.subtract).then_inc(a_dve, 1)
                if not first:
                    x1_norm(i - 1, 1 - b)
                dve.wait_ge(a_weight, i + 1)
                dve.wait_ge(a_value_mm, i + 1)
                v.tensor_tensor(WV[:], WT[:], banks[3 + b][:, 0:T], ALU.mult).then_inc(a_dve, 1)
                dve.wait_ge(a_decay, i + 1)
                need(dve, a_att_turned, i - 1)
                v.tensor_tensor_scan(SD[:, b, :], CF[:], WT[:], 0.0 if first else SD[:, 1 - b, T - 1:T], ALU.mult,
                                     ALU.add).then_inc(a_dve, 1)
                at(i, "weighted")
                v.tensor_tensor_scan(SN[:, b, :], CF[:], WV[:], 0.0 if first else SN[:, 1 - b, T - 1:T], ALU.mult,
                                     ALU.add).then_inc(a_dve, 1)
                if not last:
                    logits(i + 1, 1 - b)
                dve.wait_ge(a_att_turned, i + 1)
                need(dve, a_out, i * 2)
                v.reciprocal(RD[:], banks[7][0:P, 0:J * HEADS]).then_inc(a_out, 1)
                dve.wait_ge(a_out, i * 2 + 1)
                need(dve, a_x1, i)
                v.tensor_tensor(AO.rearrange("p (h f) -> p h f", h=J * HEADS),
                                banks[5][0:P, :].rearrange("p (h f) -> p h f", h=J * HEADS),
                                RD.rearrange("p (h o) -> p h o", o=1).to_broadcast([P, J * HEADS, D // HEADS]),
                                ALU.mult).then_inc(a_out, 1)
                dve.wait_ge(a_out, i * 2 + 2)
                dve.wait_ge(a_kept, i + 1)
                need(dve, a_x1_stored[b], uses(i, b, MOVED))
                v.tensor_tensor(X1[:, b, :], XK[:, b, :], AO[:], ALU.add).then_inc(a_x1, 1)
                dve.wait_ge(a_x1, i + 1)
                need(dve, a_x1_rstd, i)
                for j in range(J):
                    ins = v.bn_stats(a_stats[:, j, :], X1[:, b, j * D:(j + 1) * D])
                ins.then_inc(a_x1_bn, 1)
                need(dve, a_x1_normed, i)
                alone(dve, a_x1_bn, i + 1, dve_passed)
                for j in range(J):
                    ins = v.bn_aggr(a_mv[:, j, :], a_stats[:, j, :])
                ins.then_inc(a_x1_stat, 1)

            logits(0, 0)
            run(dve, attend, ET, 3)
            x1_norm(ET - 1, (ET - 1) % 2)

            dve.wait_ge(got_ready, NB // TB)
            for w, idx in enumerate((h0_idx, h_idx)):
                v.scalar_tensor_tensor(out=edge_cols[:, w, :], in0=got_slot[:], scalar=0.0, in1=plain_row[:, w, :],
                                       op0=ALU.is_equal, op1=ALU.mult).then_inc(b_idx_steps, 1)
                dve.wait_ge(b_idx_steps, 2 * w + 1)
                v.scalar_tensor_tensor(out=idx[:], in0=got_slot[:], scalar=-1.0, in1=edge_cols[:, w, :],
                                       op0=ALU.add, op1=ALU.add).then_inc(b_idx_steps, 1)
            dve.wait_ge(b_idx_steps, 4)
            dve.sem_inc(b_idx, 1)

            for t in range(STEPS):
                c = t * ET
                state = H if t else F

                def sum_lows(i, b):
                    dve.wait_ge(b_sum_high, i + (c + 1))
                    need(dve, b_n_mm, i + c)
                    v.tensor_tensor(sum_low, AG[:, b, :], sum_high, ALU.subtract).then_inc(b_sum_low, 1)

                def mask(i, b):
                    if t:
                        dve.wait_ge(b_turned, i + (c + 1))
                    else:
                        dve.wait_ge(b_relu, i + 1)
                    need(dve, b_msg, i + c)
                    for k in range(K):
                        ins = v.scalar_tensor_tensor(out=MK[:, k, :], in0=types[:, all_of(i)], scalar=float(k),
                                                     in1=banks[0][:, 0:T] if t else RG[:], op0=ALU.is_equal, op1=ALU.mult)
                    ins.then_inc(b_masked, 1)
                    v.tensor_scalar(hot[:, b, :], types[0:12, all_of(i)], part_type[:, 0:1], None,
                                    ALU.is_equal).then_inc(b_hot, 1)

                def sum_messages(i, b):
                    first = isinstance(i, int) and i == 0
                    dve.wait_ge(b_msg, i + (c + 1))
                    need(dve, b_n_mm, max(i + c - 1, c) if isinstance(i, int) else i + (c - 1))
                    if not first:
                        dve.wait_ge(b_sum, i + c)
                    v.tensor_tensor_scan(AG[:, b, :], same[:, all_of(i)], banks[1][:, 0:T],
                                         0.0 if first else AG[:, 1 - b, T - 1:T], ALU.mult, ALU.add).then_inc(b_sum, 1)

                def readout(i, b):
                    dve.wait_ge(b_gate, i + 1)
                    dve.wait_ge(b_j_mm, i + 1)
                    need(dve, b_q_turned, i)
                    v.scalar_tensor_tensor(out=Qs[:], in0=banks[7][:, 0:T], scalar=jbias[:, 0:1], in1=Gs[:],
                                           op0=ALU.add, op1=ALU.mult).then_inc(b_q, 1)

                def residual(i, b):
                    dve.wait_ge(b_q_turned, i + 1)
                    dve.wait_ge(b_x1_in[b], uses(i, b, MOVED) + MOVED)
                    need(dve, b_o_put[b], uses(i, b, 16 * J))
                    v.tensor_tensor(OB[:, b, :], XB[:, b, :], banks[6][0:P, :], ALU.add).then_inc(b_o, 1)

                def step(i, b, last):
                    first = isinstance(i, int) and i == 0
                    if not last:
                        sum_messages(i + 1, 1 - b)
                    if not (isinstance(i, int) and i + 2 >= ET):
                        mask(i + 2, b)
                    if t == STEPS - 1:
                        if not last:
                            step_own_low(dve, v, t, i + 1)
                        if not first:
                            readout(i - 1, 1 - b)
                    dve.wait_ge(b_own_mm, i + (c + 1))
                    dve.wait_ge(b_r, i + (c + 1))
                    need(dve, b_m2, i + c)
                    v.scalar_tensor_tensor(out=Ms[:], in0=banks[4][:, 0:T], scalar=bias_h[:, 2:3], in1=Rs[:],
                                           op0=ALU.add, op1=ALU.mult).then_inc(b_m1, 1)
                    dve.wait_ge(b_m1, i + (c + 1))
                    dve.wait_ge(b_n_mm, i + (c + 1))
                    v.tensor_tensor(banks[5][:, 0:T], Ms[:], banks[5][:, 0:T], ALU.add).then_inc(b_m2, 1)
                    if not last:
                        sum_lows(i + 1, 1 - b)
                    dve.wait_ge(b_z, i + (c + 1))
                    need(dve, b_h, i + c)
                    if t:
                        dve.wait_ge(b_h_kept, i + (c - ET + 1))
                    v.tensor_tensor(Ks[:], Zs[:], state[:, all_of(i)], ALU.mult).then_inc(b_keep, 1)
                    dve.wait_ge(b_n, i + (c + 1))
                    v.scalar_tensor_tensor(out=Ts[:], in0=Zs[:], scalar=1.0, in1=Ns[:], op0=ALU.subtract,
                                           op1=ALU.mult).then_inc(b_take, 1)
                    dve.wait_ge(b_take, i + (c + 1))
                    if t < STEPS - 1:
                        need(dve, b_h_kept, i + c)
                        need(dve, b_h_turned, i + c)
                    elif first:
                        dve.wait_ge(b_h_kept, c)
                        dve.wait_ge(b_h_turned, c)
                    else:
                        dve.wait_ge(b_j_mm, i)
                    v.tensor_tensor(HN[:], Ks[:], Ts[:], ALU.subtract).then_inc(b_h, 1)
                    if t == STEPS - 1 and not first:
                        residual(i - 1, 1 - b)

                if t == STEPS - 1:
                    step_own_low(dve, v, t, 0)
                mask(0, 0)
                sum_messages(0, 0)
                mask(1, 1)
                sum_lows(0, 0)
                run(dve, step, ET, 3)
            readout(ET - 1, (ET - 1) % 2)
            residual(ET - 1, (ET - 1) % 2)

        @block.scalar
        def _(act):
            a = nc.scalar
            for dst_ap, src_ap in weight_loads[1::2]:
                act.dma_start(dst_ap, src_ap).then_inc(weights_in, 16)
            act.wait_ge(setup, 2)

            def feature_copy(g, par, l):
                act.wait_ge(d_x_turned, lane(g, l))
                a.activation(Fh[:, par * LANES + l, :], banks[6][:, 0:T], ACT.Relu).then_inc(d_feat_high, 1)
                a.activation(Fd[:, par * LANES + l, :], banks[6][:, 0:T], ACT.Relu).then_inc(d_feat, 1)

            def tanh_of(g, s, l):
                b = l % 2
                act.wait_ge(d_m, unit(g, s, l))
                a.activation(Ng[:, b, :], banks[3 * b + 2][:, 0:T], ACT.Tanh, bias=bias_i[:, 2:3]).then_inc(d_n, 1)

            def dense_unit(g, par, s, l):
                b = l % 2
                q = s * LANES + l
                if 3 <= q < 3 + 2 * LANES:
                    before = (q - 3) % LANES
                    act.wait_ge(d_h, g * GU + (q - 2))
                    a.activation(Hh[:, before, :], Hd[:, before, :], ACT.Copy).then_inc(d_high, 1)
                if s >= 1:
                    i = (s - 1) * LANES + l
                    act.wait_ge(d_h_turned, g * 8 + (i + 1))
                    need(act, d_h_stored[b], g * (4 * MOVED) + MOVED * (i // 2))
                    a.activation(HO[:, b, :], banks[7][0:P, :], ACT.Copy).then_inc(d_h_copied, 1)
                need(act, d_m, g * GU + (q - 1))
                act.wait_ge(d_mm, mm_count(g, s, l, 0))
                a.activation(Rg[:, b, :], banks[3 * b][:, 0:T], ACT.Sigmoid, bias=bias_g[:, 0:1]).then_inc(d_r, 1)
                act.wait_ge(d_mm, mm_count(g, s, l, 1))
                need(act, d_take, g * GU + (q - 1))
                need(act, d_keep, g * GU + (q - 1))
                a.activation(Zg[:, b, :], banks[3 * b + 1][:, 0:T], ACT.Sigmoid, bias=bias_g[:, 1:2]).then_inc(d_z, 1)
                if q >= 1:
                    tanh_of(g, (q - 1) // LANES, (q - 1) % LANES)

            def group(g, par, last):
                for s in range(STEPS):
                    for l in range(LANES):
                        dense_unit(g, par, s, l)
                        if s == STEPS - 1 and l >= 2 and not last:
                            feature_copy(g + 1, 1 - par, l - 2)
                tanh_of(g, STEPS - 1, LANES - 1)
                for l in range(LANES):
                    b = l % 2
                    act.wait_ge(d_mm, mm_count(g, STEPS, l, 0))
                    need(act, d_q, g * LANES + (l - 1))
                    a.activation(Gt[:, b, :], banks[3 * b][:, 0:T], ACT.Sigmoid, bias=ibias[:, 0:1]).then_inc(d_gate, 1)
                    if l < 2 and not last:
                        feature_copy(g + 1, 1 - par, l + 2)

            for l in range(LANES):
                feature_copy(0, 0, l)
            run(act, group, NG)

            def sources(i, b):
                act.wait_ge(a_rows_in[b], uses(i, b, 128) + 128)
                need(act, a_x1, i - 1)
                a.activation(rows4(XK[:, b, :]), XD[:, b, :].rearrange("p (j w) -> p j w", j=J)[:, :, 0:D],
                             ACT.Copy).then_inc(a_kept, 1)
                act.wait_ge(a_src_turned, i + 1)
                need(act, a_value_mm, i)
                a.activation(ST[:], banks[0][:, 0:T], ACT.Relu).then_inc(a_src_feat, 1)
                act.wait_ge(a_dst_turned, i + 1)
                need(act, a_logit_mm, i)
                a.activation(DT[:], banks[1][:, 0:T], ACT.Relu).then_inc(a_dst_feat, 1)

            def scaled(i):
                act.wait_ge(a_logit_mm, i + 1)
                need(act, a_dve, a_count(i - 1, "leaky"))
                a.activation(LS[:], banks[2][:, 0:T], ACT.Copy, scale=SLOPE).then_inc(a_scaled, 1)

            def new_rows(i, b):
                act.wait_ge(a_x1_turned, i + 1)
                a.activation(F[:, all_of(i)], banks[6][:, 0:T], ACT.Relu).then_inc(a_feat, 1)

            def attend(i, b, last):
                if not last:
                    sources(i + 1, 1 - b)
                act.wait_ge(a_dve, a_count(i, "decay_arg"))
                need(act, a_dve, a_count(i - 1, "sum_v"))
                a.activation(CF[:], EA[:], ACT.Exp).then_inc(a_decay, 1)
                act.wait_ge(a_dve, a_count(i, "weight_arg"))
                a.activation(WT[:], EB[:], ACT.Exp).then_inc(a_weight, 1)
                act.wait_ge(a_edges_in[b], uses(i, b, 32) + 32)
                a.activation(types[:, all_of(i)], typ[:, b, :], ACT.Copy).then_inc(a_types, 1)
                if not last:
                    scaled(i + 1)
                if not (isinstance(i, int) and i == 0):
                    new_rows(i - 1, 1 - b)

            sources(0, 0)
            scaled(0)
            run(act, attend, ET, 3)
            new_rows(ET - 1, (ET - 1) % 2)

            for t in range(STEPS):
                c = t * ET

                def relu_of(i):
                    act.wait_ge(b_turned, i + 1)
                    need(act, b_masked, i)
                    a.activation(RG[:], banks[0][:, 0:T], ACT.Relu).then_inc(b_relu, 1)

                def own_highs(i):
                    if t:
                        act.wait_ge(b_h_kept, i + (c - ET + 1))
                    else:
                        act.wait_ge(a_feat, i + 1)
                    alone(act, b_own_mm, i + c, act_passed)
                    a.activation(own_high, (H if t else F)[:, all_of(i)], ACT.Copy).then_inc(b_own_high, 1)

                def sum_highs(i, b):
                    act.wait_ge(b_sum, i + (c + 1))
                    need(act, b_n_mm, i + c)
                    a.activation(sum_high, AG[:, b, :], ACT.Copy).then_inc(b_sum_high, 1)

                def finish(i, b):
                    if t < STEPS - 1:
                        alone(act, b_h, i + (c + 1), act_passed)
                        a.activation(H[:, all_of(i)], HN[:], ACT.Copy).then_inc(b_h_kept, 1)
                        act.wait_ge(b_h_turned, i + (c + 1))
                        need(act, b_h_stored[b], uses(i, b, MOVED) + MOVED * t * ((ET + 1 - b) // 2))
                        a.activation(HR[:, b, :], banks[6][0:P, :], ACT.Copy).then_inc(b_h_copied, 1)
                    else:
                        act.wait_ge(b_gate_mm, i + 1)
                        need(act, b_q, i)
                        a.activation(Gs[:], banks[5][:, 0:T], ACT.Sigmoid, bias=ibias[:, 0:1]).then_inc(b_gate, 1)

                def step(i, b, last):
                    if t == 0 and not (isinstance(i, int) and i + 2 >= ET):
                        relu_of(i + 2)
                    if not last:
                        own_highs(i + 1)
                    if not (isinstance(i, int) and i == 0):
                        finish(i - 1, 1 - b)
                    act.wait_ge(b_r_mm, i + (c + 1))
                    need(act, b_m1, i + c)
                    a.activation(Rs[:], banks[2][:, 0:T], ACT.Sigmoid, bias=bias_g[:, 0:1]).then_inc(b_r, 1)
                    act.wait_ge(b_z_mm, i + (c + 1))
                    need(act, b_take, i + c)
                    a.activation(Zs[:], banks[3][:, 0:T], ACT.Sigmoid, bias=bias_g[:, 1:2]).then_inc(b_z, 1)
                    if not last:
                        sum_highs(i + 1, 1 - b)
                    act.wait_ge(b_m2, i + (c + 1))
                    a.activation(Ns[:], banks[5][:, 0:T], ACT.Tanh, bias=bias_i[:, 2:3]).then_inc(b_n, 1)

                if t == 0:
                    act.wait_ge(b_open, 1)
                own_highs(0)
                if t == 0:
                    relu_of(0)
                    relu_of(1)
                sum_highs(0, 0)
                run(act, step, ET, 3)
                finish(ET - 1, (ET - 1) % 2)

        @block.tensor
        def _(pe):
            m = nc.tensor
            pe.wait_ge(order_steps, 3)
            m.matmul(banks[7][0:1, 0:1], descents[:, P:P + 1], ones[:], start=True, stop=True).then_inc(order_mm, 1)
            def slot_columns():
                pe.wait_ge(idx_steps, 1)
                pe.wait_ge(d_feat, 2 * LANES)
                for i in range(3):
                    ins = m.transpose(banks[6][0:P, i * NB:(i + 1) * NB], num_row[:, i, :], ident[0:NB, 0:NB])
                ins.then_inc(rows_turned, 1)

            def turn_in(g, par, l):
                pe.wait_ge(d_normed, lane(g, l))
                need(pe, d_feat, g * LANES + l)
                for j in range(J):
                    ins = m.transpose(banks[6][:, j * P:(j + 1) * P], Xd[:, par * LANES + l, j, 1, :], ident[0:P, 0:P])
                ins.then_inc(d_x_turned, 1)

            pe.wait_ge(weights_in, 16 * n_weights)
            for l in range(LANES):
                turn_in(0, 0, l)
            pe.wait_ge(setup, 4)
            pe.wait_ge(order_steps, 4)
            for i in range(2):
                ins = m.matmul(banks[7][:, i * D:(i + 1) * D], W0T[:], amat[:, i, :], start=True, stop=True)
            ins.then_inc(wse_mm, 1)
            pe.wait_ge(wse_ready, 1)
            pe.wait_ge(parts_ready, 1)

            def turn_out(src_ap):
                for j in range(J):
                    ins = m.transpose(banks[7][0:P, j * D:(j + 1) * D], src_ap[:, j * P:(j + 1) * P], ident[:])
                return ins

            def group(g, par, last):
                for s in range(STEPS):
                    for l in range(LANES):
                        q = s * LANES + l
                        b = l % 2
                        if s == 0:
                            pe.wait_ge(d_feat_high, lane(g, l))
                            high, low = Fh[:, par * LANES + l, :], Fl[:, par * LANES + l, :]
                        else:
                            pe.wait_ge(d_high, g * 8 + ((s - 1) * LANES + l + 1))
                            high, low = Hh[:, l, :], Hl[:, l, :]
                            i = (s - 1) * LANES + l
                            if i == 0:
                                need(pe, d_o, g * LANES)
                            else:
                                pe.wait_ge(d_h_copied, g * 8 + i)
                            turn_out(Hd[:, l, :]).then_inc(d_h_turned, 1)
                        for k, (used, from_readout) in enumerate(((d_r, d_gate), (d_z, d_q), (d_n, d_n))):
                            if q >= 2 or k == 2:
                                need(pe, used, g * GU + (q - 1))
                            else:
                                need(pe, from_readout, g * LANES + (l - 1))
                            out_bank = banks[3 * b + k][:, 0:T]
                            m.matmul(out_bank, Whh_part[:, 0, k, :], high, start=True, stop=False)
                            m.matmul(out_bank, Whh_part[:, 1, k, :], high, start=False, stop=False)
                            if k == 0:
                                if s == 0:
                                    pe.wait_ge(d_feat_low, lane(g, l))
                                else:
                                    pe.wait_ge(d_low[s - 1], lane(g, l))
                            m.matmul(out_bank, Whh_part[:, 0, k, :], low, start=False, stop=True).then_inc(d_mm, 1)
                        if q == 0 and not (isinstance(g, int) and g == 0):
                            readout_rows(g - 1, LANES - 1)
                        if s == STEPS - 1 and l >= 2 and not last:
                            turn_in(g + 1, 1 - par, l - 2)
                for l in range(LANES):
                    b = l % 2
                    pe.wait_ge(d_h, unit(g, STEPS - 1, l))
                    if l >= 2:
                        pe.wait_ge(d_gate, g * LANES + (l - 1))
                    else:
                        pe.wait_ge(d_r, g * GU + (GU - 1 + l))
                    m.matmul(banks[3 * b][:, 0:T], Wi[:, 0, :], Hd[:, l, :], start=True, stop=False)
                    high, low = Fh[:, par * LANES + l, :], Fl[:, par * LANES + l, :]
                    m.matmul(banks[3 * b][:, 0:T], Wi_part[:, 0, :], high, start=False, stop=False)
                    m.matmul(banks[3 * b][:, 0:T], Wi_part[:, 1, :], high, start=False, stop=False)
                    m.matmul(banks[3 * b][:, 0:T], Wi_part[:, 0, :], low, start=False, stop=True).then_inc(d_mm, 1)
                    if l >= 2:
                        pe.wait_ge(d_q, g * LANES + (l - 1))
                    else:
                        pe.wait_ge(d_z, g * GU + (GU - 1 + l))
                    m.matmul(banks[3 * b + 1][:, 0:T], Wj[:], Hd[:, l, :], start=True, stop=True).then_inc(d_mm, 1)
                    if l < 2 and not last:
                        turn_in(g + 1, 1 - par, l + 2)
                    if l >= 1:
                        readout_rows(g, l - 1)
                    if l == 1 and isinstance(g, int) and g == 0:
                        slot_columns()
                if isinstance(g, int) and g == 0:
                    pe.wait_ge(idx_steps, 2)

            def readout_rows(g, l):
                pe.wait_ge(d_q, lane(g, l))
                if l == 0:
                    pe.wait_ge(d_h_copied, g * 8 + 8)
                else:
                    pe.wait_ge(d_o, lane(g, l - 1))
                turn_out(Qo[:, l % 2, :]).then_inc(d_o_turned, 1)

            run(pe, group, NG)
            readout_rows(NG - 1, LANES - 1)

            def turn(bank_ap, rows):
                for j in range(J):
                    ins = m.transpose(bank_ap[:, j * P:(j + 1) * P], rows[:, j * D:(j + 1) * D], ident[0:P, 0:P])
                return ins

            def turn_back(bank_ap, cols):
                for j in range(J):
                    ins = m.transpose(bank_ap[0:P, j * D:(j + 1) * D], cols[:, j * P:(j + 1) * P], ident[:])
                return ins

            def sources(i, b):
                pe.wait_ge(a_rows_in[b], uses(i, b, 128) + 128)
                need(pe, a_src_feat, i)
                turn(banks[0], XS[:, b, :]).then_inc(a_src_turned, 1)
                need(pe, a_dst_feat, i)
                for j in range(J):
                    ins = m.transpose(banks[1][:, j * P:(j + 1) * P], XD[:, b, (2 * j + 1) * D:(2 * j + 2) * D],
                                      ident[0:P, 0:P])
                ins.then_inc(a_dst_turned, 1)
                pe.wait_ge(a_src_feat, i + 1)
                pe.wait_ge(a_dst_feat, i + 1)
                need(pe, a_dve, a_count(i - 1, "leaky"))
                m.matmul(banks[2][:, 0:T], Wse[:, 0, :], ST[:], start=True, stop=False)
                m.matmul(banks[2][:, 0:T], Wse[:, 1, :], DT[:], start=False, stop=True).then_inc(a_logit_mm, 1)
                need(pe, a_dve, a_count(i - 2, "weighted"))
                m.matmul(banks[3 + b][:, 0:T], W0[:], ST[:], start=True, stop=True).then_inc(a_value_mm, 1)

            def new_rows(i, b):
                pe.wait_ge(a_x1_normed, i + 1)
                need(pe, a_feat, i)
                turn(banks[6], N1[:, b, :]).then_inc(a_x1_turned, 1)

            def attend(i, b, last):
                if not last:
                    sources(i + 1, 1 - b)
                if not (isinstance(i, int) and i == 0):
                    new_rows(i - 1, 1 - b)
                pe.wait_ge(a_dve, a_count(i, "sum_v"))
                need(pe, a_out, i * 2)
                turn_back(banks[5], SN[:, b, :])
                for j in range(J):
                    ins = m.matmul(banks[7][0:P, j * HEADS:(j + 1) * HEADS], SD[:, b, j * P:(j + 1) * P], head_pick[:],
                                   start=True, stop=True)
                ins.then_inc(a_att_turned, 1)

            sources(0, 0)
            run(pe, attend, ET, 3)
            new_rows(ET - 1, (ET - 1) % 2)

            for t in range(STEPS):
                c = t * ET
                state = H if t else F

                def fetched(i, b):
                    pe.wait_ge(b_rows_in[b], uses(i, b, 16 * J) + 16 * J * (1 + t * ((ET + 1 - b) // 2)))
                    need(pe, b_masked, i + c)
                    turn(banks[0], HG[:, b, :]).then_inc(b_turned, 1)

                def messages(i, b):
                    pe.wait_ge(b_masked, i + (c + 1))
                    need(pe, b_sum, i + c)
                    for k in range(K):
                        m.matmul(banks[1][:, 0:T], Wet[:, k, :], MK[:, k, :], start=(k == 0), stop=False)
                    pe.wait_ge(b_hot, i + (c + 1))
                    m.matmul(banks[1][:, 0:T], Bet[:], hot[:, b, :], start=False, stop=True).then_inc(b_msg, 1)

                def readout(i):
                    pe.wait_ge(b_h, i + (c + 1))
                    pe.wait_ge(b_r, i + (c + 1))
                    m.matmul(banks[5][:, 0:T], Wi[:, 0, :], HN[:], start=True, stop=False)
                    m.matmul(banks[5][:, 0:T], Wi[:, 1, :], F[:, all_of(i)], start=False, stop=True).then_inc(b_gate_mm, 1)
                    need(pe, b_q, i)
                    m.matmul(banks[7][:, 0:T], Wj[:], HN[:], start=True, stop=True).then_inc(b_j_mm, 1)

                def readout_rows(i):
                    pe.wait_ge(b_q, i + 1)
                    need(pe, b_o, i)
                    turn_back(banks[6], Qs).then_inc(b_q_turned, 1)

                def finish(i):
                    if t < STEPS - 1:
                        pe.wait_ge(b_h, i + (c + 1))
                        need(pe, b_h_copied, i + c)
                        turn_back(banks[6], HN).then_inc(b_h_turned, 1)
                    else:
                        readout(i)

                def step(i, b, last):
                    first = isinstance(i, int) and i == 0
                    if not last:
                        messages(i + 1, 1 - b)
                    if not (isinstance(i, int) and i + 2 >= ET):
                        fetched(i + 2, b)
                    pe.wait_ge(b_own_high, i + (c + 1))
                    for k, used in enumerate((b_r, b_z, b_m1)):
                        need(pe, used, i + c)
                        bank_ap = banks[2 + k][:, 0:T]
                        m.matmul(bank_ap, Whh_part[:, 0, k, :], own_high, start=True, stop=False)
                        m.matmul(bank_ap, Whh_part[:, 1, k, :], own_high, start=False, stop=False)
                        if k == 0:
                            pe.wait_ge(b_own_low, i + (c + 1))
                        ins = m.matmul(bank_ap, Whh_part[:, 0, k, :], own_low, start=False, stop=(k == 2))
                    ins.then_inc(b_own_mm, 1)
                    if not first:
                        finish(i - 1)
                    pe.wait_ge(b_sum_high, i + (c + 1))
                    for k in range(2):
                        m.matmul(banks[2 + k][:, 0:T], Wih_part[:, 0, k, :], sum_high, start=False, stop=False)
                        m.matmul(banks[2 + k][:, 0:T], Wih_part[:, 1, k, :], sum_high, start=False, stop=False)
                    pe.wait_ge(b_sum_low, i + (c + 1))
                    m.matmul(banks[2][:, 0:T], Wih_part[:, 0, 0, :], sum_low, start=False, stop=True).then_inc(b_r_mm, 1)
                    m.matmul(banks[3][:, 0:T], Wih_part[:, 0, 1, :], sum_low, start=False, stop=True).then_inc(b_z_mm, 1)
                    need(pe, b_n, i + c)
                    if t == STEPS - 1:
                        need(pe, b_gate, i)
                    m.matmul(banks[5][:, 0:T], Wih_part[:, 0, 2, :], sum_high, start=True, stop=False)
                    m.matmul(banks[5][:, 0:T], Wih_part[:, 1, 2, :], sum_high, start=False, stop=False)
                    m.matmul(banks[5][:, 0:T], Wih_part[:, 0, 2, :], sum_low, start=False, stop=True).then_inc(b_n_mm, 1)
                    if t == STEPS - 1 and not first:
                        readout_rows(i - 1)

                fetched(0, 0)
                messages(0, 0)
                fetched(1, 1)
                run(pe, step, ET, 3)
                finish(ET - 1)
            readout_rows(ET - 1)


def kernel(**inputs):
    import numpy as np
    import concourse.bacc as bacc
    from concourse.bass_utils import run_bass_kernel_spmd

    a = {k: np.asarray(v) for k, v in inputs.items()}
    cols = lambda v, n: v.reshape(n, D).T
    att = a["L0_gnn_a"]
    arrays = {
        "x": a["x"], "src": a["src"], "dst": a["dst"], "etype": a["edge_type_4"],
        "w0": a["L0_gnn_W"], "w0T": a["L0_gnn_W"].T,
        "a_cols": np.stack([att[:, :32].reshape(D), att[:, 32:].reshape(D)], axis=1),
        "wetT": a["L1_gnn_W_et"].transpose(0, 2, 1), "b_et": a["L1_gnn_b_et"],
        "wihT": a["L1_gnn_W_ih"].T, "bih": cols(a["L1_gnn_b_ih"], 3),
        "whhT": a["L1_gnn_W_hh"].T, "bhh": cols(a["L1_gnn_b_hh"], 3),
        "iwT": a["L1_gnn_i_w"].T, "ib": cols(a["L1_gnn_i_b"], 1),
        "jwT": a["L1_gnn_j_w"].T, "jb": cols(a["L1_gnn_j_b"], 1),
        "ident_in": np.eye(128, dtype=np.float32),
        "headmask_in": np.kron(np.eye(HEADS, dtype=np.float32), np.ones((D // HEADS, D // HEADS), np.float32)),
        "head_pick_in": np.eye(D, dtype=np.float32)[:, ::D // HEADS],
        "part_type_in": (np.arange(12) % K).astype(np.float32)[:, None],
        "split_in": np.repeat(np.eye(3, dtype=np.float32), K, axis=0),
        "within_in": np.stack([0.5 * np.tri(P, P), 0.5 * (1 - np.tri(P, P))], axis=1).astype(np.float32),
    }
    arrays = {"in_" + k: np.ascontiguousarray(v) for k, v in arrays.items()}
    nc = bacc.Bacc("TRN2", target_bir_lowering=False, num_devices=1)
    args = [nc.dram_tensor(k, v.shape, mybir.dt.from_np(v.dtype), kind="ExternalInput").ap() for k, v in arrays.items()]
    out = nc.dram_tensor("out_0", a["x"].shape, mybir.dt.float32, kind="ExternalOutput").ap()
    gnn_kernel(nc, *args, out)
    r = run_bass_kernel_spmd(nc, [arrays], core_ids=[0])
    return r.results[0]["out_0"]
```
